# Optimizing a Trainium2 kernel written in Bass

```python
import numpy as np
import jax
import jax.numpy as jnp

def _softmax(x, axis=-1):
    return jax.nn.softmax(x, axis=axis)

def _gelu(x):
    return jax.nn.gelu(x, approximate=True)

def _silu(x):
    return jax.nn.silu(x)

def _sigmoid(x):
    return jax.nn.sigmoid(x)

def _layernorm(x, axis=-1, eps=1e-05):
    m = jnp.mean(x, axis=axis, keepdims=True)
    v = jnp.var(x, axis=axis, keepdims=True)
    return (x - m) / jnp.sqrt(v + eps)

def _scatter_add(tgt, idx, src, axis=0):
    return tgt.at[idx].add(src)

def _segment_sum(src, seg, n):
    return jax.ops.segment_sum(src, seg, n)
kernel_name = 'mk_gnn_preln_d4_gnn_r32_09e8a2'

def setup_inputs(seed: int=0):
    np.random.seed(seed)
    _w = jnp.asarray

    def _rec_inputs():
        import jax
        import jax.numpy as jnp
        _gk = jax.random.key(seed)
        x = -0.0005121 + 1.001 * jax.random.normal(jax.random.fold_in(_gk, 1), (50000, 64), jnp.float32)
        src = jax.random.randint(jax.random.fold_in(_gk, 2), (50000,), 0, 50000, jnp.int32)
        dst = jax.random.randint(jax.random.fold_in(_gk, 3), (50000,), 0, 50000, jnp.int32)
        _o = jnp.argsort(dst, stable=True)
        src = src[_o]
        dst = dst[_o]
        edge_attr_4 = -0.0005303 + 1.00001 * jax.random.normal(jax.random.fold_in(_gk, 13), (50000, 4), jnp.float32)
        edge_attr_5 = jax.random.uniform(jax.random.fold_in(_gk, 14), (50000, 5), jnp.float32, 0.0, 1)
        edge_weight = jax.random.uniform(jax.random.fold_in(_gk, 16), (50000,), jnp.float32, 0.0, 0.999998)
        return (x, src, dst, edge_attr_4, edge_attr_5, edge_weight)
    x, src, dst, edge_attr_4, edge_attr_5, edge_weight = _rec_inputs()

    def _L0_gnn_setup():
        import jax, jax.numpy as jnp
        import numpy as np
        EMB = 64
        HEADS = 2
        NUM_BOND = 5
        NEG_SLOPE = 0.2
        key = jax.random.key(seed)
        ks = jax.random.split(key, 9)
        N, E = (50000, 25000)
        x = jax.random.normal(ks[0], (N, EMB), dtype=jnp.float32)
        edge_index = jax.random.randint(ks[1], (2, E), 0, N, dtype=jnp.int64)
        edge_attr = jax.random.uniform(ks[2], (E, NUM_BOND), dtype=jnp.float32)
        W_lin = jax.random.normal(ks[3], (EMB, HEADS * EMB), dtype=jnp.float32) / np.sqrt(EMB)
        b_lin = jnp.zeros((HEADS * EMB,), dtype=jnp.float32)
        W_edge = jax.random.normal(ks[4], (NUM_BOND, HEADS * EMB), dtype=jnp.float32) / np.sqrt(NUM_BOND)
        b_edge = jnp.zeros((HEADS * EMB,), dtype=jnp.float32)
        att = jax.random.normal(ks[5], (1, HEADS, 2 * EMB), dtype=jnp.float32) / np.sqrt(2 * EMB)
        bias = jnp.zeros((EMB,), dtype=jnp.float32)
        return {'x': x, 'edge_index': edge_index, 'edge_attr': edge_attr, 'W_lin': W_lin, 'b_lin': b_lin, 'W_edge': W_edge, 'b_edge': b_edge, 'att': att, 'bias': bias}
    _L0_gnn_all = _L0_gnn_setup()
    _L0_gnn_in = {k: v for k, v in _L0_gnn_all.items() if k in ('W_lin', 'b_lin', 'W_edge', 'b_edge', 'att', 'bias')}
    del _L0_gnn_all

    def _L1_gnn_setup():
        import jax, jax.numpy as jnp
        import numpy as np
        import math
        N_NODES = 50000
        N_EDGES = 15625
        HIDDEN = 64
        N_LAYERS = 4
        DELTA = 2.5
        N_AGG = 6
        N_SCALE = 3
        EPS_BN = 1e-05

        def _batchnorm(x, gamma, beta):
            mu = jnp.mean(x, axis=0)
            var = jnp.mean(jnp.square(x - mu), axis=0)
            return (x - mu) * jax.lax.rsqrt(var + EPS_BN) * gamma + beta

        def _pna_layer(h, src, dst, WM, bM, WU, bU, g_t, b_t, Wmix, bmix, g_o, b_o):
            n = h.shape[0]
            msg = jnp.concatenate([h[src], h[dst]], axis=1) @ WM + bM
            deg = jax.ops.segment_sum(jnp.ones(src.shape[0], h.dtype), dst, num_segments=n)
            denom = jnp.maximum(deg, 1.0)[:, None]
            s = jax.ops.segment_sum(msg, dst, num_segments=n)
            mean = s / denom
            mean_sq = jax.ops.segment_sum(msg * msg, dst, num_segments=n) / denom
            var = jax.nn.relu(mean_sq - mean * mean)
            std = jnp.sqrt(var + 1e-30)
            has = (deg > 0)[:, None]
            mx = jnp.where(has, jax.ops.segment_max(msg, dst, num_segments=n), 0.0)
            mn = jnp.where(has, jax.ops.segment_min(msg, dst, num_segments=n), 0.0)
            agg = jnp.concatenate([mean, mx, mn, std, var, s], axis=1)
            logD = jnp.log(deg + 1.0)[:, None]
            amp = logD / DELTA
            att = jnp.where(logD > 0, DELTA / jnp.where(logD > 0, logD, 1.0), 0.0)
            h_neigh = jnp.concatenate([agg, agg * amp, agg * att], axis=1)
            hu = jnp.concatenate([h, h_neigh], axis=1) @ WU + bU
            hu = hu * (1.0 / math.sqrt(n))
            hbn = _batchnorm(hu, g_t, b_t)
            hm = jax.nn.leaky_relu(hbn @ Wmix + bmix, 0.01)
            out = hm + h
            return jax.nn.relu(_batchnorm(out, g_o, b_o)) + h
        key = jax.random.key(seed)
        ks = jax.random.split(key, 12)
        d = HIDDEN
        L = N_LAYERS
        din_u = (N_AGG * N_SCALE + 1) * d
        return {'node_feat': jax.random.normal(ks[0], (N_NODES, d), jnp.float32), 'edge_feat': jax.random.normal(ks[1], (N_EDGES, 4), jnp.float32), 'edge_src': jax.random.randint(ks[2], (N_EDGES,), 0, N_NODES, jnp.int32), 'edge_dst': jax.random.randint(ks[3], (N_EDGES,), 0, N_NODES, jnp.int32), 'WM': jax.random.normal(ks[4], (L, 2 * d, d), jnp.float32) / math.sqrt(2 * d), 'bM': jnp.zeros((L, d), jnp.float32), 'WU': jax.random.normal(ks[5], (L, din_u, d), jnp.float32) / math.sqrt(din_u), 'bU': jnp.zeros((L, d), jnp.float32), 'gamma_t': jnp.ones((L, d), jnp.float32), 'beta_t': jnp.zeros((L, d), jnp.float32), 'Wmix': jax.random.normal(ks[6], (L, d, d), jnp.float32) / math.sqrt(d), 'bmix': jnp.zeros((L, d), jnp.float32), 'gamma_o': jnp.ones((L, d), jnp.float32), 'beta_o': jnp.zeros((L, d), jnp.float32)}
    _L1_gnn_all = _L1_gnn_setup()
    _L1_gnn_in = {k: v for k, v in _L1_gnn_all.items() if k in ('WM', 'bM', 'WU', 'bU', 'gamma_t', 'beta_t', 'Wmix', 'bmix', 'gamma_o', 'beta_o')}
    del _L1_gnn_all

    def _L2_gnn_setup():
        import jax
        import jax.numpy as jnp
        import numpy as np
        N_NODES = 50000
        N_RAND_EDGES = 25000
        D_IN = 64
        D_HID = 64
        D_OUT = 64

        def _spmm(x, edge_index, deg_inv_sqrt, num_nodes):
            src = edge_index[0]
            dst = edge_index[1]
            coef = deg_inv_sqrt[src] * deg_inv_sqrt[dst]
            msgs = x[src] * coef[:, None]
            return jax.ops.segment_sum(msgs, dst, num_segments=num_nodes)
        key = jax.random.key(seed)
        kx, ke, kd, kw1, kw2 = jax.random.split(key, 5)
        x = jax.random.normal(kx, (N_NODES, D_IN), dtype=jnp.float32)
        rand_edges = jax.random.randint(ke, (2, N_RAND_EDGES), 0, N_NODES, dtype=jnp.int64)
        loops = jnp.broadcast_to(jnp.arange(N_NODES, dtype=jnp.int64)[None, :], (2, N_NODES))
        edge_index_with_loops = jnp.concatenate([rand_edges, loops], axis=1)
        deg_inv_sqrt = jax.random.uniform(kd, (N_NODES,), dtype=jnp.float32, minval=0.05, maxval=1.0)
        W1 = jax.random.normal(kw1, (D_IN, D_HID), dtype=jnp.float32) * 0.01
        W2 = jax.random.normal(kw2, (D_HID, D_OUT), dtype=jnp.float32) * 0.01
        return {'x': x, 'edge_index_with_loops': edge_index_with_loops, 'deg_inv_sqrt': deg_inv_sqrt, 'num_nodes': N_NODES, 'W1': W1, 'W2': W2}
    _L2_gnn_all = _L2_gnn_setup()
    _L2_gnn_in = {k: v for k, v in _L2_gnn_all.items() if k in ('W1', 'W2')}
    del _L2_gnn_all

    def _L3_gnn_setup():
        import jax, jax.numpy as jnp
        import numpy as np
        from functools import partial
        N_NODES = 50000
        N_EDGES = 25000
        IN_F = 64
        OUT_F = 64
        key = jax.random.key(seed)
        k1, k2, k3, k4, k5 = jax.random.split(key, 5)
        stdv = 1.0 / np.sqrt(OUT_F)
        x = jax.random.normal(k1, (N_NODES, IN_F), dtype=jnp.float32)
        edge_index = jax.random.randint(k2, (2, N_EDGES), 0, N_NODES, dtype=jnp.int64)
        edge_weight = jax.random.uniform(k3, (N_EDGES,), dtype=jnp.float32)
        weight = jax.random.uniform(k4, (IN_F, OUT_F), minval=-stdv, maxval=stdv, dtype=jnp.float32)
        bias = jax.random.uniform(k5, (OUT_F,), minval=-stdv, maxval=stdv, dtype=jnp.float32)
        return {'x': x, 'edge_index': edge_index, 'edge_weight': edge_weight, 'weight': weight, 'bias': bias}
    _L3_gnn_all = _L3_gnn_setup()
    _L3_gnn_in = {k: v for k, v in _L3_gnn_all.items() if k in ('weight', 'bias')}
    del _L3_gnn_all
    return {'x': x, 'src': src, 'dst': dst, 'edge_attr_4': edge_attr_4, 'edge_attr_5': edge_attr_5, 'edge_weight': edge_weight, 'L0_gnn_W_lin': _L0_gnn_in['W_lin'], 'L0_gnn_b_lin': _L0_gnn_in['b_lin'], 'L0_gnn_W_edge': _L0_gnn_in['W_edge'], 'L0_gnn_b_edge': _L0_gnn_in['b_edge'], 'L0_gnn_att': _L0_gnn_in['att'], 'L0_gnn_bias': _L0_gnn_in['bias'], 'L1_gnn_WM': _L1_gnn_in['WM'], 'L1_gnn_bM': _L1_gnn_in['bM'], 'L1_gnn_WU': _L1_gnn_in['WU'], 'L1_gnn_bU': _L1_gnn_in['bU'], 'L1_gnn_gamma_t': _L1_gnn_in['gamma_t'], 'L1_gnn_beta_t': _L1_gnn_in['beta_t'], 'L1_gnn_Wmix': _L1_gnn_in['Wmix'], 'L1_gnn_bmix': _L1_gnn_in['bmix'], 'L1_gnn_gamma_o': _L1_gnn_in['gamma_o'], 'L1_gnn_beta_o': _L1_gnn_in['beta_o'], 'L2_gnn_W1': _L2_gnn_in['W1'], 'L2_gnn_W2': _L2_gnn_in['W2'], 'L3_gnn_weight': _L3_gnn_in['weight'], 'L3_gnn_bias': _L3_gnn_in['bias']}

def reference(x, src, dst, edge_attr_4, edge_attr_5, edge_weight, L0_gnn_W_lin, L0_gnn_b_lin, L0_gnn_W_edge, L0_gnn_b_edge, L0_gnn_att, L0_gnn_bias, L1_gnn_WM, L1_gnn_bM, L1_gnn_WU, L1_gnn_bU, L1_gnn_gamma_t, L1_gnn_beta_t, L1_gnn_Wmix, L1_gnn_bmix, L1_gnn_gamma_o, L1_gnn_beta_o, L2_gnn_W1, L2_gnn_W2, L3_gnn_weight, L3_gnn_bias):
    import jax
    import jax.numpy as jnp

    def _L0_gnn_ref(x, edge_index, edge_attr, W_lin, b_lin, W_edge, b_edge, att, bias):
        import jax, jax.numpy as jnp
        import numpy as np
        EMB = 64
        HEADS = 2
        NUM_BOND = 5
        NEG_SLOPE = 0.2
        N = x.shape[0]
        h = (x @ W_lin + b_lin).reshape(N, HEADS, EMB)
        ee = (edge_attr @ W_edge + b_edge).reshape(-1, HEADS, EMB)
        src = edge_index[0]
        dst = edge_index[1]
        x_i = h[src]
        x_j = h[dst] + ee
        att_i, att_j = (att[..., :EMB], att[..., EMB:])
        alpha = (x_i * att_i).sum(-1) + (x_j * att_j).sum(-1)
        alpha = jnp.where(alpha >= 0, alpha, NEG_SLOPE * alpha)
        amax = jax.ops.segment_max(alpha, src, num_segments=N)
        e = jnp.exp(alpha - amax[src])
        denom = jax.ops.segment_sum(e, src, num_segments=N)
        alpha = e / (denom[src] + 1e-16)
        messages = x_j * alpha[:, :, None]
        out = jax.ops.segment_sum(messages, src, num_segments=N)
        out = out.mean(axis=1) + bias
        return out

    def _L1_gnn_ref(node_feat, edge_feat, edge_src, edge_dst, WM, bM, WU, bU, gamma_t, beta_t, Wmix, bmix, gamma_o, beta_o):
        import jax, jax.numpy as jnp
        import numpy as np
        import math
        N_NODES = 50000
        N_EDGES = 15625
        HIDDEN = 64
        N_LAYERS = 4
        DELTA = 2.5
        N_AGG = 6
        N_SCALE = 3
        EPS_BN = 1e-05

        def _batchnorm(x, gamma, beta):
            mu = jnp.mean(x, axis=0)
            var = jnp.mean(jnp.square(x - mu), axis=0)
            return (x - mu) * jax.lax.rsqrt(var + EPS_BN) * gamma + beta

        def _pna_layer(h, src, dst, WM, bM, WU, bU, g_t, b_t, Wmix, bmix, g_o, b_o):
            n = h.shape[0]
            msg = jnp.concatenate([h[src], h[dst]], axis=1) @ WM + bM
            deg = jax.ops.segment_sum(jnp.ones(src.shape[0], h.dtype), dst, num_segments=n)
            denom = jnp.maximum(deg, 1.0)[:, None]
            s = jax.ops.segment_sum(msg, dst, num_segments=n)
            mean = s / denom
            mean_sq = jax.ops.segment_sum(msg * msg, dst, num_segments=n) / denom
            var = jax.nn.relu(mean_sq - mean * mean)
            std = jnp.sqrt(var + 1e-30)
            has = (deg > 0)[:, None]
            mx = jnp.where(has, jax.ops.segment_max(msg, dst, num_segments=n), 0.0)
            mn = jnp.where(has, jax.ops.segment_min(msg, dst, num_segments=n), 0.0)
            agg = jnp.concatenate([mean, mx, mn, std, var, s], axis=1)
            logD = jnp.log(deg + 1.0)[:, None]
            amp = logD / DELTA
            att = jnp.where(logD > 0, DELTA / jnp.where(logD > 0, logD, 1.0), 0.0)
            h_neigh = jnp.concatenate([agg, agg * amp, agg * att], axis=1)
            hu = jnp.concatenate([h, h_neigh], axis=1) @ WU + bU
            hu = hu * (1.0 / math.sqrt(n))
            hbn = _batchnorm(hu, g_t, b_t)
            hm = jax.nn.leaky_relu(hbn @ Wmix + bmix, 0.01)
            out = hm + h
            return jax.nn.relu(_batchnorm(out, g_o, b_o)) + h
        del edge_feat
        h = node_feat
        for i in range(N_LAYERS):
            h = _pna_layer(h, edge_src, edge_dst, WM[i], bM[i], WU[i], bU[i], gamma_t[i], beta_t[i], Wmix[i], bmix[i], gamma_o[i], beta_o[i])
        return h

    def _L2_gnn_ref(x, edge_index_with_loops, deg_inv_sqrt, num_nodes, W1, W2):
        import jax
        import jax.numpy as jnp
        import numpy as np
        N_NODES = 50000
        N_RAND_EDGES = 25000
        D_IN = 64
        D_HID = 64
        D_OUT = 64

        def _spmm(x, edge_index, deg_inv_sqrt, num_nodes):
            src = edge_index[0]
            dst = edge_index[1]
            coef = deg_inv_sqrt[src] * deg_inv_sqrt[dst]
            msgs = x[src] * coef[:, None]
            return jax.ops.segment_sum(msgs, dst, num_segments=num_nodes)
        h = _spmm(x, edge_index_with_loops, deg_inv_sqrt, num_nodes) @ W1
        h = jax.nn.relu(h)
        out = _spmm(h, edge_index_with_loops, deg_inv_sqrt, num_nodes) @ W2
        return out

    def _L3_gnn_ref(x, edge_index, edge_weight, weight, bias):
        import jax, jax.numpy as jnp
        import numpy as np
        from functools import partial
        N_NODES = 50000
        N_EDGES = 25000
        IN_F = 64
        OUT_F = 64
        num_nodes = x.shape[0]
        support = x @ weight
        row, col = (edge_index[0], edge_index[1])
        deg = jax.ops.segment_sum(jnp.ones_like(row, dtype=jnp.float32), row, num_segments=num_nodes)
        deg_inv_sqrt = jnp.where(deg > 0, jax.lax.rsqrt(jnp.maximum(deg, 1.0)), 0.0)
        norm = deg_inv_sqrt[row] * edge_weight * deg_inv_sqrt[col]
        msgs = norm[:, None] * support[col]
        output = jax.ops.segment_sum(msgs, row, num_segments=num_nodes)
        return output + bias
    edge_index = jnp.stack([src, dst])
    deg = jnp.maximum(jax.ops.segment_sum(jnp.ones(dst.shape, jnp.float32), dst, num_segments=50000), 1.0)
    deg_isqrt = deg ** (-0.5)
    h = jnp.maximum(_layernorm(x, axis=-1), 0.0)
    x = x + _L0_gnn_ref(h, edge_index, edge_attr_5, L0_gnn_W_lin, L0_gnn_b_lin, L0_gnn_W_edge, L0_gnn_b_edge, L0_gnn_att, L0_gnn_bias)
    h = jnp.maximum(_layernorm(x, axis=-1), 0.0)
    x = x + _L1_gnn_ref(h, edge_attr_4, src, dst, L1_gnn_WM, L1_gnn_bM, L1_gnn_WU, L1_gnn_bU, L1_gnn_gamma_t, L1_gnn_beta_t, L1_gnn_Wmix, L1_gnn_bmix, L1_gnn_gamma_o, L1_gnn_beta_o)
    h = jnp.maximum(_layernorm(x, axis=-1), 0.0)
    x = x + _L2_gnn_ref(h, edge_index, deg_isqrt, 50000, L2_gnn_W1, L2_gnn_W2)
    h = jnp.maximum(_layernorm(x, axis=-1), 0.0)
    x = x + _L3_gnn_ref(h, edge_index, edge_weight, L3_gnn_weight, L3_gnn_bias)
    return x

_drawn_inputs = setup_inputs


def setup_inputs(seed=0):
    import zlib

    import numpy as np

    out = dict(_drawn_inputs(seed))
    spreads = {'L0_gnn_b_lin': (0.0, 0.1),
     'L0_gnn_b_edge': (0.0, 0.1),
     'L0_gnn_bias': (0.0, 0.1),
     'L1_gnn_bM': (0.0, 0.1),
     'L1_gnn_bU': (0.0, 0.8),
     'L1_gnn_gamma_t': (1.0, 0.2),
     'L1_gnn_beta_t': (0.0, 0.319),
     'L1_gnn_bmix': (0.0, 0.285),
     'L1_gnn_gamma_o': (1.0, 0.2),
     'L1_gnn_beta_o': (0.0, 0.1)}
    factors = {'edge_weight': 3.314, 'L2_gnn_W1': 8.0, 'L2_gnn_W2': 8.0, 'L3_gnn_bias': 3.75}
    for name, (base, spread) in spreads.items():
        noise = np.random.default_rng([zlib.crc32(name.encode()), seed]).standard_normal(out[name].shape)
        drawn = base * np.exp(spread * noise) if base else spread * noise
        out[name] = jnp.asarray(drawn.astype(out[name].dtype))
    for name, factor in factors.items():
        out[name] = (out[name] * factor).astype(out[name].dtype)
    return out
```

```python
import numpy as np
import concourse.bass as bass
import concourse.mybir as mybir
from concourse.alu_op_type import AluOpType as ALU
from contextlib import ExitStack

F32 = mybir.dt.float32
BF16 = mybir.dt.bfloat16
I32 = mybir.dt.int32
ACT = mybir.ActivationFunctionType
AX = mybir.AxisListType

P = 128
N = 50000
E = 50000
D = 64
LAYERS = 4
TILES = 392
ROWS = TILES * P
HALF = TILES // 2
COLS = HALF * P
TB = 4
STEPS = TILES // TB
EB = TB * P
PAIRS = TB // 2
PAD_KEY = ROWS - 1
SORTF = 512
LEVELS = 16
SRC_MID = 25000
BIG = 3.0e38
EPS = 1e-5
DELTA = 2.5
NSCALE = 1.0 / float(np.sqrt(N))
S0W = 130
PAYW = 8
G1COLS = N - COLS
STATF = 346
STATN = G1COLS // STATF
CHUNK = 512
CHUNKS = COLS // CHUNK
assert STATN * STATF == G1COLS and CHUNKS * CHUNK == COLS and STEPS % 2 == 0


class Link:

    def __init__(self, eng, sem, base=0, per=None):
        self.eng, self.sem, self.base, self.per, self.n = eng, sem, base, per, 0

    def __call__(self, ins):
        self.n += 1
        ins.then_inc(self.sem, 1)
        self.eng.wait_ge(self.sem, self.base + self.n)

    def end(self):
        assert self.per is None or self.n == self.per, (self.n, self.per)


class Sems:

    def __init__(self, nc):
        self.ctx, self.nc, self.made = ExitStack(), nc, {}

    def __call__(self, name):
        if name not in self.made:
            self.made[name] = self.ctx.enter_context(self.nc.semaphore(name))
        return self.made[name]

    def pair(self, name):
        return [self(name + "_0"), self(name + "_1")]

    def start(self, prefixes):
        with self.nc.Block() as block:
            @block.sync
            def _(sp):
                for name in FREE_TWO:
                    if name.startswith(prefixes):
                        sp.sem_inc(self(name), 2)
                for name, k in FREE_ONE.items():
                    if name.startswith(prefixes):
                        sp.sem_inc(self(name), k)
                for name, k in FREE_DMA.items():
                    if name.startswith(prefixes):
                        for s in self.pair(name):
                            sp.sem_inc(s, k)


class PhaseSems(Sems):

    def __init__(self, nc, prefix, lasting):
        super().__init__(nc)
        self.prefix, self.lasting = prefix, lasting

    def __call__(self, name):
        if "_got_" in name and name[-1] in "01" or name == "passed":
            return self.lasting(name)
        return super().__call__(name)

    def __enter__(self):
        self.start((self.prefix,))
        return self

    def __exit__(self, *error):
        with self.nc.Block() as block:
            @block.sync
            def _(sp):
                for s in self.made.values():
                    sp.sem_clear(s)
        self.ctx.close()


def gather(pool, out, table, index):
    return pool.indirect_dma_start(out=out, out_offset=None, in_=table,
                                   in_offset=bass.IndirectOffsetOnAxis(ap=index, axis=0))


def passed(eng, sems):
    eng.sem_inc(sems("passed"), 1)


def node_rows(table, g, q, n=PAIRS):
    return table.rearrange("(g q p) d -> g p q d", g=2, p=P)[g][:, bass.ds(q, n), :]


def program(nc, io, out):
    with ExitStack() as ctx:
        sems = Sems(nc)
        ctx.enter_context(sems.ctx)

        def dram(name, shape, dt=F32):
            return nc.dram_tensor(name, shape, dt, kind="Internal").ap()

        def sb(name, shape, dt=F32):
            return ctx.enter_context(nc.sbuf_tensor(name, shape, dt))

        K = {}
        K["io"] = io
        K["out"] = out
        K["sorted_src"] = dram("sorted_src", [ROWS + 1, 1])
        K["mask_dst"] = dram("mask_dst", [STEPS, 2 * EB], BF16)
        K["mask_src"] = dram("mask_src", [STEPS, 2 * EB], BF16)
        K["edge_of"] = dram("edge_of", [P, TILES], I32)
        K["pay_rows"] = dram("pay_rows", [ROWS, PAYW])
        K["pay_sorted"] = dram("pay_sorted", [P, TILES * PAYW])
        K["att_table"] = dram("att_table", [ROWS, 2 * D])
        K["att_src"] = dram("att_src", [ROWS, 2])
        K["att_scan"] = dram("att_scan", [ROWS + 1, S0W])
        K["x1"] = dram("x1", [ROWS, D])
        K["x2"] = dram("x2", [ROWS, D])
        K["x3"] = dram("x3", [ROWS, D])
        K["hT"] = dram("hT", [P, COLS])
        K["msg_table"] = dram("msg_table", [ROWS, D])
        K["pna_scan"] = dram("pna_scan", [ROWS + 1, 4 * D])
        K["table1"] = dram("table1", [ROWS, D])
        K["table2"] = dram("table2", [ROWS, D])
        K["table3"] = dram("table3", [ROWS, D])
        K["sum_scan"] = dram("sum_scan", [ROWS + 1, D])

        K["ident"] = sb("ident", [P, P])
        K["fold"] = sb("fold", [P, P])
        K["dst_src"] = sb("dst_src", [P, TILES], I32)
        K["src_src"] = sb("src_src", [P, TILES], I32)
        K["end_dst"] = sb("end_dst", [P, HALF, 2], I32)
        K["end_src"] = sb("end_src", [P, HALF, 2], I32)
        for name in ("deg", "has", "inv", "amp", "att", "dis", "has_s", "dis_s"):
            K[name] = sb("node_" + name, [P, HALF, 2])

        start(nc, K, sems)
        sems.start(("pne_", "pnn_", "mix_", "pno_", "sum_"))
        with PhaseSems(nc, "sort_", sems) as own:
            sort_edges(nc, K, own)
        with PhaseSems(nc, "mask_", sems) as own:
            masks(nc, K, own)
        with PhaseSems(nc, "deg_", sems) as own:
            degrees(nc, K, own)
        with PhaseSems(nc, "pay_", sems) as own:
            payload(nc, K, own)
        with PhaseSems(nc, "att_", sems) as own:
            attention_tables(nc, K, own)
        with PhaseSems(nc, "ate_", sems) as own:
            attention_edges(nc, K, own)
        with PhaseSems(nc, "atn_", sems) as own:
            attention_nodes(nc, K, own)
        with nc.sbuf_tensor("U", [P, COLS], F32) as U:
            K["U"] = U
            with nc.Fori(0, LAYERS) as layer:
                pna_edges(nc, K, sems, layer)
                pna_nodes(nc, K, sems, layer)
                pna_mix(nc, K, sems, layer)
                pna_out(nc, K, sems, layer)
        with PhaseSems(nc, "end_", sems) as own:
            pna_end(nc, K, own)
        sum_edges(nc, K, sems, 0, K["table1"], "dst")
        with PhaseSems(nc, "hid_", sems) as own:
            conv_hidden(nc, K, own)
        sum_edges(nc, K, sems, 1, K["table2"], "dst")
        with PhaseSems(nc, "cou_", sems) as own:
            conv_out(nc, K, own)
        sum_edges(nc, K, sems, 2, K["table3"], "src")
        with PhaseSems(nc, "fin_", sems) as own:
            last_nodes(nc, K, own)


FREE_TWO = ("pay_index_free", "att_x_used", "att_h_turned", "ate_scored", "ate_scan_done", "atn_got_used",
            "pne_turned", "pne_scanned", "pne_copied", "pnn_got_used", "pnn_multiplied", "pnn_own", "mix_mixed", "mix_biased",
            "pno_made", "pno_rows", "end_summed", "sum_turned", "sum_scanned", "sum_copied", "hid_got_used",
            "cou_got_used", "cou_summed", "fin_got_used")
FREE_ONE = {"pnn_own_used": 2, "pnn_product_used": 1, "pnn_u_kept": 1, "pnn_aggT": 3, "pnn_agg_turned": 6, "pnn_u_turned": 2}
FREE_DMA = {"pay_stored": 16, "att_stored": 64, "ate_stored": 16, "atn_stored": 80, "pne_stored": 16,
            "pno_stored": 48, "end_stored": 64, "sum_stored": 16, "hid_stored": 32, "cou_stored": 64,
            "fin_stored": 32}


def start(nc, K, sems):
    io = K["io"]
    with nc.Block() as block:
        @block.sync
        def _(sp):
            sp.dma_start(K["ident"][:], io["consts"][:, 0:P]).then_inc(sems("const_in"), 16)
            sp.dma_start(K["fold"][:], io["consts"][:, P:2 * P]).then_inc(sems("const_in"), 16)
            sp.dma_start(K["dst_src"][:], io["src_cols"]).then_inc(sems("const_in"), 16)
            for name in ("att_scan", "pna_scan", "sum_scan"):
                table = K[name][ROWS:ROWS + 1, :]
                sp.dma_start(table, io["zeros"][:, 0:table.shape[1]]).then_inc(sems("const_in"), 16)
            sp.wait_ge(sems("const_in"), 96)


class Turn:

    def __init__(self, rep, i, at, steps=STEPS):
        self.rep, self.i, self.at, self.steps, self.h = rep, i, at, steps, at % 2
        self.s = i * 2 + at

    def n(self, k=1):
        return self.rep * (self.steps * k) + self.i * (2 * k) + (self.at + 1) * k

    def slot(self, k=16):
        return self.rep * (self.steps // 2 * k) + self.i * k + (self.at // 2 + 1) * k


def pipeline(eng, sem, parts, rep=0, steps=STEPS, peel=0):
    total = steps * sum(k for _, _, k in parts)
    lag = max([peel] + [l for l, _, _ in parts])
    turns = (steps - lag) // 2
    per_turn = 2 * sum(k for _, _, k in parts)
    link = Link(eng, sem, rep * total)

    def time(t, i=0, inside=False):
        for l, part, k in parts:
            if inside or 0 <= t - l < steps:
                before = link.n
                turn = Turn(rep, i, t - l, steps)
                turn.first = not inside and t - l < 2
                part(turn, link)
                assert link.n == before + k, (part, link.n - before, k)

    for t in range(lag):
        time(t)
    done = link.n
    with eng.Fori(0, turns) as i:
        link.base, link.n = rep * total + done + i * per_turn, 0
        time(lag, i, True)
        time(lag + 1, i, True)
    link.base, link.n = rep * total, done + turns * per_turn
    for t in range(lag + 2 * turns, steps + lag):
        time(t)


def sort_edges(nc, K, sems):
    io = K["io"]
    nblk = SORTF // P
    with ExitStack() as ctx:
        sb = lambda n, s, dt=F32: ctx.enter_context(nc.sbuf_tensor("sort_" + n, s, dt))
        key_i = sb("key_i", [P, SORTF], I32)
        word_i = sb("word_i", [P, SORTF], I32)
        low_i = sb("low_i", [P, SORTF], I32)
        src_f = sb("src_f", [P, SORTF])
        neg = sb("neg", [P, SORTF])
        t1 = sb("t1", [P, SORTF])
        t2 = sb("t2", [P, SORTF])
        index = sb("index", [P, SORTF])
        signs = sb("signs", [P, LEVELS, SORTF])
        buf = [sb("a", [P, SORTF]), sb("b", [P, SORTF])]
        ps = ctx.enter_context(nc.psum_tensor("sort_ps", [P, SORTF], F32))
        ps2 = ctx.enter_context(nc.psum_tensor("sort_ps2", [P, SORTF], F32))
        loaded, turned, to_turn = sems("sort_in"), sems("sort_turned"), sems("sort_to_turn")
        ident = K["ident"]
        done, stored = sems("sort_done"), sems("sort_stored")

        plan = []
        cur = 0
        for level in range(1, LEVELS + 1):
            plan.append(("sign", level, cur))
            j = level - 1
            if j >= 9:
                plan.append(("turn", level, cur))
                while j >= 9:
                    plan.append(("step", j - 9, cur))
                    cur ^= 1
                    j -= 1
                plan.append(("turn", level, cur))
            while j >= 0:
                plan.append(("step", j, cur))
                cur ^= 1
                j -= 1
        turn_bufs = [c for kind, _, c in plan if kind == "turn"]

        with nc.Block() as block:
            @block.sync
            def _(sp):
                sp.dma_start(key_i[:], io["src_sort"]).then_inc(loaded, 16)
                sp.dma_start(index[:], io["sort_index"]).then_inc(loaded, 16)
                sp.dma_start(signs[:], io["sort_signs"]).then_inc(loaded, 16)
                sp.wait_ge(done, 1)
                sp.dma_start(K["sorted_src"][1:ROWS + 1, :].rearrange("(p f) o -> p (f o)", f=SORTF),
                             src_f[0:ROWS // SORTF, :]).then_inc(stored, 16)
                sp.dma_start(K["sorted_src"][0:1, :], io["minus_one"]).then_inc(stored, 16)
                sp.wait_ge(done, 2)
                sp.dma_start(K["edge_of"], low_i[:, 0:TILES]).then_inc(stored, 16)
                sp.wait_ge(stored, 48)

            @block.vector
            def _(dve):
                link = Link(dve, sems("sort_link"))
                V = nc.vector
                dve.wait_ge(loaded, 48)
                link(V.tensor_copy(src_f[:], key_i[:]))
                link(V.tensor_scalar(neg[:], src_f[:], float(SRC_MID), None, ALU.is_lt))
                link(V.tensor_scalar(t1[:], src_f[:], -2.0, float(0x807F + SRC_MID - 0x80 + SRC_MID), ALU.mult, ALU.add))
                link(V.tensor_tensor(t1[:], t1[:], neg[:], ALU.mult))
                link(V.scalar_tensor_tensor(t1[:], src_f[:], float(0x80 - SRC_MID), t1[:], ALU.add, ALU.add))
                link(V.tensor_copy(word_i[:], t1[:]))
                link(V.tensor_scalar(word_i[:], word_i[:], 16, None, ALU.logical_shift_left))
                link(V.tensor_scalar(t2[:], index[:], -2.0, 65535.0, ALU.mult, ALU.add))
                link(V.tensor_tensor(t2[:], t2[:], neg[:], ALU.mult))
                link(V.tensor_tensor(t2[:], t2[:], index[:], ALU.add))
                link(V.tensor_copy(low_i[:], t2[:]))
                link(V.tensor_tensor(buf[0][:].bitcast(I32), word_i[:], low_i[:], ALU.bitwise_or))
                nturn = 0
                for kind, a, c in plan:
                    x, y = buf[c], buf[c ^ 1]
                    if kind == "sign":
                        link(V.tensor_tensor(x[:], x[:], signs[:, a - 1, :], ALU.mult))
                    elif kind == "turn":
                        nturn += 1
                        V.sem_inc(to_turn, 1)
                        dve.wait_ge(turned, nturn)
                        link(V.tensor_copy(x[:], ps[:]))
                    else:
                        xs = x[:].rearrange("p (b t l) -> p b t l", t=2, l=1 << a)
                        ys = y[:].rearrange("p (b t l) -> p b t l", t=2, l=1 << a)
                        V.tensor_tensor(ys[:, :, 0], xs[:, :, 0], xs[:, :, 1], ALU.min).then_inc(sems("sort_link"), 1)
                        link.n += 1
                        link(V.tensor_tensor(ys[:, :, 1], xs[:, :, 0], xs[:, :, 1], ALU.max))
                final = buf[cur][:].bitcast(I32)
                link(V.tensor_scalar(word_i[:], final, 31, 1, ALU.logical_shift_right, ALU.bitwise_and))
                link(V.tensor_copy(neg[:], word_i[:]))
                link(V.tensor_scalar(key_i[:], final, 16, 0x7FFF, ALU.logical_shift_right, ALU.bitwise_and))
                link(V.tensor_copy(src_f[:], key_i[:]))
                link(V.tensor_scalar(low_i[:], final, 0xFFFF, None, ALU.bitwise_and))
                link(V.tensor_copy(index[:], low_i[:]))
                link(V.tensor_scalar(t1[:], src_f[:], -2.0, float(0x807F + SRC_MID - 0x8000 - SRC_MID + 0x80), ALU.mult, ALU.add))
                link(V.tensor_tensor(t1[:], t1[:], neg[:], ALU.mult))
                link(V.scalar_tensor_tensor(src_f[:], src_f[:], float(SRC_MID - 0x80), t1[:], ALU.add, ALU.add))
                V.sem_inc(done, 1)
                link(V.tensor_scalar(t2[:], index[:], -2.0, 65535.0, ALU.mult, ALU.add))
                link(V.tensor_tensor(t2[:], t2[:], neg[:], ALU.mult))
                link(V.tensor_tensor(index[:], index[:], t2[:], ALU.add))
                V.sem_inc(to_turn, 1)
                dve.wait_ge(turned, nturn + 1)
                cols = lambda t: t.rearrange("p (r c) -> p r c", c=nblk)
                psc = lambda t: t.rearrange("p (c r) -> p r c", c=nblk)
                link(V.tensor_copy(cols(K["src_src"][:]), psc(ps[:])[:, 0:ROWS // SORTF, :]))
                link(V.tensor_copy(cols(low_i[:, 0:TILES]), psc(ps2[:])[:, 0:ROWS // SORTF, :]))
                V.sem_inc(done, 1)

            @block.tensor
            def _(pe):
                for n, c in enumerate(turn_bufs):
                    pe.wait_ge(to_turn, n + 1)
                    for b in range(nblk):
                        last = nc.tensor.transpose(ps[:, b * P:(b + 1) * P], buf[c][:, b * P:(b + 1) * P], ident[:])
                    last.then_inc(turned, 1)
                pe.wait_ge(to_turn, len(turn_bufs) + 1)
                for b in range(nblk):
                    nc.tensor.transpose(ps[:, b * P:(b + 1) * P], src_f[:, b * P:(b + 1) * P], ident[:])
                    last = nc.tensor.transpose(ps2[:, b * P:(b + 1) * P], index[:, b * P:(b + 1) * P], ident[:])
                last.then_inc(turned, 1)


def masks(nc, K, sems):
    io = K["io"]
    r = ROWS // EB
    with ExitStack() as ctx:
        sb = lambda n, s, dt=F32: ctx.enter_context(nc.sbuf_tensor("mask_" + n, s, dt))
        key_i, prev_i = sb("key_i", [r, EB], I32), sb("prev_i", [r, EB], I32)
        key, prev = [sb("key0", [r, EB]), sb("key1", [r, EB])], [sb("prev0", [r, EB]), sb("prev1", [r, EB])]
        keep = sb("keep", [r, EB])
        both = [sb("both0", [r, 2, EB], BF16), sb("both1", [r, 2, EB], BF16)]
        loaded, ready, stored = sems("mask_in"), sems("mask_ready"), sems("mask_stored")
        rows = lambda t, o: t[o:o + ROWS, :].rearrange("(p f) o -> p (f o)", f=EB)
        with nc.Block() as block:
            @block.sync
            def _(sp):
                sp.dma_start(key_i[:], rows(io["dst_line"], 1)).then_inc(loaded, 16)
                sp.dma_start(prev_i[:], rows(io["dst_line"], 0)).then_inc(loaded, 16)
                sp.dma_start(key[1][:], rows(K["sorted_src"], 1)).then_inc(loaded, 16)
                sp.dma_start(prev[1][:], rows(K["sorted_src"], 0)).then_inc(loaded, 16)
                for n, name in enumerate(("mask_dst", "mask_src")):
                    sp.wait_ge(ready, n + 1)
                    sp.dma_start(K[name], both[n][:].rearrange("p a f -> p (a f)")).then_inc(stored, 16)
                sp.wait_ge(stored, 32)

            @block.vector
            def _(dve):
                link = Link(dve, sems("mask_link"))
                V = nc.vector
                dve.wait_ge(loaded, 64)
                V.tensor_copy(key[0][:], key_i[:]).then_inc(sems("mask_link"), 1)
                link.n += 1
                link(V.tensor_copy(prev[0][:], prev_i[:]))
                for n in range(2):
                    link(V.tensor_tensor(keep[:], key[n][:], prev[n][:], ALU.is_equal))
                    link(V.tensor_copy(both[n][:, 0, :], keep[:]))
                    link(V.tensor_scalar(both[n][:, 1, :], keep[:], -1.0, BIG, ALU.add, ALU.mult))
                    V.sem_inc(ready, 1)


def degrees(nc, K, sems):
    io = K["io"]
    with ExitStack() as ctx:
        sb = lambda n, s, dt=F32: ctx.enter_context(nc.sbuf_tensor("deg_" + n, s, dt))
        pb = lambda n: ctx.enter_context(nc.psum_tensor("deg_" + n, [P, 512], F32))
        iota = sb("iota", [P, TILES])
        tri = sb("tri", [P, P])
        ones = sb("ones", [P, TILES])
        zero = sb("zero", [P, TILES], BF16)
        dst_i = sb("dst_i", [P, TILES], I32)
        part_i = sb("part_i", [P, TILES], I32)
        low, high = [sb("low0", [P, TILES]), sb("low1", [P, TILES])], [sb("high0", [P, TILES]), sb("high1", [P, TILES])]
        hot_low, hot_high = sb("hot_low", [P, 2, P], BF16), sb("hot_high", [P, 2, TILES], BF16)
        count = [pb("count0"), pb("count1")]
        before, total = pb("before"), pb("total")
        deg = [sb("d0", [P, TILES]), sb("d1", [P, TILES])]
        degm, tmp, cum = sb("degm", [P, TILES]), sb("tmp", [P, TILES]), sb("cum", [P, TILES])
        tot = sb("tot", [P, TILES])
        loaded, hot, used, counted = sems("deg_in"), sems("deg_hot"), sems("deg_hot_free"), sems("deg_counted")
        ready, summed = sems("deg_ready"), sems("deg_summed")
        asked, rooted = sems("deg_asked"), sems("deg_rooted")
        by_pair = lambda t: t.rearrange("p (g q) -> p q g", g=2)
        with nc.Block() as block:
            @block.sync
            def _(sp):
                sp.dma_start(iota[:], io["consts"][:, 4 * P:4 * P + TILES]).then_inc(loaded, 16)
                sp.dma_start(tri[:], io["consts"][:, 2 * P:3 * P]).then_inc(loaded, 16)
                sp.dma_start(dst_i[:], io["dst_cols"]).then_inc(loaded, 16)
                sp.wait_ge(loaded, 48)

            @block.vector
            def _(dve):
                link = Link(dve, sems("deg_link"))
                V = nc.vector
                dve.wait_ge(loaded, 48)
                link(V.memset(ones[:], 1.0))
                for n, keys in enumerate((dst_i, K["src_src"])):
                    link(V.tensor_scalar(part_i[:], keys[:], P - 1, None, ALU.bitwise_and))
                    link(V.tensor_copy(low[n][:], part_i[:]))
                    link(V.tensor_scalar(part_i[:], keys[:], 7, None, ALU.logical_shift_right))
                    link(V.tensor_copy(high[n][:], part_i[:]))
                link(V.memset(zero[:], 0.0))
                link(V.memset(hot_high[:], 0.0))
                V.sem_inc(ready, 1)
                with dve.Fori(0, TILES) as i:
                    for n in range(2):
                        dve.wait_ge(used, i * 2 + (n + 1))
                        V.tensor_scalar(hot_low[:, n, :], iota[:, 0:P], low[n][:, bass.ds(i, 1)], None, ALU.is_equal)
                        V.tensor_scalar(hot_high[:, n, :], iota[:], high[n][:, bass.ds(i, 1)], None,
                                        ALU.is_equal).then_inc(hot, 1)
                dve.wait_ge(counted, 1)
                for n in range(2):
                    link(V.tensor_copy(deg[n][:], count[n][:, 0:TILES]))
                    V.sem_inc(ready, 1)
                for n, end in enumerate((K["end_dst"], K["end_src"])):
                    dve.wait_ge(summed, n + 1)
                    link(V.tensor_copy(tot[:], total[:, 0:TILES]))
                    link(V.tensor_tensor_scan(cum[:], ones[:], tot[:], 0.0, ALU.mult, ALU.add))
                    link(V.tensor_tensor(cum[:], cum[:], tot[:], ALU.subtract))
                    link(V.tensor_tensor(cum[:], cum[:], before[:, 0:TILES], ALU.add))
                    link(V.tensor_scalar(tot[:], deg[n][:], 1.0, None, ALU.min))
                    link(V.scalar_tensor_tensor(cum[:], cum[:], -1.0 - ROWS, tot[:], ALU.add, ALU.mult))
                    link(V.tensor_scalar(cum[:], cum[:], float(ROWS), None, ALU.add))
                    link(V.tensor_copy(end[:], by_pair(cum[:])))
                    V.sem_inc(ready, 1)
                link(V.tensor_copy(K["deg"][:], by_pair(deg[0][:])))
                link(V.tensor_scalar(K["has"][:], K["deg"][:], 1.0, None, ALU.min))
                link(V.tensor_copy(K["has_s"][:], by_pair(deg[1][:])))
                link(V.tensor_scalar(degm[:], K["has_s"][:].rearrange("p q g -> p (q g)"), 1.0, None, ALU.max))
                link(V.tensor_scalar(K["has_s"][:], K["has_s"][:], 1.0, None, ALU.min))
                V.sem_inc(asked, 1)
                dve.wait_ge(rooted, 1)
                flat = lambda t: t[:].rearrange("p q g -> p (q g)")
                link(V.reciprocal(cum[:], tmp[:]))
                link(V.tensor_tensor(flat(K["dis_s"]), cum[:], flat(K["has_s"]), ALU.mult))
                link(V.tensor_scalar(degm[:], flat(K["deg"]), 1.0, None, ALU.max))
                link(V.tensor_scalar(tot[:], flat(K["deg"]), 1.0, None, ALU.add))
                V.sem_inc(asked, 1)
                link(V.reciprocal(cum[:], degm[:]))
                link(V.tensor_tensor(flat(K["inv"]), cum[:], flat(K["has"]), ALU.mult))
                dve.wait_ge(rooted, 3)
                link(V.reciprocal(flat(K["dis"]), tmp[:]))
                link(V.tensor_scalar(flat(K["amp"]), tot[:], NSCALE / DELTA, None, ALU.mult))
                link(V.tensor_scalar(tot[:], tot[:], 0.5, None, ALU.max))
                link(V.reciprocal(cum[:], tot[:]))
                link(V.scalar_tensor_tensor(flat(K["att"]), cum[:], DELTA * NSCALE, flat(K["has"]), ALU.mult, ALU.mult))

            @block.tensor
            def _(pe):
                pe.wait_ge(ready, 1)
                for n in range(2):
                    nc.tensor.matmul(count[n][:, 0:TILES], zero[:, 0:P], hot_high[:, n, :],
                                     start=True, stop=False).then_inc(used, 1)
                with pe.Fori(0, TILES) as i:
                    for n in range(2):
                        pe.wait_ge(hot, i * 2 + (n + 1))
                        nc.tensor.matmul(count[n][:, 0:TILES], hot_low[:, n, :], hot_high[:, n, :],
                                         start=False, stop=False).then_inc(used, 1)
                for n in range(2):
                    last = nc.tensor.matmul(count[n][:, 0:TILES], zero[:, 0:P], zero[:],
                                            start=False, stop=True)
                last.then_inc(counted, 1)
                for n in range(2):
                    pe.wait_ge(ready, 3 + n)
                    nc.tensor.matmul(before[:, 0:TILES], tri[:], deg[n][:], start=True, stop=True)
                    nc.tensor.matmul(total[:, 0:TILES], ones[:, 0:P], deg[n][:], start=True, stop=True).then_inc(summed, 1)

            @block.scalar
            def _(act):
                act.wait_ge(asked, 1)
                nc.scalar.activation(tmp[:], degm[:], ACT.Sqrt).then_inc(rooted, 1)
                act.wait_ge(asked, 2)
                nc.scalar.activation(tmp[:], degm[:], ACT.Sqrt).then_inc(rooted, 1)
                nc.scalar.activation(tot[:], tot[:], ACT.Ln).then_inc(rooted, 1)


def payload(nc, K, sems):
    io = K["io"]
    with ExitStack() as ctx:
        sb = lambda n, s, dt=F32: ctx.enter_context(nc.sbuf_tensor("pay_" + n, s, dt))
        rows = sb("natural", [P, TILES, PAYW])
        dst = sb("dst", [P, TILES], I32)
        index = sb("index", [P, 2, TB], I32)
        got = sb("got", [P, 2, TB, PAYW])
        loaded, packed, put = sems("pay_in"), sems("pay_packed"), sems("pay_put")
        index_in, index_free = sems.pair("pay_index_in"), sems("pay_index_free")
        got_in, stored = sems.pair("pay_got"), sems.pair("pay_stored")
        with nc.Block() as block:
            @block.sync
            def _(sp):
                sp.dma_start(rows[:], io["pay"].rearrange("(p t) c -> p t c", p=P)).then_inc(loaded, 16)
                sp.dma_start(dst[:], io["dst_line"][1:ROWS + 1, :].rearrange("(p t) o -> p (t o)", p=P)).then_inc(loaded, 16)
                sp.wait_ge(packed, 1)
                sp.dma_start(K["pay_rows"].rearrange("(p t) c -> p t c", p=P), rows[:]).then_inc(put, 16)
                sp.wait_ge(put, 16)

            @block.vector
            def _(dve):
                dve.wait_ge(loaded, 32)
                nc.vector.tensor_copy(rows[:, :, PAYW - 1].bitcast(I32), dst[:]).then_inc(packed, 1)
        with nc.Block() as block:
            @block.sync
            def _(sp):
                with sp.Fori(0, STEPS // 2) as i:
                    for h in range(2):
                        t = Turn(0, i, h)
                        sp.wait_ge(index_free, t.n())
                        sp.dma_start(index[:, h, :], K["edge_of"][:, bass.ds(i * (2 * TB) + h * TB, TB)]).then_inc(index_in[h], 16)

            @block.gpsimd
            def _(pool):
                with pool.Fori(0, STEPS // 2) as i:
                    for h in range(2):
                        t = Turn(0, i, h)
                        pool.wait_ge(index_in[h], t.slot())
                        pool.wait_ge(stored[h], t.slot())
                        passed(pool, sems)
                        for j in range(TB):
                            gather(pool, got[:, h, j, :], K["pay_rows"], index[:, h, j:j + 1]).then_inc(got_in[h], 16)

            @block.scalar
            def _(act):
                with act.Fori(0, STEPS // 2) as i:
                    for h in range(2):
                        t = Turn(0, i, h)
                        act.wait_ge(got_in[h], t.slot(16 * TB))
                        act.sem_inc(index_free, 1)
                        act.dma_start(K["pay_sorted"][:, bass.ds(i * (2 * TB * PAYW) + h * TB * PAYW, TB * PAYW)],
                                      got[:, h].rearrange("p j c -> p (j c)")).then_inc(stored[h], 16)
                for h in range(2):
                    act.wait_ge(stored[h], 16 + 16 * (STEPS // 2))


class Norm:
    LINKS = 7

    def __init__(self, sb, sems, name):
        self.total, self.cent = sb(name + "_total", [P, TB]), sb(name + "_cent", [P, TB, D])
        self.sq, self.ss = sb(name + "_sq", [P, TB, D]), sb(name + "_ss", [P, TB])
        self.sd, self.rs = sb(name + "_sd", [P, TB]), sb(name + "_rs", [P, TB])
        self.eps = sb(name + "_eps", [P, 1])
        self.asked, self.rooted = sems(name + "_asked"), sems(name + "_rooted")

    def vector(self, nc, dve, link, x, out, count):
        V = nc.vector
        link(V.reduce_sum(self.total[:], x, axis=AX.X))
        link(V.tensor_scalar(self.total[:], self.total[:], -1.0 / D, None, ALU.mult))
        link(V.tensor_tensor(self.cent[:], x, per_tile(self.total[:]), ALU.add))
        link(V.tensor_tensor(self.sq[:], self.cent[:], self.cent[:], ALU.mult))
        link(V.reduce_sum(self.ss[:], self.sq[:], axis=AX.X))
        V.sem_inc(self.asked, 1)
        dve.wait_ge(self.rooted, count)
        link(V.reciprocal(self.rs[:], self.sd[:]))
        link(V.scalar_tensor_tensor(out, self.cent[:], 0.0, per_tile(self.rs[:]), ALU.max, ALU.mult))

    def scalar(self, nc, act, count):
        act.wait_ge(self.asked, count)
        nc.scalar.activation(self.sd[:], self.ss[:], ACT.Sqrt, bias=self.eps[:], scale=1.0 / D).then_inc(self.rooted, 1)


def per_tile(v):
    return v.unsqueeze(2).broadcast_to([P, v.shape[1], D])


def per_feature(v, n=TB):
    return v.unsqueeze(1).broadcast_to([P, n, v.shape[1]])


def attention_tables(nc, K, sems):
    io = K["io"]
    with ExitStack() as ctx:
        sb = lambda n, s, dt=F32: ctx.enter_context(nc.sbuf_tensor("att_" + n, s, dt))
        pb = lambda n, s: ctx.enter_context(nc.psum_tensor("att_" + n, s, F32))
        x, h_ = sb("x", [P, 2, PAIRS, 2, D]), sb("h", [P, 2, PAIRS, 2 * D])
        hT = sb("hT", [P, 2, PAIRS * P])
        w = sb("w", [P, 4 * D])
        bias, att = sb("bias", [P, 2 * D]), sb("att", [P, 2 * D])
        rows, prod = sb("rows", [P, 2, TB, 2 * D]), sb("prod", [P, TB, 2 * D])
        srow = sb("srow", [P, 2, TB, 2])
        psT, psR = pb("psT", [P, 2, 512]), pb("psR", [P, 2, TB * 2 * D])
        norm = Norm(sb, sems, "att_norm")
        loaded, x_in, x_used = sems("att_in"), sems.pair("att_x_in"), sems("att_x_used")
        h_ready, h_turned, hT_ready, multiplied, rows_ready = (sems("att_" + n) for n in
            ("h_ready", "h_turned", "hT_ready", "multiplied", "rows_ready"))
        stored = sems.pair("att_stored")
        LINKS = 2 * (Norm.LINKS + 3)
        with nc.Block() as block:
            @block.sync
            def _(sp):
                sp.dma_start(w[:], io["w_lin"]).then_inc(loaded, 16)
                sp.dma_start(bias[:], io["b_lin"]).then_inc(loaded, 16)
                sp.dma_start(att[:], io["att_own"]).then_inc(loaded, 16)
                with sp.Fori(0, STEPS // 2) as i:
                    for h in range(2):
                        t = Turn(0, i, h)
                        sp.wait_ge(x_used, t.n())
                        for g in range(2):
                            sp.dma_start(x[:, h, :, g, :], node_rows(io["x"], g, i * (2 * PAIRS) + h * PAIRS)).then_inc(x_in[h], 16)

            @block.vector
            def _(dve):
                V = nc.vector
                dve.wait_ge(loaded, 48)
                link = Link(dve, sems("att_first"))
                link(V.memset(norm.eps[:], EPS))
                with dve.Fori(0, STEPS // 2) as i:
                    link = Link(dve, sems("att_link"), i * LINKS, LINKS)
                    for h in range(2):
                        t = Turn(0, i, h)
                        dve.wait_ge(x_in[h], t.slot(32))
                        dve.wait_ge(h_turned, t.n())
                        norm.vector(nc, dve, link, x[:, h].rearrange("p k g d -> p (k g) d"),
                                    h_[:, h].rearrange("p k (g d) -> p (k g) d", g=2), t.n())
                        V.sem_inc(x_used, 1)
                        V.sem_inc(h_ready, 1)
                        dve.wait_ge(multiplied, t.n())
                        dve.wait_ge(stored[h], t.slot(64))
                        link(V.tensor_tensor(rows[:, h], psR[:, h].rearrange("p (n c) -> p n c", n=TB),
                                             per_feature(bias[:]), ALU.add))
                        link(V.tensor_tensor(prod[:], rows[:, h], per_feature(att[:]), ALU.mult))
                        link(V.reduce_sum(srow[:, h].rearrange("p n a -> p (n a)"),
                                          prod[:].rearrange("p n (a d) -> p (n a) d", a=2), axis=AX.X))
                        V.sem_inc(rows_ready, 1)
                    link.end()

            @block.scalar
            def _(act):
                nc.scalar.preload_act_table(ACT.Sqrt)
                with act.Fori(0, STEPS // 2) as i:
                    for h in range(2):
                        t = Turn(0, i, h)
                        norm.scalar(nc, act, t.n())
                        act.wait_ge(h_turned, t.n() + 2)
                        nc.scalar.copy(hT[:, h], psT[:, h, 0:PAIRS * P]).then_inc(hT_ready, 1)
                        act.wait_ge(rows_ready, t.n())
                        for g in range(2):
                            q = i * (2 * PAIRS) + h * PAIRS
                            act.dma_start(node_rows(K["att_table"], g, q),
                                          rows[:, h].rearrange("p (k g) c -> p k g c", g=2)[:, :, g, :]).then_inc(stored[h], 16)
                            act.dma_start(node_rows(K["att_src"], g, q),
                                          srow[:, h].rearrange("p (k g) c -> p k g c", g=2)[:, :, g, :]).then_inc(stored[h], 16)
                for h in range(2):
                    act.wait_ge(stored[h], 64 + 64 * (STEPS // 2))

            @block.tensor
            def _(pe):
                pe.wait_ge(loaded, 48)
                with pe.Fori(0, STEPS // 2) as i:
                    for h in range(2):
                        t = Turn(0, i, h)
                        pe.wait_ge(h_ready, t.n())
                        for k in range(PAIRS):
                            last = nc.tensor.transpose(psT[:, h, k * P:(k + 1) * P], h_[:, h, k, :], K["ident"][:])
                        last.then_inc(h_turned, 1)
                        pe.wait_ge(hT_ready, t.n())
                        for k in range(PAIRS):
                            last = nc.tensor.matmul(psR[:, h, k * 4 * D:(k + 1) * 4 * D], hT[:, h, k * P:(k + 1) * P], w[:],
                                                    start=True, stop=True)
                        last.then_inc(multiplied, 1)


def attention_edges(nc, K, sems):
    io = K["io"]
    with ExitStack() as ctx:
        sb = lambda n, s, dt=F32: ctx.enter_context(nc.sbuf_tensor("ate_" + n, s, dt))
        pb = lambda n, s: ctx.enter_context(nc.psum_tensor("ate_" + n, s, F32))
        w_edge, att, sel = sb("w_edge", [6, 2 * D]), sb("att", [P, 2]), sb("sel", [2, P])
        index = sb("index", [P, 2, TB], I32)
        pay = sb("pay", [P, 2, TB, PAYW])
        mask = sb("mask", [2, 2, 2, EB], BF16)
        got, gots = sb("got", [P, 2, TB, 2 * D]), sb("gots", [P, 2, TB, 2])
        payT, xT = sb("payT", [PAYW, EB]), sb("xT", [P, 2, EB])
        score, lrel = sb("score", [2, EB]), sb("lrel", [2, EB])
        top = sb("top", [2, 2, EB + 1])
        down, diff = sb("down", [2, EB]), sb("diff", [2, EB])
        r0, r, p = sb("r0", [2, EB]), sb("r", [2, EB]), sb("p", [2, EB])
        px = sb("px", [P, EB])
        num, den = sb("num", [P, 2, EB]), sb("den", [2, 2, EB])
        out = sb("out", [P, 2, TB, S0W])
        psP, psX = pb("psP", [PAYW, EB]), pb("psX", [P, EB])
        psS = pb("psS", [2, EB])
        psR, psB = pb("psR", [P, EB]), pb("psB", [P, EB])
        psN, psD = pb("psN", [P, TB, 2 * D]), pb("psD", [P, TB, P])
        loaded = sems("ate_in")
        n_ = lambda name: sems("ate_" + name)
        index_in, pay_in, mask_in, got_in, stored = (sems.pair("ate_" + n) for n in
                                                     ("index_in", "pay_in", "mask_in", "got", "stored"))
        LINKS = 2 * 9
        with nc.Block() as block:
            @block.sync
            def _(sp):
                sp.dma_start(w_edge[:], io["w_edge"]).then_inc(loaded, 16)
                sp.dma_start(att[:], io["att_other"]).then_inc(loaded, 16)
                sp.dma_start(sel[:], io["consts"][0:2, 3 * P:4 * P]).then_inc(loaded, 16)
                with sp.Fori(0, STEPS // 2) as i:
                    for h in range(2):
                        t = Turn(0, i, h)
                        s = i * 2 + h
                        sp.wait_ge(n_("scored"), t.n())
                        sp.dma_start(index[:, h, :], K["src_src"][:, bass.ds(s * TB, TB)]).then_inc(index_in[h], 16)
                        sp.dma_start(pay[:, h].rearrange("p j c -> p (j c)"),
                                     K["pay_sorted"][:, bass.ds(s * (TB * PAYW), TB * PAYW)]).then_inc(pay_in[h], 16)
                        sp.wait_ge(n_("scan_done"), t.n())
                        for a in range(2):
                            sp.dma_start(mask[a:a + 1, h].rearrange("p a f -> p (a f)"),
                                         K["mask_src"][bass.ds(s, 1), :]).then_inc(mask_in[h], 16)

            @block.gpsimd
            def _(pool):
                with pool.Fori(0, STEPS // 2) as i:
                    for h in range(2):
                        t = Turn(0, i, h)
                        pool.wait_ge(index_in[h], t.slot())
                        pool.wait_ge(pay_in[h], t.slot())
                        passed(pool, sems)
                        for j in range(TB):
                            gather(pool, gots[:, h, j, :], K["att_src"], index[:, h, j:j + 1]).then_inc(got_in[h], 16)
                            gather(pool, got[:, h, j, :], K["att_table"],
                                   pay[:, h, j, PAYW - 1:PAYW].bitcast(I32)).then_inc(got_in[h], 16)

            @block.tensor
            def _(pe):
                ident = K["ident"]
                pe.wait_ge(loaded, 48)
                with pe.Fori(0, STEPS // 2) as i:
                    for h in range(2):
                        t = Turn(0, i, h)
                        pe.wait_ge(pay_in[h], t.slot())
                        for j in range(TB):
                            last = nc.tensor.transpose(psP[:, j * P:(j + 1) * P], pay[:, h, j, :], ident[:])
                        last.then_inc(n_("pay_turned"), 1)
                        pe.wait_ge(n_("payT"), t.n())
                        pe.wait_ge(got_in[h], t.slot(32 * TB))
                        for j in range(TB):
                            nc.tensor.matmul(psX[:, j * P:(j + 1) * P], got[:, h, j, :], ident[:], start=True, stop=False)
                            last = nc.tensor.matmul(psX[:, j * P:(j + 1) * P], w_edge[:], payT[0:6, j * P:(j + 1) * P],
                                                    start=False, stop=True)
                        last.then_inc(n_("x_summed"), 1)
                        pe.wait_ge(n_("xT"), t.n())
                        for j in range(TB):
                            nc.tensor.matmul(psS[:, j * P:(j + 1) * P], gots[:, h, j, :], ident[:], start=True, stop=False)
                            last = nc.tensor.matmul(psS[:, j * P:(j + 1) * P], att[:], xT[:, h, j * P:(j + 1) * P],
                                                    start=False, stop=True)
                        last.then_inc(n_("scored"), 1)
                        pe.wait_ge(n_("p"), t.n())
                        nc.tensor.matmul(psB[:], sel[:], p[:], start=True, stop=True).then_inc(n_("p_spread"), 1)
                        pe.wait_ge(n_("r"), t.n())
                        nc.tensor.matmul(psR[:], sel[:], r[:], start=True, stop=True).then_inc(n_("r_spread"), 1)
                        pe.wait_ge(n_("scan_done"), t.n() + 2)
                        for j in range(TB):
                            nc.tensor.transpose(psN[:, j, :], num[:, h, j * P:(j + 1) * P], ident[:])
                            last = nc.tensor.transpose(psD[:, j, 0:2], den[:, h, j * P:(j + 1) * P], ident[0:2, 0:2])
                        last.then_inc(n_("back"), 1)

            @block.scalar
            def _(act):
                S = nc.scalar
                S.preload_act_table(ACT.Exp)
                with act.Fori(0, STEPS // 2) as i:
                    for h in range(2):
                        t = Turn(0, i, h)
                        act.wait_ge(n_("pay_turned"), t.n())
                        S.copy(payT[:], psP[:]).then_inc(n_("payT"), 1)
                        act.wait_ge(n_("x_summed"), t.n())
                        S.copy(xT[:, h, :], psX[:]).then_inc(n_("xT"), 1)
                        act.wait_ge(n_("scored"), t.n() + 2)
                        S.copy(score[:], psS[:]).then_inc(n_("score"), 1)
                        act.wait_ge(n_("diff"), t.n())
                        S.activation(p[:], diff[:], ACT.Exp).then_inc(n_("p"), 1)
                        act.wait_ge(n_("down"), t.n())
                        S.activation(r0[:], down[:], ACT.Exp).then_inc(n_("r0"), 1)
                        act.wait_ge(n_("back"), t.n())
                        act.wait_ge(stored[h], t.slot())
                        S.copy(out[:, h, :, 0:2 * D], psN[:]).then_inc(n_("out"), 1)
                        S.copy(out[:, h, :, 2 * D:S0W], psD[:, :, 0:2]).then_inc(n_("out"), 1)
                        act.wait_ge(n_("out"), t.n(2))
                        act.dma_start(K["att_scan"][0:ROWS, :].rearrange("(t p) c -> p t c", p=P)[:, bass.ds((i * 2 + h) * TB, TB), :],
                                      out[:, h]).then_inc(stored[h], 16)
                for h in range(2):
                    act.wait_ge(stored[h], 16 + 16 * (STEPS // 2))

            @block.vector
            def _(dve):
                V = nc.vector
                first = Link(dve, sems("ate_first"))
                first(V.memset(top[:], 0.0))
                first(V.memset(num[:], 0.0))
                first(V.memset(den[:], 0.0))
                passed(dve, sems)
                with dve.Fori(0, STEPS // 2) as i:
                    link = Link(dve, sems("ate_link"), i * LINKS, LINKS)
                    for h in range(2):
                        t = Turn(0, i, h)
                        dve.wait_ge(n_("score"), t.n())
                        dve.wait_ge(mask_in[h], t.slot(32))
                        link(V.scalar_tensor_tensor(lrel[:], score[:], 0.2, score[:], ALU.mult, ALU.max))
                        link(V.tensor_copy(top[:, h, 0:1], top[:, 1 - h, EB:EB + 1]))
                        link(V.tensor_tensor_scan(top[:, h, 1:EB + 1], mask[:, h, 1, :], lrel[:], top[:, h, 0:1], ALU.add, ALU.max))
                        V.tensor_tensor(diff[:], lrel[:], top[:, h, 1:EB + 1], ALU.subtract).then_inc(n_("diff"), 1)
                        link(V.tensor_tensor(down[:], top[:, h, 0:EB], top[:, h, 1:EB + 1], ALU.subtract))
                        link(V.tensor_scalar(down[:], down[:], 0.0, None, ALU.min))
                        V.sem_inc(n_("down"), 1)
                        dve.wait_ge(n_("r0"), t.n())
                        link(V.tensor_tensor(r[:], r0[:], mask[:, h, 0, :], ALU.mult))
                        V.sem_inc(n_("r"), 1)
                        dve.wait_ge(n_("p"), t.n())
                        link(V.tensor_tensor_scan(den[:, h, :], r[:], p[:], den[:, 1 - h, EB - 1:EB], ALU.mult, ALU.add))
                        dve.wait_ge(n_("p_spread"), t.n())
                        link(V.tensor_tensor(px[:], psB[:], xT[:, h, :], ALU.mult))
                        dve.wait_ge(n_("r_spread"), t.n())
                        link(V.tensor_tensor_scan(num[:, h, :], psR[:], px[:], num[:, 1 - h, EB - 1:EB], ALU.mult, ALU.add))
                        V.sem_inc(n_("scan_done"), 1)
                    link.end()


class Turned:

    def __init__(self, nc, sb, pb, sems, name, width=D):
        self.nc, self.width = nc, width
        self.hT = sb(name + "_hT", [P, 2, PAIRS * P])
        self.psT = pb(name + "_psT", [P, 2, 512])
        self.psR = pb(name + "_psR", [P, 2, max(512, TB * width)])
        self.ready, self.turned, self.copied, self.multiplied = (
            sems(name + "_" + n) for n in ("ready", "turned", "copied", "multiplied"))

    def product(self, h):
        return self.psR[:, h, 0:TB * self.width].rearrange("p (n c) -> p n c", n=TB)

    def tensor(self, pe, t, h_, ident, w):
        nc, h = self.nc, t.h
        pe.wait_ge(self.ready, t.n())
        for k in range(PAIRS):
            last = nc.tensor.transpose(self.psT[:, h, k * P:(k + 1) * P], h_[:, h, k, :], ident[:])
        last.then_inc(self.turned, 1)
        if w is not None:
            pe.wait_ge(self.copied, t.n())
            for k in range(PAIRS):
                last = nc.tensor.matmul(self.psR[:, h, k * 2 * self.width:(k + 1) * 2 * self.width],
                                        self.hT[:, h, k * P:(k + 1) * P], w[:], start=True, stop=True)
            last.then_inc(self.multiplied, 1)

    def scalar(self, act, t):
        act.wait_ge(self.turned, t.n())
        self.nc.scalar.copy(self.hT[:, t.h], self.psT[:, t.h, 0:PAIRS * P]).then_inc(self.copied, 1)


def index_loads(nc, sp, K, sems, name, t, index, ends, s):
    if not t.first:
        sp.wait_ge(sems.pair(name + "_got")[t.h], t.slot(16 * TB) - 16 * TB)
    sp.dma_start(index[:, t.h], K[ends][:, bass.ds(s * PAIRS, PAIRS), :]).then_inc(sems.pair(name + "_index_in")[t.h], 16)


def gathers(nc, pool, sems, name, t, got, table, index):
    pool.wait_ge(sems.pair(name + "_index_in")[t.h], t.slot())
    pool.wait_ge(sems(name + "_got_used"), t.n())
    passed(pool, sems)
    for n in range(TB):
        gather(pool, got[:, t.h, n, :], table, index[:, n]).then_inc(sems.pair(name + "_got")[t.h], 16)


def store_rows(act, table, rows, q, sem):
    for g in range(2):
        act.dma_start(node_rows(table, g, q), rows.rearrange("p (k g) c -> p k g c", g=2)[:, :, g, :]).then_inc(sem, 16)


def attention_nodes(nc, K, sems):
    io = K["io"]
    with ExitStack() as ctx:
        sb = lambda n, s, dt=F32: ctx.enter_context(nc.sbuf_tensor("atn_" + n, s, dt))
        pb = lambda n, s: ctx.enter_context(nc.psum_tensor("atn_" + n, s, F32))
        index, got = sb("index", [P, 2, TB], I32), sb("got", [P, 2, TB, S0W])
        x, x1, h_ = sb("x", [P, 2, PAIRS, 2, D]), sb("x1", [P, 2, TB, D]), sb("h", [P, 2, PAIRS, 2 * D])
        half_has, dens = sb("half_has", [P, HALF, 2]), sb("dens", [P, TB, 2])
        heads, both = sb("heads", [P, TB, 2, D]), sb("both", [P, TB, D])
        w, bias = sb("w", [P, 2 * D]), sb("bias", [P, D])
        rows = sb("msg_rows", [P, 2, TB, D])
        norm = Norm(sb, sems, "atn_norm")
        turn = Turned(nc, sb, pb, sems, "atn")
        loaded, x_in, got_in = sems("atn_in"), sems.pair("atn_x_in"), sems.pair("atn_got")
        stored, rows_ready, used = sems.pair("atn_stored"), sems("atn_rows_ready"), sems("atn_got_used")
        LINKS = 2 * (Norm.LINKS + 8)
        with nc.Block() as block:
            @block.sync
            def _(sp):
                sp.dma_start(w[:], io["w_top"][0]).then_inc(loaded, 16)
                sp.dma_start(bias[:], io["att_bias"]).then_inc(loaded, 16)

                def loads(t, link):
                    index_loads(nc, sp, K, sems, "atn", t, index[:].rearrange("p h (k g) -> p h k g", g=2), "end_src", t.s)
                    sp.wait_ge(used, t.n())
                    for g in range(2):
                        sp.dma_start(x[:, t.h, :, g, :], node_rows(io["x"], g, t.s * PAIRS)).then_inc(x_in[t.h], 16)
                pipeline(sp, None, [(0, loads, 0)], peel=2)

            @block.gpsimd
            def _(pool):
                with pool.Fori(0, STEPS // 2) as i:
                    for h in range(2):
                        gathers(nc, pool, sems, "atn", Turn(0, i, h), got, K["att_scan"],
                                index[:, h].rearrange("p (n o) -> p n o", o=1))

            @block.vector
            def _(dve):
                V = nc.vector
                dve.wait_ge(loaded, 32)
                first = Link(dve, sems("atn_first"))
                first(V.memset(norm.eps[:], EPS))
                first(V.tensor_scalar(half_has[:], K["has_s"][:], 0.5, None, ALU.mult))
                passed(dve, sems)
                with dve.Fori(0, STEPS // 2) as i:
                    link = Link(dve, sems("atn_link"), i * LINKS, LINKS)
                    for h in range(2):
                        t = Turn(0, i, h)
                        own = half_has[:, bass.ds(i * (2 * PAIRS) + h * PAIRS, PAIRS), :].rearrange("p k g -> p (k g)")
                        dve.wait_ge(got_in[h], t.slot(16 * TB))
                        dve.wait_ge(x_in[h], t.slot(32))
                        dve.wait_ge(stored[h], t.slot(80))
                        link(V.tensor_scalar(dens[:], got[:, h, :, 2 * D:S0W], 1e-16, None, ALU.add))
                        link(V.reciprocal(dens[:], dens[:]))
                        link(V.tensor_tensor(dens[:], dens[:], own.unsqueeze(2).broadcast_to([P, TB, 2]), ALU.mult))
                        link(V.tensor_tensor(heads[:], got[:, h, :, 0:2 * D].rearrange("p n (a d) -> p n a d", a=2),
                                             dens[:].unsqueeze(3).broadcast_to([P, TB, 2, D]), ALU.mult))
                        link(V.tensor_tensor(both[:], heads[:, :, 0, :], heads[:, :, 1, :], ALU.add))
                        link(V.tensor_tensor(both[:], both[:], per_feature(bias[:]), ALU.add))
                        link(V.tensor_tensor(x1[:, h], both[:], x[:, h].rearrange("p k g d -> p (k g) d"), ALU.add))
                        V.sem_inc(used, 1)
                        norm.vector(nc, dve, link, x1[:, h], h_[:, h].rearrange("p k (g d) -> p (k g) d", g=2), t.n())
                        V.sem_inc(turn.ready, 1)
                        dve.wait_ge(turn.multiplied, t.n())
                        link(V.tensor_copy(rows[:, h], turn.product(h)))
                        V.sem_inc(rows_ready, 1)
                    link.end()

            @block.scalar
            def _(act):
                nc.scalar.preload_act_table(ACT.Sqrt)
                with act.Fori(0, STEPS // 2) as i:
                    for h in range(2):
                        t = Turn(0, i, h)
                        norm.scalar(nc, act, t.n())
                        turn.scalar(act, t)
                        act.wait_ge(turn.copied, t.n())
                        act.dma_start(K["hT"][:, bass.ds((i * 2 + h) * (PAIRS * P), PAIRS * P)], turn.hT[:, h]).then_inc(stored[h], 16)
                        act.wait_ge(rows_ready, t.n())
                        store_rows(act, K["x1"], x1[:, h], i * (2 * PAIRS) + h * PAIRS, stored[h])
                        store_rows(act, K["msg_table"], rows[:, h], i * (2 * PAIRS) + h * PAIRS, stored[h])
                for h in range(2):
                    act.wait_ge(stored[h], 80 + 80 * (STEPS // 2))

            @block.tensor
            def _(pe):
                pe.wait_ge(loaded, 32)
                with pe.Fori(0, STEPS // 2) as i:
                    for h in range(2):
                        turn.tensor(pe, Turn(0, i, h), h_, K["ident"], w)


def pna_edges(nc, K, sems, rep):
    with ExitStack() as ctx:
        sb = lambda n, s, dt=F32: ctx.enter_context(nc.sbuf_tensor("pne_" + n, s, dt))
        pb = lambda n, s: ctx.enter_context(nc.psum_tensor("pne_" + n, s, F32))
        index, mask = sb("index", [P, 2, TB], I32), sb("mask", [P, 2, 2, EB], BF16)
        z = sb("z", [P, 2, TB, 3 * D])
        sums, tops = sb("sums", [P, 2, EB]), sb("tops", [P, 2, EB])
        out = sb("out", [P, 2, TB, 4 * D])
        psS, psM = pb("psS", [P, 2, EB]), pb("psM", [P, 2, EB])
        psB = pb("psB", [P, 2, TB, 2 * D])
        n_ = lambda name: sems("pne_" + name)
        index_in, mask_in, got_in, stored = (sems.pair("pne_" + n) for n in ("index_in", "mask_in", "got", "stored"))
        ident = K["ident"]
        with nc.Block() as block:
            @block.sync
            def _(sp):
                def loads(t, link):
                    if not t.first:
                        sp.wait_ge(got_in[t.h], t.slot(16 * TB) - 16 * TB)
                    sp.dma_start(index[:, t.h, :], K["dst_src"][:, bass.ds(t.s * TB, TB)]).then_inc(index_in[t.h], 16)
                    sp.wait_ge(n_("scanned"), t.n())
                    sp.dma_start(mask[:, t.h].rearrange("p a f -> p (a f)"),
                                 K["mask_dst"][bass.ds(t.s, 1), :].broadcast_to([P, 2 * EB])).then_inc(mask_in[t.h], 16)
                pipeline(sp, None, [(0, loads, 0)], rep, peel=2)

            @block.gpsimd
            def _(pool):
                def gathers_a(t, link):
                    pool.wait_ge(index_in[t.h], t.slot())
                    pool.wait_ge(n_("turned"), t.n())
                    passed(pool, sems)
                    for j in range(TB):
                        gather(pool, z[:, t.h, j, D:2 * D], K["msg_table"], index[:, t.h, j:j + 1]).then_inc(got_in[t.h], 16)
                pipeline(pool, None, [(0, gathers_a, 0)], rep)

            @block.tensor
            def _(pe):
                def turn(t, link):
                    pe.wait_ge(n_("squared"), t.n())
                    pe.wait_ge(n_("negated"), t.n())
                    pe.wait_ge(n_("scanned"), t.n())
                    for j in range(TB):
                        nc.tensor.transpose(psS[:, t.h, j * P:(j + 1) * P], z[:, t.h, j, 0:2 * D], ident[:])
                        last = nc.tensor.transpose(psM[:, t.h, j * P:(j + 1) * P], z[:, t.h, j, D:3 * D], ident[:])
                    last.then_inc(n_("turned"), 1)

                def turn_back(t, link):
                    pe.wait_ge(n_("scanned"), t.n() + 2)
                    for b, scans in enumerate((sums, tops)):
                        pe.wait_ge(n_("copied"), t.n(2) + (b - 1))
                        for j in range(TB):
                            last = nc.tensor.transpose(psB[:, b, j, :], scans[:, t.h, j * P:(j + 1) * P], ident[:])
                        last.then_inc(n_("back"), 1)
                pipeline(pe, None, [(0, turn, 0), (1, turn_back, 0)], rep)

            @block.scalar
            def _(act):
                S = nc.scalar
                S.preload_act_table(ACT.Square)

                def square(t, link):
                    act.wait_ge(got_in[t.h], t.slot(16 * TB))
                    S.activation(z[:, t.h, :, 0:D], z[:, t.h, :, D:2 * D], ACT.Square).then_inc(n_("squared"), 1)

                def store(t, link):
                    act.wait_ge(stored[t.h], t.slot())
                    for b in range(2):
                        act.wait_ge(n_("back"), t.n(2) + (b - 1))
                        S.copy(out[:, t.h, :, b * 2 * D:(b + 1) * 2 * D], psB[:, b]).then_inc(n_("copied"), 1)
                    act.wait_ge(n_("copied"), t.n(2) + 2)
                    act.dma_start(K["pna_scan"][0:ROWS, :].rearrange("(t p) c -> p t c", p=P)[:, bass.ds(t.s * TB, TB), :],
                                  out[:, t.h]).then_inc(stored[t.h], 16)
                pipeline(act, None, [(0, square, 0), (1, store, 0)], rep)

            @block.vector
            def _(dve):
                V = nc.vector
                first = Link(dve, sems("pne_first"), rep * 2)
                first(V.memset(sums[:], 0.0))
                first(V.memset(tops[:], 0.0))
                passed(dve, sems)

                def negate(t, link):
                    dve.wait_ge(got_in[t.h], t.slot(16 * TB))
                    V.tensor_scalar(z[:, t.h, :, 2 * D:3 * D], z[:, t.h, :, D:2 * D], -1.0, None, ALU.mult).then_inc(n_("negated"), 1)

                def scan(t, link):
                    dve.wait_ge(n_("turned"), t.n() + 2)
                    dve.wait_ge(mask_in[t.h], t.slot())
                    V.tensor_tensor_scan(sums[:, t.h, :], mask[:, t.h, 0, :], psS[:, t.h, :], sums[:, 1 - t.h, EB - 1:EB],
                                         ALU.mult, ALU.add)
                    link(V.tensor_tensor_scan(tops[:, t.h, :], mask[:, t.h, 1, :], psM[:, t.h, :], tops[:, 1 - t.h, EB - 1:EB],
                                              ALU.add, ALU.max))
                    V.sem_inc(n_("scanned"), 1)
                pipeline(dve, sems("pne_link"), [(0, negate, 0), (1, scan, 1)], rep)
        stores_done(nc, sems, [(stored, 16)], rep)


def stores_done(nc, sems, which, rep):
    with nc.Block() as block:
        @block.sync
        def _(sp):
            for pair, k in which:
                for s in pair:
                    sp.wait_ge(s, rep * (STEPS // 2 * k) + (STEPS // 2 + 1) * k)
            passed(sp, sems)


def pna_nodes(nc, K, sems, rep):
    io = K["io"]
    W = 3 * D
    with ExitStack() as ctx:
        sb = lambda n, s, dt=F32: ctx.enter_context(nc.sbuf_tensor("pnn_" + n, s, dt))
        pb = lambda n, s: ctx.enter_context(nc.psum_tensor("pnn_" + n, s, F32))
        index, got = sb("index", [P, 2, TB], I32), sb("got", [P, 2, TB, 4 * D])
        hT, hT2 = sb("hT", [P, 2, PAIRS * P]), sb("hT2", [P, 2, PAIRS * P])
        w_bot, w_own, w_agg = sb("w_bot", [P, 2 * D]), sb("w_own", [P, 2 * D]), sb("w_agg", [P, 3, W])
        bM, bU, tiny = sb("bM", [P, D]), sb("bU", [P, 1]), sb("tiny", [P, 1])
        mq, m2 = sb("mq", [P, TB, 2 * D]), sb("m2", [P, TB, D])
        base = sb("base", [P, TB, D])
        agg = sb("agg", [P, 2, TB, 6 * D])
        aggT = sb("aggT", [P, 2, 3, TB * P])
        u0, u1, u2 = sb("u0", [P, TB, D]), sb("u1", [P, TB, D]), sb("u2", [P, 2, PAIRS, 2 * D])
        psO, psT = pb("psO", [P, 2, 512]), pb("psT", [P, 3, 512])
        psH, psU = pb("psH", [P, TB, 256]), pb("psU", [P, 512])
        n_ = lambda name: sems("pnn_" + name)
        loaded, got_in, hT_in, hT2_in = n_("in"), sems.pair("pnn_got"), sems.pair("pnn_hT_in"), sems.pair("pnn_hT2_in")
        ident, U = K["ident"], K["U"]
        agg_of = lambda t, a: agg[:, t.h, :, a * D:(a + 1) * D]
        with nc.Block() as block:
            @block.sync
            def _(sp):
                lay = lambda a: a[bass.ds(rep, 1)].rearrange("o p c -> p (o c)")
                sp.dma_start(w_bot[:], lay(io["w_bot"])).then_inc(loaded, 16)
                sp.dma_start(w_own[:], lay(io["w_own"])).then_inc(loaded, 16)
                sp.dma_start(w_agg[:].rearrange("p c w -> p (c w)"), lay(io["w_agg"])).then_inc(loaded, 16)
                sp.dma_start(bM[:], lay(io["bM"])).then_inc(loaded, 16)
                sp.dma_start(bU[:], lay(io["bU"])).then_inc(loaded, 16)

                def loads(t, link):
                    index_loads(nc, sp, K, sems, "pnn", t, index[:].rearrange("p h (k g) -> p h k g", g=2), "end_dst", t.s)
                    sp.wait_ge(n_("own"), t.n())
                    sp.dma_start(hT[:, t.h], K["hT"][:, bass.ds(t.s * (PAIRS * P), PAIRS * P)]).then_inc(hT_in[t.h], 16)

                def load_again(t, link):
                    sp.wait_ge(n_("multiplied"), t.n())
                    sp.dma_start(hT2[:, t.h], K["hT"][:, bass.ds(t.s * (PAIRS * P), PAIRS * P)]).then_inc(hT2_in[t.h], 16)
                pipeline(sp, None, [(0, loads, 0), (2, load_again, 0)], rep)

            @block.gpsimd
            def _(pool):
                def gather_scans(t, link):
                    gathers(nc, pool, sems, "pnn", t, got, K["pna_scan"], index[:, t.h].rearrange("p (n o) -> p n o", o=1))
                pipeline(pool, None, [(0, gather_scans, 0)], rep)

            @block.vector
            def _(dve):
                V = nc.vector
                dve.wait_ge(loaded, rep * 80 + 80)
                first = Link(dve, n_("first"), rep * 2)
                first(V.memset(tiny[:], 1e-30))
                first(V.tensor_scalar(bU[:], bU[:], NSCALE, None, ALU.mult))
                V.sem_inc(n_("scaled"), 1)
                passed(dve, sems)

                def own(t, name, w=D):
                    return K[name][:, bass.ds(t.s * PAIRS, PAIRS), :].rearrange("p k g -> p (k g)").unsqueeze(2).broadcast_to([P, TB, w])

                def aggregate(t, link):
                    dve.wait_ge(got_in[t.h], t.slot(16 * TB))
                    dve.wait_ge(n_("agg_turned"), t.n(3))
                    link(V.tensor_tensor(mq[:], got[:, t.h, :, 0:2 * D], own(t, "inv", 2 * D), ALU.mult))
                    link(V.tensor_tensor(m2[:], mq[:, :, D:2 * D], mq[:, :, D:2 * D], ALU.mult))
                    link(V.tensor_tensor(m2[:], mq[:, :, 0:D], m2[:], ALU.subtract))
                    V.tensor_scalar(agg_of(t, 4), m2[:], 0.0, None, ALU.max).then_inc(n_("var"), 1)
                    dve.wait_ge(n_("own"), t.n() + 2)
                    link(V.tensor_tensor(base[:], psO[:, t.h, 0:TB * D].rearrange("p (n d) -> p n d", d=D), per_feature(bM[:]), ALU.add))
                    V.sem_inc(n_("own_used"), 1)
                    link(V.tensor_tensor(base[:], base[:], own(t, "has"), ALU.mult))
                    link(V.tensor_tensor(agg_of(t, 0), mq[:, :, D:2 * D], base[:], ALU.add))
                    V.tensor_tensor(agg_of(t, 1), got[:, t.h, :, 2 * D:3 * D], base[:], ALU.add)
                    V.tensor_tensor(agg_of(t, 2), base[:], got[:, t.h, :, 3 * D:4 * D], ALU.subtract)
                    link(V.tensor_tensor(agg_of(t, 5), agg_of(t, 0), own(t, "deg"), ALU.mult))
                    V.sem_inc(n_("agg"), 1)
                    V.sem_inc(n_("got_used"), 1)

                def combine(t, link):
                    dve.wait_ge(n_("multiplied"), t.n() + 2)
                    dve.wait_ge(n_("u_turned"), t.n())
                    link(V.tensor_tensor(u1[:], psH[:, :, D:2 * D], own(t, "amp"), ALU.mult))
                    link(V.scalar_tensor_tensor(u0[:], psH[:, :, 0:D], NSCALE, u1[:], ALU.mult, ALU.add))
                    link(V.tensor_tensor(u1[:], psH[:, :, 2 * D:3 * D], own(t, "att"), ALU.mult))
                    V.sem_inc(n_("product_used"), 1)
                    link(V.tensor_tensor(u2[:, t.h].rearrange("p k (g d) -> p (k g) d", g=2), u0[:], u1[:], ALU.add))
                    V.sem_inc(n_("u"), 1)
                pipeline(dve, n_("link"), [(3, combine, 4), (0, aggregate, 7)], rep)

            @block.scalar
            def _(act):
                nc.scalar.preload_act_table(ACT.Sqrt)
                act.wait_ge(n_("scaled"), rep + 1)
                passed(act, sems)

                def root(t, link):
                    act.wait_ge(n_("var"), t.n())
                    nc.scalar.activation(agg_of(t, 3), agg_of(t, 4), ACT.Sqrt, bias=tiny[:]).then_inc(n_("std"), 1)

                def copy_agg(t, link):
                    act.wait_ge(n_("multiplied"), t.n())
                    for c in range(3):
                        act.wait_ge(n_("agg_turned"), t.n(3) + (c + 4))
                        nc.scalar.copy(aggT[:, t.h, c, :], psT[:, c, :]).then_inc(n_("aggT"), 1)

                def keep_u(t, link):
                    act.wait_ge(n_("u_turned"), t.n() + 2)
                    passed(act, sems)
                    nc.scalar.activation(U[:, bass.ds(t.s * (PAIRS * P), PAIRS * P)], psU[:, 0:PAIRS * P],
                                         ACT.Identity, bias=bU[:]).then_inc(n_("u_kept"), 1)
                pipeline(act, None, [(0, root, 0), (1, copy_agg, 0), (4, keep_u, 0)], rep)

            @block.tensor
            def _(pe):
                pe.wait_ge(loaded, rep * 80 + 80)
                passed(pe, sems)

                def multiply_own(t, link):
                    pe.wait_ge(hT_in[t.h], t.slot())
                    pe.wait_ge(n_("own_used"), t.n())
                    for k in range(PAIRS):
                        last = nc.tensor.matmul(psO[:, t.h, k * 2 * D:(k + 1) * 2 * D], hT[:, t.h, k * P:(k + 1) * P], w_bot[:],
                                                start=True, stop=True)
                    last.then_inc(n_("own"), 1)

                def turn_agg(t, link):
                    pe.wait_ge(n_("agg"), t.n())
                    pe.wait_ge(n_("std"), t.n())
                    for c in range(3):
                        pe.wait_ge(n_("aggT"), t.n(3) + (c - 2))
                        for n in range(TB):
                            last = nc.tensor.transpose(psT[:, c, n * P:(n + 1) * P], agg[:, t.h, n, c * P:(c + 1) * P], ident[:])
                        last.then_inc(n_("agg_turned"), 1)

                def multiply(t, link):
                    pe.wait_ge(n_("aggT"), t.n(3) + 3)
                    pe.wait_ge(hT2_in[t.h], t.slot())
                    pe.wait_ge(n_("product_used"), t.n())
                    for n in range(TB):
                        k, g = n // 2, n % 2
                        for c in range(3):
                            last = nc.tensor.matmul(psH[:, n, 0:W], aggT[:, t.h, c, n * P:(n + 1) * P], w_agg[:, c, :],
                                                    start=(c == 0), stop=(c == 2))
                            if c == 0:
                                nc.tensor.matmul(psH[:, n, 0:D], hT2[:, t.h, k * P:(k + 1) * P], w_own[:, g * D:(g + 1) * D],
                                                 start=False, stop=False)
                    last.then_inc(n_("multiplied"), 1)

                def turn_u(t, link):
                    pe.wait_ge(n_("u"), t.n())
                    pe.wait_ge(n_("u_kept"), t.n())
                    for k in range(PAIRS):
                        last = nc.tensor.transpose(psU[:, k * P:(k + 1) * P], u2[:, t.h, k, :], ident[:])
                    last.then_inc(n_("u_turned"), 1)
                pipeline(pe, None, [(0, multiply_own, 0), (1, turn_agg, 0), (2, multiply, 0), (4, turn_u, 0)], rep)


def feature_stats(nc, K, sems, rep, name, sb, pb, gamma, beta):
    U = K["U"]
    stats, rest = sb("stats", [P, STATN, 6]), sb("rest", [P, 6])
    mv, mvr = sb("mv", [P, 2]), sb("mvr", [P, 2])
    raw, rawr = sb("raw", [P, 2]), sb("rawr", [P, 2])
    mean, var, sd = sb("mean", [P, 2]), sb("var", [P, 1]), sb("sd", [P, 1])
    scale, shift, eps = sb("scale", [P, 1]), sb("shift", [P, 1]), sb("eps", [P, 1])
    psF = pb("psF", [P, 512])
    loaded, summed, folded, asked, rooted = (sems(name + "_" + n) for n in ("in", "summed", "folded", "asked", "rooted"))
    with nc.Block() as block:
        @block.vector
        def _(dve):
            V = nc.vector
            dve.wait_ge(loaded, rep * 32 + 32)
            passed(dve, sems)
            counted = sems(name + "_counted")
            with dve.Fori(0, STATN) as i:
                V.bn_stats(stats[:, bass.ds(i, 1), :].rearrange("p o c -> p (o c)"), U[:, bass.ds(i * STATF, STATF)]).then_inc(counted, 1)
            V.bn_stats(rest[0:D, :], U[0:D, G1COLS:COLS]).then_inc(counted, 1)
            dve.wait_ge(counted, rep * (STATN + 1) + STATN + 1)
            link = Link(dve, sems(name + "_link"), rep * 21)
            link(V.memset(eps[:], EPS))
            passed(dve, sems)
            link(V.bn_aggr(mv[:], stats[:]))
            link(V.memset(mvr[:], 0.0))
            passed(dve, sems)
            link(V.bn_aggr(mvr[0:D, :], rest[0:D, :].unsqueeze(1)))
            for (m, r, n) in ((mv, raw, G1COLS), (mvr, rawr, COLS - G1COLS)):
                link(V.tensor_tensor(r[:, 1:2], m[:, 0:1], m[:, 0:1], ALU.mult))
                link(V.tensor_tensor(r[:, 1:2], r[:, 1:2], m[:, 1:2], ALU.add))
                link(V.tensor_scalar(r[:, 1:2], r[:, 1:2], float(n), None, ALU.mult))
                link(V.tensor_scalar(r[:, 0:1], m[:, 0:1], float(n), None, ALU.mult))
            link(V.tensor_tensor(raw[:], raw[:], rawr[:], ALU.add))
            V.sem_inc(summed, 1)
            dve.wait_ge(folded, rep + 1)
            link(V.tensor_scalar(mean[:], psF[:, 0:2], 1.0 / N, None, ALU.mult))
            link(V.tensor_tensor(var[:], mean[:, 0:1], mean[:, 0:1], ALU.mult))
            link(V.tensor_tensor(var[:], mean[:, 1:2], var[:], ALU.subtract))
            link(V.tensor_scalar(var[:], var[:], 0.0, None, ALU.max))
            V.sem_inc(asked, 1)
            dve.wait_ge(rooted, rep + 1)
            link(V.reciprocal(scale[:], sd[:]))
            link(V.tensor_tensor(scale[:], scale[:], gamma[:], ALU.mult))
            link(V.tensor_tensor(shift[:], mean[:, 0:1], scale[:], ALU.mult))
            link(V.tensor_tensor(shift[:], beta[:], shift[:], ALU.subtract))
            passed(dve, sems)
            assert link.n == 21, link.n

        @block.tensor
        def _(pe):
            pe.wait_ge(summed, rep + 1)
            nc.tensor.matmul(psF[:, 0:2], K["fold"][:], raw[:], start=True, stop=True).then_inc(folded, 1)

        @block.scalar
        def _(act):
            act.wait_ge(asked, rep + 1)
            nc.scalar.activation(sd[:], var[:], ACT.Sqrt, bias=eps[:]).then_inc(rooted, 1)

        @block.sync
        def _(sp):
            lay = lambda a: a[bass.ds(rep, 1)].rearrange("o p c -> p (o c)")
            g, b = ("gamma_t", "beta_t") if name == "mix" else ("gamma_o", "beta_o")
            sp.dma_start(gamma[:], lay(K["io"][g])).then_inc(loaded, 16)
            sp.dma_start(beta[:], lay(K["io"][b])).then_inc(loaded, 16)
    return scale, shift


def pna_mix(nc, K, sems, rep):
    io, U = K["io"], K["U"]
    C = PAIRS * P
    with ExitStack() as ctx:
        sb = lambda n, s, dt=F32: ctx.enter_context(nc.sbuf_tensor("mix_" + n, s, dt))
        pb = lambda n, s: ctx.enter_context(nc.psum_tensor("mix_" + n, s, F32))
        gamma, beta = sb("gamma", [P, 1]), sb("beta", [P, 1])
        scale, shift = feature_stats(nc, K, sems, rep, "mix", sb, pb, gamma, beta)
        w, ws, bias, moved = sb("w", [P, 2 * D]), sb("ws", [P, 2 * D]), sb("bias", [P, 1]), sb("moved", [P, 1])
        hT, y, z = sb("hT", [P, 2, C]), sb("y", [P, 2, C]), sb("z", [P, 2, C])
        psM, psB = pb("psM", [P, 2, 512]), pb("psB", [P, 512])
        n_ = lambda name: sems("mix_" + name)
        loaded, hT_in = n_("w_in"), sems.pair("mix_hT_in")
        LINKS = 2 * 2
        with nc.Block() as block:
            @block.sync
            def _(sp):
                lay = lambda a: a[bass.ds(rep, 1)].rearrange("o p c -> p (o c)")
                sp.dma_start(w[:], lay(io["w_mix"])).then_inc(loaded, 16)
                sp.dma_start(bias[:], lay(io["b_mix"])).then_inc(loaded, 16)
                with sp.Fori(0, STEPS // 2) as i:
                    for h in range(2):
                        t = Turn(rep, i, h)
                        sp.wait_ge(n_("mixed"), t.n())
                        sp.dma_start(hT[:, h], K["hT"][:, bass.ds((i * 2 + h) * C, C)]).then_inc(hT_in[h], 16)

            @block.tensor
            def _(pe):
                pe.wait_ge(loaded, rep * 32 + 32)
                nc.tensor.matmul(psB[:, 0:1], w[:], shift[:], start=True, stop=True).then_inc(n_("shifted"), 1)
                pe.wait_ge(n_("scaled"), rep + 1)
                passed(pe, sems)
                with pe.Fori(0, STEPS // 2) as i:
                    for h in range(2):
                        t = Turn(rep, i, h)
                        pe.wait_ge(n_("biased"), t.n())
                        nc.tensor.matmul(psM[:, h, 0:C], ws[:], U[:, bass.ds((i * 2 + h) * C, C)],
                                         start=True, stop=True).then_inc(n_("multiplied"), 1)

            @block.scalar
            def _(act):
                act.wait_ge(n_("scaled"), rep + 1)
                passed(act, sems)
                nc.scalar.preload_act_table(ACT.Identity)
                with act.Fori(0, STEPS // 2) as i:
                    for h in range(2):
                        t = Turn(rep, i, h)
                        act.wait_ge(n_("multiplied"), t.n())
                        act.wait_ge(n_("mixed"), t.n())
                        nc.scalar.activation(y[:, h], psM[:, h, 0:C], ACT.Identity, bias=moved[:]).then_inc(n_("biased"), 1)

            @block.vector
            def _(dve):
                V = nc.vector
                first = Link(dve, n_("first"), rep * 2)
                dve.wait_ge(loaded, rep * 32 + 32)
                first(V.tensor_scalar(ws[:], w[:], scale[:], None, ALU.mult))
                dve.wait_ge(n_("shifted"), rep + 1)
                first(V.tensor_tensor(moved[:], psB[:, 0:1], bias[:], ALU.add))
                V.sem_inc(n_("scaled"), 1)
                passed(dve, sems)
                with dve.Fori(0, STEPS // 2) as i:
                    link = Link(dve, n_("dve_link"), (rep * (STEPS // 2) + i) * LINKS, LINKS)
                    for h in range(2):
                        t = Turn(rep, i, h)
                        dve.wait_ge(n_("biased"), t.n() + 2)
                        dve.wait_ge(hT_in[h], t.slot())
                        link(V.scalar_tensor_tensor(z[:, h], y[:, h], 0.01, y[:, h], ALU.mult, ALU.max))
                        link(V.tensor_tensor(U[:, bass.ds((i * 2 + h) * C, C)], z[:, h], hT[:, h], ALU.add))
                        V.sem_inc(n_("mixed"), 1)
                    link.end()


def pna_out(nc, K, sems, rep):
    io, U = K["io"], K["U"]
    C = PAIRS * P
    with ExitStack() as ctx:
        sb = lambda n, s, dt=F32: ctx.enter_context(nc.sbuf_tensor("pno_" + n, s, dt))
        pb = lambda n, s: ctx.enter_context(nc.psum_tensor("pno_" + n, s, F32))
        gamma, beta = sb("gamma", [P, 1]), sb("beta", [P, 1])
        scale, shift = feature_stats(nc, K, sems, rep, "pno", sb, pb, gamma, beta)
        w = sb("w", [P, 2 * D])
        hT, y, hn = sb("hT", [P, 2, C]), sb("y", [P, 2, C]), sb("hn", [P, 2, C])
        rows = sb("msg_rows", [P, 2, TB, D])
        psR = pb("psR", [P, 2, 512])
        n_ = lambda name: sems("pno_" + name)
        loaded, hT_in, stored = n_("w_in"), sems.pair("pno_hT_in"), sems.pair("pno_stored")
        LINKS = 2 * 2
        with nc.Block() as block:
            @block.sync
            def _(sp):
                sp.dma_start(w[:], io["w_top"][bass.ds(rep + 1, 1)].rearrange("o p c -> p (o c)")).then_inc(loaded, 16)
                with sp.Fori(0, STEPS // 2) as i:
                    for h in range(2):
                        t = Turn(rep, i, h)
                        sp.wait_ge(n_("made"), t.n())
                        sp.dma_start(hT[:, h], K["hT"][:, bass.ds((i * 2 + h) * C, C)]).then_inc(hT_in[h], 16)

            @block.vector
            def _(dve):
                V = nc.vector
                with dve.Fori(0, STEPS // 2) as i:
                    link = Link(dve, n_("dve_link"), (rep * (STEPS // 2) + i) * LINKS, LINKS)
                    for h in range(2):
                        t = Turn(rep, i, h)
                        link(V.tensor_scalar(y[:, h], U[:, bass.ds((i * 2 + h) * C, C)], scale[:], shift[:], ALU.mult, ALU.add))
                        dve.wait_ge(hT_in[h], t.slot())
                        dve.wait_ge(stored[h], t.slot(48))
                        link(V.scalar_tensor_tensor(hn[:, h], y[:, h], 0.0, hT[:, h], ALU.max, ALU.add))
                        V.sem_inc(n_("made"), 1)
                    link.end()

            @block.tensor
            def _(pe):
                pe.wait_ge(loaded, rep * 16 + 16)
                passed(pe, sems)
                with pe.Fori(0, STEPS // 2) as i:
                    for h in range(2):
                        t = Turn(rep, i, h)
                        pe.wait_ge(n_("made"), t.n() + 2)
                        pe.wait_ge(n_("rows"), t.n())
                        for k in range(PAIRS):
                            last = nc.tensor.matmul(psR[:, h, k * 2 * D:(k + 1) * 2 * D], hn[:, h, k * P:(k + 1) * P], w[:],
                                                    start=True, stop=True)
                        last.then_inc(n_("multiplied"), 1)

            @block.scalar
            def _(act):
                nc.scalar.preload_act_table(ACT.Square)
                with act.Fori(0, STEPS // 2) as i:
                    for h in range(2):
                        t = Turn(rep, i, h)
                        act.wait_ge(n_("made"), t.n() + 2)
                        act.dma_start(K["hT"][:, bass.ds((i * 2 + h) * C, C)], hn[:, h]).then_inc(stored[h], 16)
                        act.wait_ge(n_("multiplied"), t.n())
                        nc.scalar.copy(rows[:, h], psR[:, h, 0:TB * D].rearrange("p (n d) -> p n d", d=D)).then_inc(n_("rows"), 1)
                        act.wait_ge(n_("rows"), t.n() + 2)
                        store_rows(act, K["msg_table"], rows[:, h], i * (2 * PAIRS) + h * PAIRS, stored[h])
        stores_done(nc, sems, [(stored, 48)], rep)


def pna_end(nc, K, sems):
    C = PAIRS * P
    with ExitStack() as ctx:
        sb = lambda n, s, dt=F32: ctx.enter_context(nc.sbuf_tensor("end_" + n, s, dt))
        pb = lambda n, s: ctx.enter_context(nc.psum_tensor("end_" + n, s, F32))
        hT, x1, x2 = sb("hT", [P, 2, C]), sb("x1", [P, 2, PAIRS, 2, D]), sb("x2", [P, 2, TB, D])
        hn, rows = sb("hn", [P, TB, D]), sb("rows", [P, 2, TB, D])
        psT = pb("psT", [P, 2, 512])
        norm = Norm(sb, sems, "end_norm")
        n_ = lambda name: sems("end_" + name)
        x_in, stored = sems.pair("end_x_in"), sems.pair("end_stored")
        LINKS = 2 * (Norm.LINKS + 2)
        with nc.Block() as block:
            @block.sync
            def _(sp):
                with sp.Fori(0, STEPS // 2) as i:
                    for h in range(2):
                        t = Turn(0, i, h)
                        s = i * 2 + h
                        sp.wait_ge(n_("summed"), t.n())
                        sp.dma_start(hT[:, h], K["hT"][:, bass.ds(s * C, C)]).then_inc(x_in[h], 16)
                        for g in range(2):
                            sp.dma_start(x1[:, h, :, g, :], node_rows(K["x1"], g, s * PAIRS)).then_inc(x_in[h], 16)

            @block.tensor
            def _(pe):
                with pe.Fori(0, STEPS // 2) as i:
                    for h in range(2):
                        t = Turn(0, i, h)
                        pe.wait_ge(x_in[h], t.slot(48))
                        for k in range(PAIRS):
                            last = nc.tensor.transpose(psT[:, h, k * P:(k + 1) * P], hT[:, h, k * P:(k + 1) * P], K["ident"][:])
                        last.then_inc(n_("turned"), 1)

            @block.vector
            def _(dve):
                V = nc.vector
                first = Link(dve, n_("first"))
                first(V.memset(norm.eps[:], EPS))
                passed(dve, sems)
                with dve.Fori(0, STEPS // 2) as i:
                    link = Link(dve, n_("link"), i * LINKS, LINKS)
                    for h in range(2):
                        t = Turn(0, i, h)
                        dve.wait_ge(n_("turned"), t.n())
                        dve.wait_ge(x_in[h], t.slot(48))
                        dve.wait_ge(stored[h], t.slot(64))
                        link(V.tensor_tensor(x2[:, h], psT[:, h, 0:TB * D].rearrange("p (n d) -> p n d", d=D),
                                             x1[:, h].rearrange("p k g d -> p (k g) d"), ALU.add))
                        V.sem_inc(n_("summed"), 1)
                        norm.vector(nc, dve, link, x2[:, h], hn[:], t.n())
                        link(V.tensor_tensor(rows[:, h], hn[:], per_tile(own_nodes(K, "dis", i, h)), ALU.mult))
                        V.sem_inc(n_("rows"), 1)
                    link.end()

            @block.scalar
            def _(act):
                nc.scalar.preload_act_table(ACT.Sqrt)
                with act.Fori(0, STEPS // 2) as i:
                    for h in range(2):
                        t = Turn(0, i, h)
                        norm.scalar(nc, act, t.n())
                        act.wait_ge(n_("rows"), t.n())
                        store_rows(act, K["x2"], x2[:, h], i * (2 * PAIRS) + h * PAIRS, stored[h])
                        store_rows(act, K["table1"], rows[:, h], i * (2 * PAIRS) + h * PAIRS, stored[h])
        stores_done(nc, sems, [(stored, 64)], 0)


def own_nodes(K, name, i, h):
    return K[name][:, bass.ds(i * (2 * PAIRS) + h * PAIRS, PAIRS), :].rearrange("p k g -> p (k g)")


def sum_edges(nc, K, sems, rep, table, order):
    by_src = order == "src"
    with ExitStack() as ctx:
        sb = lambda n, s, dt=F32: ctx.enter_context(nc.sbuf_tensor("sum%d_" % rep + n, s, dt))
        pb = lambda n, s: ctx.enter_context(nc.psum_tensor("sum%d_" % rep + n, s, F32))
        index, mask = sb("index", [P, 2, TB], I32), sb("mask", [D, 2, EB], BF16)
        pay = sb("pay", [P, 2, TB, PAYW])
        got, z, sums = sb("got", [P, 2, TB, D]), sb("z", [P, 2, TB, D]), sb("sums", [D, 2, EB])
        out = sb("out", [P, 2, TB, D])
        psS, psB = pb("psS", [D, 2, EB]), pb("psB", [P, 2, 512])
        n_ = lambda name: sems("sum_" + name)
        index_in, mask_in, got_in, stored = (sems.pair("sum_" + n) for n in ("index_in", "mask_in", "got", "stored"))
        links, links_before = (2 * 2, 0) if by_src else (2 * 1, rep * (STEPS // 2) * 2)
        link_sem = n_("src_link") if by_src else n_("dst_link")
        with nc.Block() as block:
            @block.sync
            def _(sp):
                with sp.Fori(0, STEPS // 2) as i:
                    for h in range(2):
                        t = Turn(rep, i, h)
                        s = i * 2 + h
                        sp.wait_ge(n_("turned"), t.n())
                        if by_src:
                            sp.dma_start(pay[:, h].rearrange("p j c -> p (j c)"),
                                         K["pay_sorted"][:, bass.ds(s * (TB * PAYW), TB * PAYW)]).then_inc(index_in[h], 16)
                        else:
                            sp.dma_start(index[:, h, :], K["dst_src"][:, bass.ds(s * TB, TB)]).then_inc(index_in[h], 16)
                        sp.wait_ge(n_("scanned"), t.n())
                        sp.dma_start(mask[:, h], K["mask_" + order][bass.ds(s, 1), 0:EB].broadcast_to([D, EB])).then_inc(mask_in[h], 16)

            @block.gpsimd
            def _(pool):
                with pool.Fori(0, STEPS // 2) as i:
                    for h in range(2):
                        t = Turn(rep, i, h)
                        pool.wait_ge(index_in[h], t.slot())
                        passed(pool, sems)
                        for j in range(TB):
                            at = pay[:, h, j, PAYW - 1:PAYW].bitcast(I32) if by_src else index[:, h, j:j + 1]
                            gather(pool, got[:, h, j, :], table, at).then_inc(got_in[h], 16)

            @block.tensor
            def _(pe):
                with pe.Fori(0, STEPS // 2) as i:
                    for h in range(2):
                        t = Turn(rep, i, h)
                        if by_src:
                            pe.wait_ge(n_("weighted"), t.n() - rep * STEPS)
                        else:
                            pe.wait_ge(got_in[h], t.slot(16 * TB))
                        passed(pe, sems)
                        for j in range(TB):
                            last = nc.tensor.transpose(psS[:, h, j * P:(j + 1) * P], (z if by_src else got)[:, h, j, :], K["ident"][:])
                        last.then_inc(n_("turned"), 1)
                        pe.wait_ge(n_("scanned"), t.n() + 2)
                        pe.wait_ge(n_("copied"), t.n())
                        passed(pe, sems)
                        for j in range(TB):
                            last = nc.tensor.transpose(psB[:, h, j * D:(j + 1) * D], sums[:, h, j * P:(j + 1) * P], K["ident"][0:D, 0:D])
                        last.then_inc(n_("back"), 1)

            @block.vector
            def _(dve):
                V = nc.vector
                first = Link(dve, n_("first"), rep)
                first(V.memset(sums[:], 0.0))
                passed(dve, sems)
                with dve.Fori(0, STEPS // 2) as i:
                    link = Link(dve, link_sem, links_before + i * links, links)
                    for h in range(2):
                        t = Turn(rep, i, h)
                        if by_src:
                            dve.wait_ge(got_in[h], t.slot(16 * TB))
                            link(V.tensor_tensor(z[:, h], got[:, h], pay[:, h, :, PAYW - 2:PAYW - 1].broadcast_to([P, TB, D]), ALU.mult))
                            V.sem_inc(n_("weighted"), 1)
                        dve.wait_ge(n_("turned"), t.n() + 2)
                        dve.wait_ge(mask_in[h], t.slot())
                        link(V.tensor_tensor_scan(sums[:, h, :], mask[:, h, :], psS[:, h, :], sums[:, 1 - h, EB - 1:EB], ALU.mult, ALU.add))
                        V.sem_inc(n_("scanned"), 1)
                    link.end()

            @block.scalar
            def _(act):
                nc.scalar.preload_act_table(ACT.Square)
                with act.Fori(0, STEPS // 2) as i:
                    for h in range(2):
                        t = Turn(rep, i, h)
                        act.wait_ge(n_("back"), t.n())
                        act.wait_ge(stored[h], t.slot())
                        nc.scalar.copy(out[:, h], psB[:, h, 0:TB * D].rearrange("p (j d) -> p j d", d=D)).then_inc(n_("copied"), 1)
                        act.wait_ge(n_("copied"), t.n() + 2)
                        act.dma_start(K["sum_scan"][0:ROWS, :].rearrange("(t p) c -> p t c", p=P)[:, bass.ds((i * 2 + h) * TB, TB), :],
                                      out[:, h]).then_inc(stored[h], 16)
        stores_done(nc, sems, [(stored, 16)], rep)


def conv_hidden(nc, K, sems):
    io = K["io"]
    with ExitStack() as ctx:
        sb = lambda n, s, dt=F32: ctx.enter_context(nc.sbuf_tensor("hid_" + n, s, dt))
        pb = lambda n, s: ctx.enter_context(nc.psum_tensor("hid_" + n, s, F32))
        index, got = sb("index", [P, 2, TB], I32), sb("got", [P, 2, TB, D])
        y, w, rows = sb("y", [P, 2, PAIRS, 2 * D]), sb("w", [P, 2 * D]), sb("rows", [P, 2, TB, D])
        dis_has = sb("dis_has", [P, HALF, 2])
        K["dis_has"] = dis_has
        turn = Turned(nc, sb, pb, sems, "hid")
        n_ = lambda name: sems("hid_" + name)
        got_in, stored, loaded = sems.pair("hid_got"), sems.pair("hid_stored"), n_("in")
        LINKS = 2 * 2
        with nc.Block() as block:
            @block.sync
            def _(sp):
                sp.dma_start(w[:], io["w1"]).then_inc(loaded, 16)

                def loads(t, link):
                    index_loads(nc, sp, K, sems, "hid", t, index[:].rearrange("p h (k g) -> p h k g", g=2), "end_dst", t.s)
                pipeline(sp, None, [(0, loads, 0)], peel=2)

            @block.gpsimd
            def _(pool):
                with pool.Fori(0, STEPS // 2) as i:
                    for h in range(2):
                        gathers(nc, pool, sems, "hid", Turn(0, i, h), got, K["sum_scan"],
                                index[:, h].rearrange("p (n o) -> p n o", o=1))

            @block.tensor
            def _(pe):
                pe.wait_ge(loaded, 16)
                with pe.Fori(0, STEPS // 2) as i:
                    for h in range(2):
                        turn.tensor(pe, Turn(0, i, h), y, K["ident"], w)

            @block.vector
            def _(dve):
                V = nc.vector
                first = Link(dve, n_("first"))
                first(V.tensor_tensor(dis_has[:], K["dis"][:], K["has"][:], ALU.mult))
                passed(dve, sems)
                with dve.Fori(0, STEPS // 2) as i:
                    link = Link(dve, n_("link"), i * LINKS, LINKS)
                    for h in range(2):
                        t = Turn(0, i, h)
                        dve.wait_ge(got_in[h], t.slot(16 * TB))
                        link(V.tensor_tensor(y[:, h].rearrange("p k (g d) -> p (k g) d", g=2), got[:, h],
                                             per_tile(own_nodes(K, "dis_has", i, h)), ALU.mult))
                        V.sem_inc(n_("got_used"), 1)
                        V.sem_inc(turn.ready, 1)
                        dve.wait_ge(turn.multiplied, t.n())
                        dve.wait_ge(stored[h], t.slot(32))
                        link(V.scalar_tensor_tensor(rows[:, h], turn.product(h), 0.0, per_tile(own_nodes(K, "dis", i, h)),
                                                    ALU.max, ALU.mult))
                        V.sem_inc(n_("rows"), 1)
                    link.end()

            @block.scalar
            def _(act):
                nc.scalar.preload_act_table(ACT.Square)
                with act.Fori(0, STEPS // 2) as i:
                    for h in range(2):
                        t = Turn(0, i, h)
                        turn.scalar(act, t)
                        act.wait_ge(n_("rows"), t.n())
                        store_rows(act, K["table2"], rows[:, h], i * (2 * PAIRS) + h * PAIRS, stored[h])
        stores_done(nc, sems, [(stored, 32)], 0)


def conv_out(nc, K, sems):
    io = K["io"]
    with ExitStack() as ctx:
        sb = lambda n, s, dt=F32: ctx.enter_context(nc.sbuf_tensor("cou_" + n, s, dt))
        pb = lambda n, s: ctx.enter_context(nc.psum_tensor("cou_" + n, s, F32))
        index, got = sb("index", [P, 2, TB], I32), sb("got", [P, 2, TB, D])
        y, w, w3 = sb("y", [P, 2, PAIRS, 2 * D]), sb("w", [P, 2 * D]), sb("w3", [P, 2 * D])
        rows, hn = sb("rows", [P, 2, TB, D]), sb("hn", [P, 2, PAIRS, 2 * D])
        x2, x3 = sb("x2", [P, 2, PAIRS, 2, D]), sb("x3", [P, 2, TB, D])
        dis_has = sb("dis_has", [P, HALF, 2])
        K["dis_has"] = dis_has
        turn = Turned(nc, sb, pb, sems, "cou")
        hT3 = sb("hT3", [P, 2, PAIRS * P])
        norm = Norm(sb, sems, "cou_norm")
        n_ = lambda name: sems("cou_" + name)
        got_in, stored, loaded, x_in = sems.pair("cou_got"), sems.pair("cou_stored"), n_("in"), sems.pair("cou_x_in")
        LINKS = 2 * (Norm.LINKS + 3)
        with nc.Block() as block:
            @block.sync
            def _(sp):
                sp.dma_start(w[:], io["w2"]).then_inc(loaded, 16)
                sp.dma_start(w3[:], io["w3"]).then_inc(loaded, 16)

                def loads(t, link):
                    index_loads(nc, sp, K, sems, "cou", t, index[:].rearrange("p h (k g) -> p h k g", g=2), "end_dst", t.s)
                    sp.wait_ge(n_("summed"), t.n())
                    for g in range(2):
                        sp.dma_start(x2[:, t.h, :, g, :], node_rows(K["x2"], g, t.s * PAIRS)).then_inc(x_in[t.h], 16)
                pipeline(sp, None, [(0, loads, 0)], peel=2)

            @block.gpsimd
            def _(pool):
                with pool.Fori(0, STEPS // 2) as i:
                    for h in range(2):
                        gathers(nc, pool, sems, "cou", Turn(0, i, h), got, K["sum_scan"],
                                index[:, h].rearrange("p (n o) -> p n o", o=1))

            @block.tensor
            def _(pe):
                pe.wait_ge(loaded, 32)
                with pe.Fori(0, STEPS // 2) as i:
                    for h in range(2):
                        t = Turn(0, i, h)
                        turn.tensor(pe, t, y, K["ident"], w)
                        pe.wait_ge(n_("hn"), t.n())
                        for k in range(PAIRS):
                            last = nc.tensor.transpose(turn.psT[:, h, k * P:(k + 1) * P], hn[:, h, k, :], K["ident"][:])
                        last.then_inc(n_("turned3"), 1)
                        pe.wait_ge(n_("copied3"), t.n())
                        for k in range(PAIRS):
                            last = nc.tensor.matmul(turn.psR[:, h, k * 2 * D:(k + 1) * 2 * D], hT3[:, h, k * P:(k + 1) * P], w3[:],
                                                    start=True, stop=True)
                        last.then_inc(n_("multiplied3"), 1)

            @block.vector
            def _(dve):
                V = nc.vector
                first = Link(dve, n_("first"))
                first(V.tensor_tensor(dis_has[:], K["dis"][:], K["has"][:], ALU.mult))
                first(V.memset(norm.eps[:], EPS))
                passed(dve, sems)
                with dve.Fori(0, STEPS // 2) as i:
                    link = Link(dve, n_("link"), i * LINKS, LINKS)
                    for h in range(2):
                        t = Turn(0, i, h)
                        dve.wait_ge(got_in[h], t.slot(16 * TB))
                        link(V.tensor_tensor(y[:, h].rearrange("p k (g d) -> p (k g) d", g=2), got[:, h],
                                             per_tile(own_nodes(K, "dis_has", i, h)), ALU.mult))
                        V.sem_inc(n_("got_used"), 1)
                        V.sem_inc(turn.ready, 1)
                        dve.wait_ge(turn.multiplied, t.n())
                        dve.wait_ge(stored[h], t.slot(64))
                        dve.wait_ge(x_in[h], t.slot(32))
                        link(V.tensor_tensor(x3[:, h], turn.product(h), x2[:, h].rearrange("p k g d -> p (k g) d"), ALU.add))
                        V.sem_inc(n_("summed"), 1)
                        norm.vector(nc, dve, link, x3[:, h], hn[:, h].rearrange("p k (g d) -> p (k g) d", g=2), t.n())
                        V.sem_inc(n_("hn"), 1)
                        dve.wait_ge(n_("multiplied3"), t.n())
                        link(V.tensor_tensor(rows[:, h], turn.product(h), per_tile(own_nodes(K, "dis_s", i, h)), ALU.mult))
                        V.sem_inc(n_("rows"), 1)
                    link.end()

            @block.scalar
            def _(act):
                nc.scalar.preload_act_table(ACT.Sqrt)
                with act.Fori(0, STEPS // 2) as i:
                    for h in range(2):
                        t = Turn(0, i, h)
                        turn.scalar(act, t)
                        norm.scalar(nc, act, t.n())
                        act.wait_ge(n_("turned3"), t.n())
                        nc.scalar.copy(hT3[:, h], turn.psT[:, h, 0:PAIRS * P]).then_inc(n_("copied3"), 1)
                        act.wait_ge(n_("rows"), t.n())
                        store_rows(act, K["x3"], x3[:, h], i * (2 * PAIRS) + h * PAIRS, stored[h])
                        store_rows(act, K["table3"], rows[:, h], i * (2 * PAIRS) + h * PAIRS, stored[h])
        stores_done(nc, sems, [(stored, 64)], 0)


def last_nodes(nc, K, sems):
    io = K["io"]
    with ExitStack() as ctx:
        sb = lambda n, s, dt=F32: ctx.enter_context(nc.sbuf_tensor("fin_" + n, s, dt))
        index, got = sb("index", [P, 2, TB], I32), sb("got", [P, 2, TB, D])
        bias, x3, y = sb("bias", [P, D]), sb("x3", [P, 2, PAIRS, 2, D]), sb("y", [P, 2, TB, D])
        n_ = lambda name: sems("fin_" + name)
        got_in, stored, loaded, x_in = sems.pair("fin_got"), sems.pair("fin_stored"), n_("in"), sems.pair("fin_x_in")
        LINKS = 2 * 3
        with nc.Block() as block:
            @block.sync
            def _(sp):
                sp.dma_start(bias[:], io["last_bias"]).then_inc(loaded, 16)

                def loads(t, link):
                    index_loads(nc, sp, K, sems, "fin", t, index[:].rearrange("p h (k g) -> p h k g", g=2), "end_src", t.s)
                    sp.wait_ge(n_("got_used"), t.n())
                    for g in range(2):
                        sp.dma_start(x3[:, t.h, :, g, :], node_rows(K["x3"], g, t.s * PAIRS)).then_inc(x_in[t.h], 16)
                pipeline(sp, None, [(0, loads, 0)], peel=2)

            @block.gpsimd
            def _(pool):
                with pool.Fori(0, STEPS // 2) as i:
                    for h in range(2):
                        gathers(nc, pool, sems, "fin", Turn(0, i, h), got, K["sum_scan"],
                                index[:, h].rearrange("p (n o) -> p n o", o=1))

            @block.vector
            def _(dve):
                V = nc.vector
                dve.wait_ge(loaded, 16)
                with dve.Fori(0, STEPS // 2) as i:
                    link = Link(dve, n_("link"), i * LINKS, LINKS)
                    for h in range(2):
                        t = Turn(0, i, h)
                        dve.wait_ge(got_in[h], t.slot(16 * TB))
                        dve.wait_ge(x_in[h], t.slot(32))
                        dve.wait_ge(stored[h], t.slot(32))
                        link(V.tensor_tensor(y[:, h], got[:, h], per_tile(own_nodes(K, "dis_s", i, h)), ALU.mult))
                        link(V.tensor_tensor(y[:, h], y[:, h], per_feature(bias[:]), ALU.add))
                        link(V.tensor_tensor(y[:, h], y[:, h], x3[:, h].rearrange("p k g d -> p (k g) d"), ALU.add))
                        V.sem_inc(n_("got_used"), 1)
                        V.sem_inc(n_("y"), 1)
                    link.end()

            @block.scalar
            def _(act):
                with act.Fori(0, STEPS // 2) as i:
                    for h in range(2):
                        t = Turn(0, i, h)
                        act.wait_ge(n_("y"), t.n())
                        store_rows(act, K["out"], y[:, h], i * (2 * PAIRS) + h * PAIRS, stored[h])
        stores_done(nc, sems, [(stored, 32)], 0)


def both_halves(w, w1=None):
    w1 = w if w1 is None else w1
    z = np.zeros(w.shape[:-2] + (D, w.shape[-1]), np.float32)
    return np.concatenate([np.concatenate([w, z], -1), np.concatenate([z, w1], -1)], -2)


def layout(inputs):
    g = {k: np.asarray(v) for k, v in inputs.items()}
    a = {}
    pad = ROWS - E
    src = np.concatenate([g["src"], np.zeros(pad, np.int32)])
    dst = np.concatenate([g["dst"], np.full(pad, PAD_KEY, np.int32)])
    a["src_cols"] = np.ascontiguousarray(src.reshape(TILES, P).T)
    a["dst_cols"] = np.ascontiguousarray(dst.reshape(TILES, P).T)
    a["dst_line"] = np.concatenate([np.full(1, -1, np.int32), dst])[:, None]
    a["src_sort"] = np.concatenate([g["src"], np.full(pad, PAD_KEY, np.int32),
                                    np.full(P * SORTF - ROWS, 57000, np.int32)]).reshape(P, SORTF)
    i = np.arange(P * SORTF).reshape(P, SORTF)
    a["sort_index"] = i.astype(np.float32)
    bit = [(i >> k) & 1 for k in range(1, LEVELS + 1)]
    turn = [bit[0]] + [bit[k - 1] ^ bit[k] for k in range(1, LEVELS)]
    a["sort_signs"] = np.ascontiguousarray(np.stack([1.0 - 2.0 * t for t in turn], 1).astype(np.float32))
    a["zeros"] = np.zeros((1, 4 * D), np.float32)
    a["minus_one"] = np.full((1, 1), -1.0, np.float32)
    eye = np.eye(P, dtype=np.float32)
    fold = np.tile(np.eye(D, dtype=np.float32), (2, 2))
    tri = np.triu(np.ones((P, P), np.float32))
    sel = np.zeros((P, P), np.float32)
    sel[0, 0:D] = 1.0
    sel[1, D:] = 1.0
    zeros = lambda n: np.zeros((pad, n), np.float32)
    a["pay"] = np.concatenate([np.concatenate([g["edge_attr_5"], zeros(5)]),
                               np.ones((ROWS, 1), np.float32),
                               np.concatenate([g["edge_weight"][:, None], zeros(1)]),
                               np.zeros((ROWS, 1), np.float32)], 1)
    a["x"] = np.concatenate([g["x"], zeros(D)])
    rows = lambda v: np.ascontiguousarray(np.broadcast_to(v.reshape(1, -1), (P, v.size)))
    a["w_lin"] = both_halves(g["L0_gnn_W_lin"])
    a["b_lin"] = rows(g["L0_gnn_b_lin"])
    a["att_own"] = rows(g["L0_gnn_att"][0, :, :D])
    a["att_other"] = both_halves(g["L0_gnn_att"][0, 0, D:, None], g["L0_gnn_att"][0, 1, D:, None])
    a["w_edge"] = np.concatenate([g["L0_gnn_W_edge"], g["L0_gnn_b_edge"][None]])
    a["att_bias"] = rows(g["L0_gnn_bias"])
    wide = lambda v: np.ascontiguousarray(np.broadcast_to(v[:, None, :], (LAYERS, P, D)))
    twice = lambda v: np.ascontiguousarray(np.concatenate([v, v], 1)[:, :, None])
    top = both_halves(g["L1_gnn_WM"][:, :D])
    a["w_top"] = np.concatenate([top, top[:1]])
    a["w_bot"] = both_halves(g["L1_gnn_WM"][:, D:])
    a["w_own"] = both_halves(g["L1_gnn_WU"][:, :D])
    agg = g["L1_gnn_WU"][:, D:].reshape(LAYERS, 3, 3, P, D)
    a["w_agg"] = np.ascontiguousarray(agg.transpose(0, 3, 2, 1, 4)).reshape(LAYERS, P, 9 * D)
    a["bM"], a["bU"] = wide(g["L1_gnn_bM"]), twice(g["L1_gnn_bU"])
    a["w_mix"] = both_halves(g["L1_gnn_Wmix"])
    a["b_mix"] = twice(g["L1_gnn_bmix"])
    for name in ("gamma_t", "beta_t", "gamma_o", "beta_o"):
        a[name] = twice(g["L1_gnn_" + name])
    a["w1"], a["w2"] = both_halves(g["L2_gnn_W1"]), both_halves(g["L2_gnn_W2"])
    a["w3"], a["last_bias"] = both_halves(g["L3_gnn_weight"]), rows(g["L3_gnn_bias"])
    a["consts"] = np.concatenate([eye, fold, tri, sel, np.tile(np.arange(TILES, dtype=np.float32), (P, 1))], 1)
    return a


def kernel(**inputs):
    import concourse.bacc as bacc
    from concourse.bass_utils import run_bass_kernel_spmd

    nc = bacc.Bacc("TRN2", target_bir_lowering=False, num_devices=1)
    arrays = {"in_" + k: np.ascontiguousarray(v) for k, v in layout(inputs).items()}
    io = {k[3:]: nc.dram_tensor(k, a.shape, mybir.dt.from_np(a.dtype), kind="ExternalInput").ap() for k, a in arrays.items()}
    out = nc.dram_tensor("out", [ROWS, D], F32, kind="ExternalOutput").ap()
    program(nc, io, out)
    r = run_bass_kernel_spmd(nc, [arrays], core_ids=[0])
    return r.results[0]["out"][:N]
```

```python
import numpy as np
import concourse.bass as bass
import concourse.mybir as mybir
from concourse.alu_op_type import AluOpType as ALU
from contextlib import ExitStack

F32 = mybir.dt.float32
BF16 = mybir.dt.bfloat16
I32 = mybir.dt.int32
ACT = mybir.ActivationFunctionType
AX = mybir.AxisListType

P = 128
N = 50000
E = 50000
D = 64
LAYERS = 4
TILES = 392
ROWS = TILES * P
HALF = TILES // 2
COLS = HALF * P
TB = 4
STEPS = TILES // TB
EB = TB * P
PAIRS = TB // 2
WB = 8
WSTEPS = TILES // WB
WPAIRS = WB // 2
DPAIRS = 7
DSTEPS = HALF // DPAIRS
DC = DPAIRS * P
DM = DC // 2
PAD_KEY = ROWS - 1
SORTF = 512
LEVELS = 16
SRC_MID = 25000
BIG = 3.0e38
EPS = 1e-5
DELTA = 2.5
NSCALE = 1.0 / float(np.sqrt(N))
S0W = 130
PAYW = 8
G1COLS = N - COLS
STATF = 346
STATN = G1COLS // STATF
STATB = 4
HOTB = 4
assert STATN % STATB == 0 and TILES % HOTB == 0 and STATN * STATF == G1COLS and WSTEPS * WB == TILES and STEPS % 2 == 0 and DSTEPS * DPAIRS == HALF


class Link:

    def __init__(self, eng, sem, base=0):
        self.eng, self.sem, self.base, self.n = eng, sem, base, 0

    def __call__(self, ins):
        self.n += 1
        ins.then_inc(self.sem, 1)
        self.eng.wait_ge(self.sem, self.base + self.n)

    def put(self, ins):
        self.n += 1
        ins.then_inc(self.sem, 1)
        return self.n

    def on(self, n):
        self.eng.wait_ge(self.sem, self.base + n)


class Sems:

    def __init__(self, nc):
        self.ctx, self.nc, self.made = ExitStack(), nc, {}

    def __call__(self, name):
        if name not in self.made:
            self.made[name] = self.ctx.enter_context(self.nc.semaphore(name))
        return self.made[name]

    def pair(self, name):
        return [self(name + "_0"), self(name + "_1")]

    def start(self, prefixes):
        with self.nc.Block() as block:
            @block.sync
            def _(sp):
                for name in FREE_TWO:
                    if name.startswith(prefixes):
                        sp.sem_inc(self(name), 2)
                for name, k in FREE_SOME.items():
                    if name.startswith(prefixes):
                        sp.sem_inc(self(name), k)
                for name, k in FREE_DMA.items():
                    if name.startswith(prefixes):
                        for s in self.pair(name):
                            sp.sem_inc(s, k)


class PhaseSems(Sems):

    def __init__(self, nc, prefix, lasting):
        super().__init__(nc)
        self.prefix, self.lasting = prefix, lasting

    def __call__(self, name):
        if "_got_" in name and name[-1] in "01" or name == "passed":
            return self.lasting(name)
        return super().__call__(name)

    def __enter__(self):
        self.start((self.prefix,))
        return self

    def __exit__(self, *error):
        with self.nc.Block() as block:
            @block.sync
            def _(sp):
                for s in self.made.values():
                    sp.sem_clear(s)
        self.ctx.close()


def gather(pool, out, table, index):
    return pool.indirect_dma_start(out=out, out_offset=None, in_=table,
                                   in_offset=bass.IndirectOffsetOnAxis(ap=index, axis=0))


def passed(eng, sems):
    eng.sem_inc(sems("passed"), 1)


def node_rows(table, g, q, n=WPAIRS):
    return table.rearrange("(g q p) d -> g p q d", g=2, p=P)[g][:, bass.ds(q, n), :]


def program(nc, io, out):
    with ExitStack() as ctx:
        sems = Sems(nc)
        ctx.enter_context(sems.ctx)

        def dram(name, shape, dt=F32):
            return nc.dram_tensor(name, shape, dt, kind="Internal").ap()

        def sb(name, shape, dt=F32):
            return ctx.enter_context(nc.sbuf_tensor(name, shape, dt))

        mem = {"io": io, "out": out}
        mem["sorted_src"] = dram("sorted_src", [ROWS + 1, 1])
        mem["mask_dst"] = dram("mask_dst", [STEPS, 2 * EB], BF16)
        mem["mask_src"] = dram("mask_src", [STEPS, 2 * EB], BF16)
        mem["edge_of"] = dram("edge_of", [P, TILES], I32)
        mem["pay_rows"] = dram("pay_rows", [ROWS, PAYW])
        mem["pay_sorted"] = dram("pay_sorted", [P, TILES * PAYW])
        mem["att_table"] = dram("att_table", [ROWS, 2 * D])
        mem["att_src"] = dram("att_src", [ROWS, 2])
        mem["att_scan"] = dram("att_scan", [ROWS + 1, S0W])
        mem["x1"] = dram("x1", [ROWS, D])
        mem["x2"] = dram("x2", [ROWS, D])
        mem["x3"] = dram("x3", [ROWS, D])
        mem["hT"] = dram("hT", [P, COLS])
        mem["msg_table"] = dram("msg_table", [ROWS, D])
        mem["pna_scan"] = dram("pna_scan", [ROWS + 1, 4 * D])
        mem["table1"] = dram("table1", [ROWS, D])
        mem["table2"] = dram("table2", [ROWS, D])
        mem["table3"] = dram("table3", [ROWS, D])
        mem["sum_scan"] = dram("sum_scan", [ROWS + 1, D])

        mem["ident"] = sb("ident", [P, P])
        mem["fold"] = sb("fold", [P, P])
        mem["dst_src"] = sb("dst_src", [P, TILES], I32)
        mem["src_src"] = sb("src_src", [P, TILES], I32)
        mem["end_dst"] = sb("end_dst", [P, HALF, 2], I32)
        mem["end_src"] = sb("end_src", [P, HALF, 2], I32)
        for name in ("deg", "has", "inv", "amp", "att", "dis", "has_s", "dis_s"):
            mem[name] = sb("node_" + name, [P, HALF, 2])

        start(nc, mem, sems)
        sems.start(("pne_", "pnn_", "mix_", "pno_", "sum_"))
        with PhaseSems(nc, "sort_", sems) as own:
            sort_edges(nc, mem, own)
        with PhaseSems(nc, "mask_", sems) as own:
            masks(nc, mem, own)
        with PhaseSems(nc, "deg_", sems) as own:
            degrees(nc, mem, own)
        with PhaseSems(nc, "att_", sems) as own:
            attention_tables(nc, mem, own)
        with PhaseSems(nc, "ate_", sems) as own:
            attention_edges(nc, mem, own)
        with PhaseSems(nc, "atn_", sems) as own:
            attention_nodes(nc, mem, own)
        with nc.sbuf_tensor("U", [P, COLS], F32) as U:
            mem["U"] = U
            with nc.Fori(0, LAYERS) as layer:
                pna_edges(nc, mem, sems, layer)
                pna_nodes(nc, mem, sems, layer)
                pna_mix(nc, mem, sems, layer)
                pna_out(nc, mem, sems, layer)
        with PhaseSems(nc, "end_", sems) as own:
            pna_end(nc, mem, own)
        sum_edges(nc, mem, sems, 0, mem["table1"], "dst")
        with PhaseSems(nc, "hid_", sems) as own:
            conv_hidden(nc, mem, own)
        sum_edges(nc, mem, sems, 1, mem["table2"], "dst")
        with PhaseSems(nc, "cou_", sems) as own:
            conv_out(nc, mem, own)
        sum_edges(nc, mem, sems, 2, mem["table3"], "src")
        with PhaseSems(nc, "fin_", sems) as own:
            last_nodes(nc, mem, own)


FREE_TWO = ("att_x_used", "att_turned", "att_copied", "att_multiplied", "att_used",
            "ate_pay_turned", "ate_mask_used", "ate_scored", "ate_x_summed", "ate_back", "ate_num", "ate_px", "ate_out",
            "atn_got_used", "atn_turned", "atn_copied", "atn_multiplied", "atn_used",
            "pne_turned", "pne_scanned", "pne_copied",
            "pnn_got_used", "pnn_multiplied", "pnn_own", "pnn_product_used", "pnn_u_turned",
            "mix_mixed", "mix_biased", "pno_made", "pno_multiplied",
            "end_summed", "sum_turned", "sum_weighted", "sum_scanned", "sum_copied",
            "hid_got_used", "hid_turned", "hid_copied", "hid_multiplied", "hid_used",
            "cou_got_used", "cou_summed", "cou_turned", "cou_copied", "cou_multiplied", "cou_used",
            "cou_three_turned", "cou_three_copied", "cou_three_multiplied", "cou_three_used", "fin_got_used")
FREE_SOME = {"ate_payT": 1, "ate_xT": 1, "ate_score": 1, "ate_score_used": 1, "ate_p_spread": 1, "ate_r_spread": 1,
             "pnn_own_used": 1, "pnn_u_kept": 1, "pnn_aggT": 3, "pnn_agg_turned": 6, "pno_rows": 4}
FREE_DMA = {"deg_stored": 16, "att_stored": 64, "ate_stored": 16,
            "atn_x1_stored": 32, "atn_hT_stored": 16, "atn_rows_stored": 32, "pne_stored": 16,
            "pno_hn_stored": 16, "pno_rows_stored": 32, "end_x2_stored": 32, "end_rows_stored": 32,
            "sum_stored": 16, "hid_stored": 32, "cou_x3_stored": 32, "cou_rows_stored": 32, "fin_stored": 32}


def start(self, prefixes):
        with self.nc.Block() as block:
            @block.sync
            def _(sp):
                for name in FREE_TWO:
                    if name.startswith(prefixes):
                        sp.sem_inc(self(name), 2)
                for name, k in FREE_SOME.items():
                    if name.startswith(prefixes):
                        sp.sem_inc(self(name), k)
                for name, k in FREE_DMA.items():
                    if name.startswith(prefixes):
                        for s in self.pair(name):
                            sp.sem_inc(s, k)


class PhaseSems(Sems):

    def __init__(self, nc, prefix, lasting):
        super().__init__(nc)
        self.prefix, self.lasting = prefix, lasting

    def __call__(self, name):
        if "_got_" in name and name[-1] in "01" or name == "passed":
            return self.lasting(name)
        return super().__call__(name)

    def __enter__(self):
        self.start((self.prefix,))
        return self

    def __exit__(self, *error):
        with self.nc.Block() as block:
            @block.sync
            def _(sp):
                for s in self.made.values():
                    sp.sem_clear(s)
        self.ctx.close()


def gather(pool, out, table, index):
    return pool.indirect_dma_start(out=out, out_offset=None, in_=table,
                                   in_offset=bass.IndirectOffsetOnAxis(ap=index, axis=0))


def passed(eng, sems):
    eng.sem_inc(sems("passed"), 1)


def node_rows(table, g, q, n=WPAIRS):
    return table.rearrange("(g q p) d -> g p q d", g=2, p=P)[g][:, bass.ds(q, n), :]


def program(nc, io, out):
    with ExitStack() as ctx:
        sems = Sems(nc)
        ctx.enter_context(sems.ctx)

        def dram(name, shape, dt=F32):
            return nc.dram_tensor(name, shape, dt, kind="Internal").ap()

        def sb(name, shape, dt=F32):
            return ctx.enter_context(nc.sbuf_tensor(name, shape, dt))

        mem = {"io": io, "out": out}
        mem["sorted_src"] = dram("sorted_src", [ROWS + 1, 1])
        mem["mask_dst"] = dram("mask_dst", [STEPS, 2 * EB], BF16)
        mem["mask_src"] = dram("mask_src", [STEPS, 2 * EB], BF16)
        mem["edge_of"] = dram("edge_of", [P, TILES], I32)
        mem["pay_rows"] = dram("pay_rows", [ROWS, PAYW])
        mem["pay_sorted"] = dram("pay_sorted", [P, TILES * PAYW])
        mem["att_table"] = dram("att_table", [ROWS, 2 * D])
        mem["att_src"] = dram("att_src", [ROWS, 2])
        mem["att_scan"] = dram("att_scan", [ROWS + 1, S0W])
        mem["x1"] = dram("x1", [ROWS, D])
        mem["x2"] = dram("x2", [ROWS, D])
        mem["x3"] = dram("x3", [ROWS, D])
        mem["hT"] = dram("hT", [P, COLS])
        mem["msg_table"] = dram("msg_table", [ROWS, D])
        mem["pna_scan"] = dram("pna_scan", [ROWS + 1, 4 * D])
        mem["table1"] = dram("table1", [ROWS, D])
        mem["table2"] = dram("table2", [ROWS, D])
        mem["table3"] = dram("table3", [ROWS, D])
        mem["sum_scan"] = dram("sum_scan", [ROWS + 1, D])

        mem["ident"] = sb("ident", [P, P])
        mem["fold"] = sb("fold", [P, P])
        mem["dst_src"] = sb("dst_src", [P, TILES], I32)
        mem["src_src"] = sb("src_src", [P, TILES], I32)
        mem["end_dst"] = sb("end_dst", [P, HALF, 2], I32)
        mem["end_src"] = sb("end_src", [P, HALF, 2], I32)
        for name in ("deg", "has", "inv", "amp", "att", "dis", "has_s", "dis_s"):
            mem[name] = sb("node_" + name, [P, HALF, 2])

        start(nc, mem, sems)
        sems.start(("pne_", "pnn_", "mix_", "pno_", "sum_"))
        with PhaseSems(nc, "sort_", sems) as own:
            sort_edges(nc, mem, own)
        with PhaseSems(nc, "mask_", sems) as own:
            masks(nc, mem, own)
        with PhaseSems(nc, "deg_", sems) as own:
            degrees(nc, mem, own)
        with PhaseSems(nc, "att_", sems) as own:
            attention_tables(nc, mem, own)
        with PhaseSems(nc, "ate_", sems) as own:
            attention_edges(nc, mem, own)
        with PhaseSems(nc, "atn_", sems) as own:
            attention_nodes(nc, mem, own)
        with nc.sbuf_tensor("U", [P, COLS], F32) as U:
            mem["U"] = U
            with nc.Fori(0, LAYERS) as layer:
                pna_edges(nc, mem, sems, layer)
                pna_nodes(nc, mem, sems, layer)
                pna_mix(nc, mem, sems, layer)
                pna_out(nc, mem, sems, layer)
        with PhaseSems(nc, "end_", sems) as own:
            pna_end(nc, mem, own)
        sum_edges(nc, mem, sems, 0, mem["table1"], "dst")
        with PhaseSems(nc, "hid_", sems) as own:
            conv_hidden(nc, mem, own)
        sum_edges(nc, mem, sems, 1, mem["table2"], "dst")
        with PhaseSems(nc, "cou_", sems) as own:
            conv_out(nc, mem, own)
        sum_edges(nc, mem, sems, 2, mem["table3"], "src")
        with PhaseSems(nc, "fin_", sems) as own:
            last_nodes(nc, mem, own)


FREE_TWO = ("att_x_used", "att_turned", "att_copied", "att_multiplied", "att_used",
            "ate_pay_turned", "ate_mask_used", "ate_scored", "ate_x_summed", "ate_back", "ate_num", "ate_px", "ate_out",
            "atn_got_used", "atn_turned", "atn_copied", "atn_multiplied", "atn_used",
            "pne_turned", "pne_scanned", "pne_copied", "pnn_got_used", "pnn_multiplied", "pnn_own", "mix_mixed", "mix_biased",
            "pno_made", "pno_multiplied", "end_summed", "sum_turned", "sum_weighted", "sum_scanned", "sum_copied",
            "hid_got_used", "hid_turned", "hid_copied", "hid_multiplied", "hid_used",
            "cou_got_used", "cou_summed", "cou_turned", "cou_copied", "cou_multiplied", "cou_used",
            "cou_three_turned", "cou_three_copied", "cou_three_multiplied", "cou_three_used", "fin_got_used")
FREE_SOME = {"pno_rows": 4, "ate_payT": 1, "ate_xT": 1, "ate_score": 1, "ate_score_used": 1, "ate_p_spread": 1,
            "ate_r_spread": 1, "pnn_own_used": 1, "pnn_product_used": 2, "pnn_u_kept": 1, "pnn_aggT": 3, "pnn_agg_turned": 6, "pnn_u_turned": 2}
FREE_DMA = {"deg_stored": 16, "att_stored": 64, "ate_stored": 16, "atn_x1_stored": 32, "atn_hT_stored": 16, "atn_rows_stored": 32, "pne_stored": 16,
            "pno_hn_stored": 16, "pno_rows_stored": 32, "end_x2_stored": 32, "end_rows_stored": 32, "sum_stored": 16, "hid_stored": 32, "cou_x3_stored": 32, "cou_rows_stored": 32,
            "fin_stored": 32}


def start(nc, mem, sems):
    io = mem["io"]
    with nc.Block() as block:
        @block.sync
        def _(sp):
            sp.dma_start(mem["ident"][:], io["consts"][:, 0:P]).then_inc(sems("const_in"), 16)
            sp.dma_start(mem["fold"][:], io["consts"][:, P:2 * P]).then_inc(sems("const_in"), 16)
            sp.dma_start(mem["dst_src"][:], io["src_cols"]).then_inc(sems("const_in"), 16)
            for name in ("att_scan", "pna_scan", "sum_scan"):
                table = mem[name][ROWS:ROWS + 1, :]
                sp.dma_start(table, io["zeros"][:, 0:table.shape[1]]).then_inc(sems("const_in"), 16)
            sp.wait_ge(sems("const_in"), 96)


class Turn:

    def __init__(self, rep, i, at, steps=STEPS):
        self.rep, self.i, self.at, self.steps, self.h = rep, i, at, steps, at % 2
        self.s = i * 2 + at

    def n(self, k=1):
        return self.rep * (self.steps * k) + self.i * (2 * k) + (self.at + 1) * k

    def slot(self, k=16):
        return self.rep * (self.steps // 2 * k) + self.i * k + (self.at // 2 + 1) * k


def pipeline(eng, sem, parts, rep=0, steps=STEPS, peel=0):
    total = steps * sum(k for _, _, k in parts)
    lag = max([peel] + [l for l, _, _ in parts])
    turns = (steps - lag) // 2
    per_turn = 2 * sum(k for _, _, k in parts)
    link = Link(eng, sem, rep * total)

    def time(t, i=0, inside=False):
        for l, part, k in parts:
            if inside or 0 <= t - l < steps:
                before = link.n
                turn = Turn(rep, i, t - l, steps)
                turn.first = not inside and t - l < 2
                part(turn, link)
                assert link.n == before + k, (part, link.n - before, k)

    for t in range(lag):
        time(t)
    done = link.n
    with eng.Fori(0, turns) as i:
        link.base, link.n = rep * total + done + i * per_turn, 0
        time(lag, i, True)
        time(lag + 1, i, True)
    link.base, link.n = rep * total, done + turns * per_turn
    for t in range(lag + 2 * turns, steps + lag):
        time(t)


def node_pipeline(eng, sem, parts, peel=0):
    pipeline(eng, sem, parts, 0, WSTEPS, peel)


def sort_edges(nc, mem, sems):
    io = mem["io"]
    nblk = SORTF // P
    with ExitStack() as ctx:
        sb = lambda n, s, dt=F32: ctx.enter_context(nc.sbuf_tensor("sort_" + n, s, dt))
        key_i = sb("key_i", [P, SORTF], I32)
        word_i = sb("word_i", [P, SORTF], I32)
        low_i = sb("low_i", [P, SORTF], I32)
        src_f = sb("src_f", [P, SORTF])
        neg = sb("neg", [P, SORTF])
        t1 = sb("t1", [P, SORTF])
        t2 = sb("t2", [P, SORTF])
        index = sb("index", [P, SORTF])
        signs = sb("signs", [P, LEVELS, SORTF])
        buf = [sb("a", [P, SORTF]), sb("b", [P, SORTF])]
        ps = ctx.enter_context(nc.psum_tensor("sort_ps", [P, SORTF], F32))
        ps2 = ctx.enter_context(nc.psum_tensor("sort_ps2", [P, SORTF], F32))
        loaded, turned, to_turn = sems("sort_in"), sems("sort_turned"), sems("sort_to_turn")
        ident = mem["ident"]
        done, stored = sems("sort_done"), sems("sort_stored")

        plan = []
        cur = 0
        for level in range(1, LEVELS + 1):
            plan.append(("sign", level, cur))
            j = level - 1
            if j >= 9:
                plan.append(("turn", level, cur))
                while j >= 9:
                    plan.append(("step", j - 9, cur))
                    cur ^= 1
                    j -= 1
                plan.append(("turn", level, cur))
            while j >= 0:
                plan.append(("step", j, cur))
                cur ^= 1
                j -= 1
        turn_bufs = [c for kind, _, c in plan if kind == "turn"]

        with nc.Block() as block:
            @block.sync
            def _(sp):
                sp.dma_start(key_i[:], io["src_sort"]).then_inc(loaded, 16)
                sp.dma_start(index[:], io["sort_index"]).then_inc(loaded, 16)
                sp.dma_start(signs[:], io["sort_signs"]).then_inc(loaded, 16)
                sp.wait_ge(done, 1)
                sp.dma_start(mem["sorted_src"][1:ROWS + 1, :].rearrange("(p f) o -> p (f o)", f=SORTF),
                             src_f[0:ROWS // SORTF, :]).then_inc(stored, 16)
                sp.dma_start(mem["sorted_src"][0:1, :], io["minus_one"]).then_inc(stored, 16)
                sp.wait_ge(done, 2)
                sp.dma_start(mem["edge_of"], low_i[:, 0:TILES]).then_inc(stored, 16)
                sp.wait_ge(stored, 48)

            @block.vector
            def _(dve):
                link = Link(dve, sems("sort_link"))
                V = nc.vector
                dve.wait_ge(loaded, 48)
                link(V.tensor_copy(src_f[:], key_i[:]))
                link(V.tensor_scalar(neg[:], src_f[:], float(SRC_MID), None, ALU.is_lt))
                link(V.tensor_scalar(t1[:], src_f[:], -2.0, float(0x807F + SRC_MID - 0x80 + SRC_MID), ALU.mult, ALU.add))
                link(V.tensor_tensor(t1[:], t1[:], neg[:], ALU.mult))
                link(V.scalar_tensor_tensor(t1[:], src_f[:], float(0x80 - SRC_MID), t1[:], ALU.add, ALU.add))
                link(V.tensor_copy(word_i[:], t1[:]))
                link(V.tensor_scalar(word_i[:], word_i[:], 16, None, ALU.logical_shift_left))
                link(V.tensor_scalar(t2[:], index[:], -2.0, 65535.0, ALU.mult, ALU.add))
                link(V.tensor_tensor(t2[:], t2[:], neg[:], ALU.mult))
                link(V.tensor_tensor(t2[:], t2[:], index[:], ALU.add))
                link(V.tensor_copy(low_i[:], t2[:]))
                link(V.tensor_tensor(buf[0][:].bitcast(I32), word_i[:], low_i[:], ALU.bitwise_or))
                nturn = 0
                for kind, a, c in plan:
                    x, y = buf[c], buf[c ^ 1]
                    if kind == "sign":
                        link(V.tensor_tensor(x[:], x[:], signs[:, a - 1, :], ALU.mult))
                    elif kind == "turn":
                        nturn += 1
                        V.sem_inc(to_turn, 1)
                        dve.wait_ge(turned, nturn)
                        link(V.tensor_copy(x[:], ps[:]))
                    else:
                        xs = x[:].rearrange("p (b t l) -> p b t l", t=2, l=1 << a)
                        ys = y[:].rearrange("p (b t l) -> p b t l", t=2, l=1 << a)
                        V.tensor_tensor(ys[:, :, 0], xs[:, :, 0], xs[:, :, 1], ALU.min).then_inc(sems("sort_link"), 1)
                        link.n += 1
                        link(V.tensor_tensor(ys[:, :, 1], xs[:, :, 0], xs[:, :, 1], ALU.max))
                final = buf[cur][:].bitcast(I32)
                link(V.tensor_scalar(word_i[:], final, 31, 1, ALU.logical_shift_right, ALU.bitwise_and))
                link(V.tensor_copy(neg[:], word_i[:]))
                link(V.tensor_scalar(key_i[:], final, 16, 0x7FFF, ALU.logical_shift_right, ALU.bitwise_and))
                link(V.tensor_copy(src_f[:], key_i[:]))
                link(V.tensor_scalar(low_i[:], final, 0xFFFF, None, ALU.bitwise_and))
                link(V.tensor_copy(index[:], low_i[:]))
                link(V.tensor_scalar(t1[:], src_f[:], -2.0, float(0x807F + SRC_MID - 0x8000 - SRC_MID + 0x80), ALU.mult, ALU.add))
                link(V.tensor_tensor(t1[:], t1[:], neg[:], ALU.mult))
                link(V.scalar_tensor_tensor(src_f[:], src_f[:], float(SRC_MID - 0x80), t1[:], ALU.add, ALU.add))
                V.sem_inc(done, 1)
                link(V.tensor_scalar(t2[:], index[:], -2.0, 65535.0, ALU.mult, ALU.add))
                link(V.tensor_tensor(t2[:], t2[:], neg[:], ALU.mult))
                link(V.tensor_tensor(index[:], index[:], t2[:], ALU.add))
                V.sem_inc(to_turn, 1)
                dve.wait_ge(turned, nturn + 1)
                cols = lambda t: t.rearrange("p (r c) -> p r c", c=nblk)
                psc = lambda t: t.rearrange("p (c r) -> p r c", c=nblk)
                link(V.tensor_copy(cols(mem["src_src"][:]), psc(ps[:])[:, 0:ROWS // SORTF, :]))
                link(V.tensor_copy(cols(low_i[:, 0:TILES]), psc(ps2[:])[:, 0:ROWS // SORTF, :]))
                V.sem_inc(done, 1)

            @block.tensor
            def _(pe):
                for n, c in enumerate(turn_bufs):
                    pe.wait_ge(to_turn, n + 1)
                    for b in range(nblk):
                        last = nc.tensor.transpose(ps[:, b * P:(b + 1) * P], buf[c][:, b * P:(b + 1) * P], ident[:])
                    last.then_inc(turned, 1)
                pe.wait_ge(to_turn, len(turn_bufs) + 1)
                for b in range(nblk):
                    nc.tensor.transpose(ps[:, b * P:(b + 1) * P], src_f[:, b * P:(b + 1) * P], ident[:])
                    last = nc.tensor.transpose(ps2[:, b * P:(b + 1) * P], index[:, b * P:(b + 1) * P], ident[:])
                last.then_inc(turned, 1)


def masks(nc, mem, sems):
    io = mem["io"]
    r = ROWS // EB
    with ExitStack() as ctx:
        sb = lambda n, s, dt=F32: ctx.enter_context(nc.sbuf_tensor("mask_" + n, s, dt))
        key_i, prev_i = sb("key_i", [r, EB], I32), sb("prev_i", [r, EB], I32)
        key, prev = [sb("key0", [r, EB]), sb("key1", [r, EB])], [sb("prev0", [r, EB]), sb("prev1", [r, EB])]
        keep = sb("keep", [r, EB])
        both = [sb("both0", [r, 2, EB], BF16), sb("both1", [r, 2, EB], BF16)]
        loaded, ready, stored = sems("mask_in"), sems("mask_ready"), sems("mask_stored")
        rows = lambda t, o: t[o:o + ROWS, :].rearrange("(p f) o -> p (f o)", f=EB)
        with nc.Block() as block:
            @block.sync
            def _(sp):
                sp.dma_start(key_i[:], rows(io["dst_line"], 1)).then_inc(loaded, 16)
                sp.dma_start(prev_i[:], rows(io["dst_line"], 0)).then_inc(loaded, 16)
                sp.dma_start(key[1][:], rows(mem["sorted_src"], 1)).then_inc(loaded, 16)
                sp.dma_start(prev[1][:], rows(mem["sorted_src"], 0)).then_inc(loaded, 16)
                for n, name in enumerate(("mask_dst", "mask_src")):
                    sp.wait_ge(ready, n + 1)
                    sp.dma_start(mem[name], both[n][:].rearrange("p a f -> p (a f)")).then_inc(stored, 16)
                sp.wait_ge(stored, 32)

            @block.vector
            def _(dve):
                link = Link(dve, sems("mask_link"))
                V = nc.vector
                dve.wait_ge(loaded, 64)
                V.tensor_copy(key[0][:], key_i[:]).then_inc(sems("mask_link"), 1)
                link.n += 1
                link(V.tensor_copy(prev[0][:], prev_i[:]))
                for n in range(2):
                    link(V.tensor_tensor(keep[:], key[n][:], prev[n][:], ALU.is_equal))
                    link(V.tensor_copy(both[n][:, 0, :], keep[:]))
                    link(V.tensor_scalar(both[n][:, 1, :], keep[:], -1.0, BIG, ALU.add, ALU.mult))
                    V.sem_inc(ready, 1)


def degrees(nc, mem, sems):
    io = mem["io"]
    with ExitStack() as ctx:
        sb = lambda n, s, dt=F32: ctx.enter_context(nc.sbuf_tensor("deg_" + n, s, dt))
        pb = lambda n: ctx.enter_context(nc.psum_tensor("deg_" + n, [P, 512], F32))
        iota, iota_h = sb("iota", [P, TILES]), sb("iota_h", [P, TILES], mybir.dt.float16)
        tri = sb("tri", [P, P])
        ones = sb("ones", [P, TILES])
        zero = sb("zero", [P, TILES], BF16)
        dst_i = sb("dst_i", [P, TILES], I32)
        part_i = sb("part_i", [P, TILES], I32)
        low, high = [sb("low0", [P, TILES]), sb("low1", [P, TILES])], [sb("high0", [P, TILES]), sb("high1", [P, TILES])]
        hot_low, hot_high = sb("hot_low", [P, 2, P], BF16), sb("hot_high", [P, 2, TILES], BF16)
        count = [pb("count0"), pb("count1")]
        before, total = pb("before"), pb("total")
        deg = [sb("d0", [P, TILES]), sb("d1", [P, TILES])]
        degm, tmp, cum = sb("degm", [P, TILES]), sb("tmp", [P, TILES]), sb("cum", [P, TILES])
        tot = sb("tot", [P, TILES])
        loaded, hot, used, counted = sems("deg_in"), sems("deg_hot"), sems("deg_hot_free"), sems("deg_counted")
        ready, summed = sems("deg_ready"), sems("deg_summed")
        asked, rooted = sems("deg_asked"), sems("deg_rooted")
        rows = sb("rows", [P, TILES, PAYW])
        dst_rows = sb("dst_rows", [P, TILES], I32)
        index, got = sb("index", [P, 2, TB], I32), sb("got", [P, 2, TB, PAYW])
        pay_in, packed, put = sems("deg_pay_in"), sems("deg_packed"), sems("deg_put")
        index_in, got_in, stored = sems.pair("deg_index_in"), sems.pair("deg_got"), sems.pair("deg_stored")
        by_pair = lambda t: t.rearrange("p (g q) -> p q g", g=2)
        with nc.Block() as block:
            @block.sync
            def _(sp):
                sp.dma_start(iota[:], io["consts"][:, 4 * P:4 * P + TILES]).then_inc(loaded, 16)
                sp.dma_start(tri[:], io["consts"][:, 2 * P:3 * P]).then_inc(loaded, 16)
                sp.dma_start(dst_i[:], io["dst_cols"]).then_inc(loaded, 16)
                sp.dma_start(rows[:], io["pay"].rearrange("(p t) c -> p t c", p=P)).then_inc(pay_in, 16)
                sp.dma_start(dst_rows[:], io["dst_line"][1:ROWS + 1, :].rearrange("(p t) o -> p (t o)", p=P)).then_inc(pay_in, 16)
                sp.wait_ge(packed, 1)
                sp.dma_start(mem["pay_rows"].rearrange("(p t) c -> p t c", p=P), rows[:]).then_inc(put, 16)

                def load_index(t, link):
                    if not t.first:
                        sp.wait_ge(got_in[t.h], t.slot(16 * TB) - 16 * TB)
                    sp.dma_start(index[:, t.h, :], mem["edge_of"][:, bass.ds(t.s * TB, TB)]).then_inc(index_in[t.h], 16)
                pipeline(sp, None, [(0, load_index, 0)], peel=2)

            @block.gpsimd
            def _(pool):
                pool.wait_ge(put, 16)

                def gather_pay(t, link):
                    pool.wait_ge(index_in[t.h], t.slot())
                    pool.wait_ge(stored[t.h], t.slot())
                    passed(pool, sems)
                    for j in range(TB):
                        gather(pool, got[:, t.h, j, :], mem["pay_rows"], index[:, t.h, j:j + 1]).then_inc(got_in[t.h], 16)
                pipeline(pool, None, [(0, gather_pay, 0)])

            @block.vector
            def _(dve):
                link = Link(dve, sems("deg_link"))
                V = nc.vector
                dve.wait_ge(pay_in, 32)
                V.tensor_copy(rows[:, :, PAYW - 1].bitcast(I32), dst_rows[:]).then_inc(packed, 1)
                dve.wait_ge(loaded, 48)
                link(V.memset(ones[:], 1.0))
                link(V.tensor_copy(iota_h[:], iota[:]))
                for n, keys in enumerate((dst_i, mem["src_src"])):
                    link(V.tensor_scalar(part_i[:], keys[:], P - 1, None, ALU.bitwise_and))
                    link(V.tensor_copy(low[n][:], part_i[:]))
                    link(V.tensor_scalar(part_i[:], keys[:], 7, None, ALU.logical_shift_right))
                    link(V.tensor_copy(high[n][:], part_i[:]))
                link(V.memset(zero[:], 0.0))
                link(V.memset(hot_high[:], 0.0))
                V.sem_inc(ready, 1)
                with dve.Fori(0, TILES // HOTB) as i:
                    for j in range(HOTB):
                        for n in range(2):
                            dve.wait_ge(used, i * (2 * HOTB) + (2 * j + n + 1))
                            V.tensor_scalar(hot_low[:, n, :], iota_h[:, 0:P], low[n][:, bass.ds(i * HOTB + j, 1)], None,
                                            ALU.is_equal)
                            V.tensor_scalar(hot_high[:, n, :], iota_h[:], high[n][:, bass.ds(i * HOTB + j, 1)], None,
                                            ALU.is_equal).then_inc(hot, 1)
                dve.wait_ge(counted, 1)
                for n in range(2):
                    link(V.tensor_copy(deg[n][:], count[n][:, 0:TILES]))
                    V.sem_inc(ready, 1)
                for n, end in enumerate((mem["end_dst"], mem["end_src"])):
                    dve.wait_ge(summed, n + 1)
                    link(V.tensor_copy(tot[:], total[:, 0:TILES]))
                    link(V.tensor_tensor_scan(cum[:], ones[:], tot[:], 0.0, ALU.mult, ALU.add))
                    link(V.tensor_tensor(cum[:], cum[:], tot[:], ALU.subtract))
                    link(V.tensor_tensor(cum[:], cum[:], before[:, 0:TILES], ALU.add))
                    link(V.tensor_scalar(tot[:], deg[n][:], 1.0, None, ALU.min))
                    link(V.scalar_tensor_tensor(cum[:], cum[:], -1.0 - ROWS, tot[:], ALU.add, ALU.mult))
                    link(V.tensor_scalar(cum[:], cum[:], float(ROWS), None, ALU.add))
                    link(V.tensor_copy(end[:], by_pair(cum[:])))
                    V.sem_inc(ready, 1)
                link(V.tensor_copy(mem["deg"][:], by_pair(deg[0][:])))
                link(V.tensor_scalar(mem["has"][:], mem["deg"][:], 1.0, None, ALU.min))
                link(V.tensor_copy(mem["has_s"][:], by_pair(deg[1][:])))
                link(V.tensor_scalar(degm[:], mem["has_s"][:].rearrange("p q g -> p (q g)"), 1.0, None, ALU.max))
                link(V.tensor_scalar(mem["has_s"][:], mem["has_s"][:], 1.0, None, ALU.min))
                V.sem_inc(asked, 1)
                dve.wait_ge(rooted, 1)
                flat = lambda t: t[:].rearrange("p q g -> p (q g)")
                link(V.reciprocal(cum[:], tmp[:]))
                link(V.tensor_tensor(flat(mem["dis_s"]), cum[:], flat(mem["has_s"]), ALU.mult))
                link(V.tensor_scalar(degm[:], flat(mem["deg"]), 1.0, None, ALU.max))
                link(V.tensor_scalar(tot[:], flat(mem["deg"]), 1.0, None, ALU.add))
                V.sem_inc(asked, 1)
                link(V.reciprocal(cum[:], degm[:]))
                link(V.tensor_tensor(flat(mem["inv"]), cum[:], flat(mem["has"]), ALU.mult))
                dve.wait_ge(rooted, 3)
                link(V.reciprocal(flat(mem["dis"]), tmp[:]))
                link(V.tensor_scalar(flat(mem["amp"]), tot[:], NSCALE / DELTA, None, ALU.mult))
                link(V.tensor_scalar(tot[:], tot[:], 0.5, None, ALU.max))
                link(V.reciprocal(cum[:], tot[:]))
                link(V.scalar_tensor_tensor(flat(mem["att"]), cum[:], DELTA * NSCALE, flat(mem["has"]), ALU.mult, ALU.mult))

            @block.tensor
            def _(pe):
                pe.wait_ge(ready, 1)
                for n in range(2):
                    nc.tensor.matmul(count[n][:, 0:TILES], zero[:, 0:P], hot_high[:, n, :],
                                     start=True, stop=False).then_inc(used, 1)
                with pe.Fori(0, TILES // HOTB) as i:
                    for j in range(HOTB):
                        for n in range(2):
                            pe.wait_ge(hot, i * (2 * HOTB) + (2 * j + n + 1))
                            nc.tensor.matmul(count[n][:, 0:TILES], hot_low[:, n, :], hot_high[:, n, :],
                                             start=False, stop=False).then_inc(used, 1)
                for n in range(2):
                    last = nc.tensor.matmul(count[n][:, 0:TILES], zero[:, 0:P], zero[:],
                                            start=False, stop=True)
                last.then_inc(counted, 1)
                for n in range(2):
                    pe.wait_ge(ready, 3 + n)
                    nc.tensor.matmul(before[:, 0:TILES], tri[:], deg[n][:], start=True, stop=True)
                    nc.tensor.matmul(total[:, 0:TILES], ones[:, 0:P], deg[n][:], start=True, stop=True).then_inc(summed, 1)

            @block.scalar
            def _(act):
                def store(t, link):
                    act.wait_ge(got_in[t.h], t.slot(16 * TB))
                    act.dma_start(mem["pay_sorted"][:, bass.ds(t.s * (TB * PAYW), TB * PAYW)],
                                  got[:, t.h].rearrange("p j c -> p (j c)")).then_inc(stored[t.h], 16)
                pipeline(act, None, [(0, store, 0)])
                act.wait_ge(asked, 1)
                nc.scalar.activation(tmp[:], degm[:], ACT.Sqrt).then_inc(rooted, 1)
                act.wait_ge(asked, 2)
                nc.scalar.activation(tmp[:], degm[:], ACT.Sqrt).then_inc(rooted, 1)
                nc.scalar.activation(tot[:], tot[:], ACT.Ln).then_inc(rooted, 1)
        stores_done(nc, sems, [(stored, 16)], 0)


class Norm:
    FIRST, SECOND = 5, 2

    def __init__(self, nc, sb, sems, name):
        self.nc = nc
        self.total, self.cent = sb(name + "_total", [P, WB]), sb(name + "_cent", [P, 2, WB, D])
        self.sq, self.ss = sb(name + "_sq", [P, WB, D]), sb(name + "_ss", [P, 2, WB])
        self.sd, self.rs = sb(name + "_sd", [P, 2, WB]), sb(name + "_rs", [P, WB])
        self.eps = sb(name + "_eps", [P, 1])
        self.asked, self.rooted = sems(name + "_asked"), sems(name + "_rooted")

    def first(self, link, t, x):
        V = self.nc.vector
        link(V.reduce_sum(self.total[:], x, axis=AX.X))
        link(V.tensor_scalar(self.total[:], self.total[:], -1.0 / D, None, ALU.mult))
        link(V.tensor_tensor(self.cent[:, t.h], x, per_tile(self.total[:]), ALU.add))
        link(V.tensor_tensor(self.sq[:], self.cent[:, t.h], self.cent[:, t.h], ALU.mult))
        link(V.reduce_sum(self.ss[:, t.h], self.sq[:], axis=AX.X))
        V.sem_inc(self.asked, 1)

    def scalar(self, act, t):
        act.wait_ge(self.asked, t.n())
        self.nc.scalar.activation(self.sd[:, t.h], self.ss[:, t.h], ACT.Sqrt, bias=self.eps[:],
                                  scale=1.0 / D).then_inc(self.rooted, 1)

    def second(self, dve, link, t, out):
        V = self.nc.vector
        dve.wait_ge(self.rooted, t.n())
        link(V.reciprocal(self.rs[:], self.sd[:, t.h]))
        link(V.scalar_tensor_tensor(out, self.cent[:, t.h], 0.0, per_tile(self.rs[:]), ALU.max, ALU.mult))


def per_tile(v):
    return v.unsqueeze(2).broadcast_to([P, v.shape[1], D])


def per_feature(v, n):
    return v.unsqueeze(1).broadcast_to([P, n, v.shape[1]])


def attention_tables(nc, mem, sems):
    io = mem["io"]
    with ExitStack() as ctx:
        sb = lambda n, s, dt=F32: ctx.enter_context(nc.sbuf_tensor("att_" + n, s, dt))
        pb = lambda n, s: ctx.enter_context(nc.psum_tensor("att_" + n, s, F32))
        x, h_ = sb("x", [P, 2, WPAIRS, 2, D]), sb("h", [P, 2, WPAIRS, 2 * D])
        w = sb("w", [P, 4 * D])
        bias, att = sb("bias", [P, 2 * D]), sb("att", [P, 2 * D])
        rows, prod = sb("rows", [P, 2, WB, 2 * D]), sb("prod", [P, WB, 2 * D])
        srow = sb("srow", [P, 2, WB, 2])
        norm = Norm(nc, sb, sems, "att_norm")
        turn = Turned(nc, sb, pb, sems, "att", 2 * D)
        loaded, x_in, x_used = sems("att_in"), sems.pair("att_x_in"), sems("att_x_used")
        rows_ready, stored = sems("att_rows_ready"), sems.pair("att_stored")
        with nc.Block() as block:
            @block.sync
            def _(sp):
                sp.dma_start(w[:], io["w_lin"]).then_inc(loaded, 16)
                sp.dma_start(bias[:], io["b_lin"]).then_inc(loaded, 16)
                sp.dma_start(att[:], io["att_own"]).then_inc(loaded, 16)

                def load_x(t, link):
                    sp.wait_ge(x_used, t.n())
                    for g in range(2):
                        sp.dma_start(x[:, t.h, :, g, :], node_rows(io["x"], g, t.s * WPAIRS)).then_inc(x_in[t.h], 16)
                node_pipeline(sp, None, [(0, load_x, 0)])

            @block.vector
            def _(dve):
                V = nc.vector
                dve.wait_ge(loaded, 48)
                link = Link(dve, sems("att_first"))
                link(V.memset(norm.eps[:], EPS))

                def center(t, link):
                    dve.wait_ge(x_in[t.h], t.slot(32))
                    norm.first(link, t, x[:, t.h].rearrange("p k g d -> p (k g) d"))
                    V.sem_inc(x_used, 1)

                def normed(t, link):
                    dve.wait_ge(turn.turned, t.n())
                    norm.second(dve, link, t, h_[:, t.h].rearrange("p k (g d) -> p (k g) d", g=2))
                    V.sem_inc(turn.ready, 1)

                def make_rows(t, link):
                    dve.wait_ge(turn.multiplied, t.n() + 2)
                    dve.wait_ge(stored[t.h], t.slot(64))
                    link(V.tensor_tensor(rows[:, t.h], turn.product(t.h), per_feature(bias[:], WB), ALU.add))
                    V.sem_inc(turn.used, 1)
                    link(V.tensor_tensor(prod[:], rows[:, t.h], per_feature(att[:], WB), ALU.mult))
                    link(V.reduce_sum(srow[:, t.h].rearrange("p n a -> p (n a)"),
                                      prod[:].rearrange("p n (a d) -> p (n a) d", a=2), axis=AX.X))
                    V.sem_inc(rows_ready, 1)
                node_pipeline(dve, sems("att_link"), [(0, center, Norm.FIRST), (1, normed, Norm.SECOND), (3, make_rows, 3)])

            @block.scalar
            def _(act):
                nc.scalar.preload_act_table(ACT.Sqrt)

                def store(t, link):
                    act.wait_ge(rows_ready, t.n())
                    store_rows(act, mem["att_table"], rows[:, t.h], t.s * WPAIRS, stored[t.h])
                    store_rows(act, mem["att_src"], srow[:, t.h], t.s * WPAIRS, stored[t.h])
                node_pipeline(act, None, [(0, lambda t, link: norm.scalar(act, t), 0),
                                     (1, lambda t, link: turn.scalar(act, t), 0), (3, store, 0)])

            @block.tensor
            def _(pe):
                pe.wait_ge(loaded, 48)
                node_pipeline(pe, None, [(1, lambda t, link: turn.turn(pe, t, h_, mem["ident"]), 0),
                                    (2, lambda t, link: turn.multiply(pe, t, w), 0)])
        stores_done(nc, sems, [(stored, 64)], 0, WSTEPS)


def attention_edges(nc, mem, sems):
    io = mem["io"]
    with ExitStack() as ctx:
        sb = lambda n, s, dt=F32: ctx.enter_context(nc.sbuf_tensor("ate_" + n, s, dt))
        pb = lambda n, s: ctx.enter_context(nc.psum_tensor("ate_" + n, s, F32))
        w_edge, att, sel = sb("w_edge", [6, 2 * D]), sb("att", [P, 2]), sb("sel", [2, P])
        index = sb("index", [P, 2, TB], I32)
        pay = sb("pay", [P, 2, TB, PAYW])
        mask = sb("mask", [2, 2, 2, EB], BF16)
        got, gots = sb("got", [P, 2, TB, 2 * D]), sb("gots", [P, 2, TB, 2])
        payT, xT = sb("payT", [PAYW, EB]), sb("xT", [P, 2, EB])
        score, lrel = sb("score", [2, EB]), sb("lrel", [2, EB])
        top = sb("top", [2, 2, EB + 1])
        down, diff = sb("down", [2, EB]), sb("diff", [2, EB])
        r0, r, p = sb("r0", [2, EB]), sb("r", [2, EB]), sb("p", [2, EB])
        px = sb("px", [P, EB])
        num, den = sb("num", [P, 2, EB]), sb("den", [2, 2, EB])
        out = sb("out", [P, 2, TB, S0W])
        psP, psX = pb("psP", [PAYW, EB]), pb("psX", [P, EB])
        psS = pb("psS", [2, EB])
        psR, psB = pb("psR", [P, EB]), pb("psB", [P, EB])
        psN, psD = pb("psN", [P, TB, 2 * D]), pb("psD", [P, TB, P])
        loaded = sems("ate_in")
        n_ = lambda name: sems("ate_" + name)
        index_in, pay_in, mask_in, got_in, stored = (sems.pair("ate_" + n) for n in
                                                     ("index_in", "pay_in", "mask_in", "got", "stored"))
        with nc.Block() as block:
            @block.sync
            def _(sp):
                sp.dma_start(w_edge[:], io["w_edge"]).then_inc(loaded, 16)
                sp.dma_start(att[:], io["att_other"]).then_inc(loaded, 16)
                sp.dma_start(sel[:], io["consts"][0:2, 3 * P:4 * P]).then_inc(loaded, 16)

                def loads(t, link):
                    if not t.first:
                        sp.wait_ge(got_in[t.h], t.slot(32 * TB) - 32 * TB)
                    sp.dma_start(index[:, t.h, :], mem["src_src"][:, bass.ds(t.s * TB, TB)]).then_inc(index_in[t.h], 16)
                    sp.wait_ge(n_("pay_turned"), t.n())
                    sp.dma_start(pay[:, t.h].rearrange("p j c -> p (j c)"),
                                 mem["pay_sorted"][:, bass.ds(t.s * (TB * PAYW), TB * PAYW)]).then_inc(pay_in[t.h], 16)

                def load_masks(t, link):
                    sp.wait_ge(n_("mask_used"), t.n())
                    for a in range(2):
                        sp.dma_start(mask[a:a + 1, t.h].rearrange("p a f -> p (a f)"),
                                     mem["mask_src"][bass.ds(t.s, 1), :]).then_inc(mask_in[t.h], 16)
                pipeline(sp, None, [(0, loads, 0), (1, load_masks, 0)], peel=2)

            @block.gpsimd
            def _(pool):
                def gather_rows(t, link):
                    pool.wait_ge(index_in[t.h], t.slot())
                    pool.wait_ge(pay_in[t.h], t.slot())
                    pool.wait_ge(n_("x_summed"), t.n())
                    passed(pool, sems)
                    for j in range(TB):
                        gather(pool, got[:, t.h, j, :], mem["att_table"],
                               pay[:, t.h, j, PAYW - 1:PAYW].bitcast(I32)).then_inc(got_in[t.h], 16)
                    pool.wait_ge(n_("scored"), t.n())
                    passed(pool, sems)
                    for j in range(TB):
                        gather(pool, gots[:, t.h, j, :], mem["att_src"], index[:, t.h, j:j + 1]).then_inc(got_in[t.h], 16)
                pipeline(pool, None, [(0, gather_rows, 0)])

            @block.tensor
            def _(pe):
                ident = mem["ident"]
                pe.wait_ge(loaded, 48)

                def turn_pay(t, link):
                    pe.wait_ge(pay_in[t.h], t.slot())
                    pe.wait_ge(n_("payT"), t.n())
                    for j in range(TB):
                        last = nc.tensor.transpose(psP[:, j * P:(j + 1) * P], pay[:, t.h, j, :], ident[:])
                    last.then_inc(n_("pay_turned"), 1)

                def turn_back(t, link):
                    pe.wait_ge(n_("num"), t.n() + 2)
                    pe.wait_ge(n_("out"), t.n(2))
                    for j in range(TB):
                        nc.tensor.transpose(psN[:, j, :], num[:, t.h, j * P:(j + 1) * P], ident[:])
                        last = nc.tensor.transpose(psD[:, j, 0:2], den[:, t.h, j * P:(j + 1) * P], ident[0:2, 0:2])
                    last.then_inc(n_("back"), 1)

                def messages(t, link):
                    pe.wait_ge(n_("payT"), t.n() + 1)
                    pe.wait_ge(got_in[t.h], t.slot(32 * TB))
                    pe.wait_ge(n_("xT"), t.n())
                    for j in range(TB):
                        nc.tensor.matmul(psX[:, j * P:(j + 1) * P], got[:, t.h, j, :], ident[:], start=True, stop=False)
                        last = nc.tensor.matmul(psX[:, j * P:(j + 1) * P], w_edge[:], payT[0:6, j * P:(j + 1) * P],
                                                start=False, stop=True)
                    last.then_inc(n_("x_summed"), 1)

                def scores(t, link):
                    pe.wait_ge(n_("xT"), t.n() + 1)
                    pe.wait_ge(n_("score"), t.n())
                    for j in range(TB):
                        nc.tensor.matmul(psS[:, j * P:(j + 1) * P], gots[:, t.h, j, :], ident[:], start=True, stop=False)
                        last = nc.tensor.matmul(psS[:, j * P:(j + 1) * P], att[:], xT[:, t.h, j * P:(j + 1) * P],
                                                start=False, stop=True)
                    last.then_inc(n_("scored"), 1)

                def spread(t, link):
                    pe.wait_ge(n_("p"), t.n())
                    pe.wait_ge(n_("px"), t.n() + 1)
                    nc.tensor.matmul(psB[:], sel[:], p[:], start=True, stop=True).then_inc(n_("p_spread"), 1)
                    pe.wait_ge(n_("r"), t.n())
                    pe.wait_ge(n_("num"), t.n() + 1)
                    nc.tensor.matmul(psR[:], sel[:], r[:], start=True, stop=True).then_inc(n_("r_spread"), 1)
                pipeline(pe, None, [(0, turn_pay, 0), (3, turn_back, 0), (0, messages, 0), (0, scores, 0), (1, spread, 0)])

            @block.scalar
            def _(act):
                S = nc.scalar
                S.preload_act_table(ACT.Exp)

                def copy_messages(t, link):
                    act.wait_ge(n_("pay_turned"), t.n() + 2)
                    act.wait_ge(n_("x_summed"), t.n() + 1)
                    S.copy(payT[:], psP[:]).then_inc(n_("payT"), 1)
                    act.wait_ge(n_("x_summed"), t.n() + 2)
                    act.wait_ge(n_("px"), t.n())
                    S.copy(xT[:, t.h, :], psX[:]).then_inc(n_("xT"), 1)

                def store(t, link):
                    act.wait_ge(n_("back"), t.n() + 2)
                    act.wait_ge(stored[t.h], t.slot())
                    S.copy(out[:, t.h, :, 0:2 * D], psN[:]).then_inc(n_("out"), 1)
                    S.copy(out[:, t.h, :, 2 * D:S0W], psD[:, :, 0:2]).then_inc(n_("out"), 1)
                    act.wait_ge(n_("out"), t.n(2) + 2)
                    act.dma_start(mem["att_scan"][0:ROWS, :].rearrange("(t p) c -> p t c", p=P)[:, bass.ds(t.s * TB, TB), :],
                                  out[:, t.h]).then_inc(stored[t.h], 16)

                def exponents(t, link):
                    act.wait_ge(n_("diff"), t.n())
                    act.wait_ge(n_("p_spread"), t.n())
                    S.activation(p[:], diff[:], ACT.Exp).then_inc(n_("p"), 1)
                    act.wait_ge(n_("down"), t.n())
                    S.activation(r0[:], down[:], ACT.Exp).then_inc(n_("r0"), 1)

                def copy_scores(t, link):
                    act.wait_ge(n_("scored"), t.n() + 2)
                    act.wait_ge(n_("score_used"), t.n())
                    S.copy(score[:], psS[:]).then_inc(n_("score"), 1)
                pipeline(act, None, [(0, copy_messages, 0), (3, store, 0), (1, exponents, 0), (0, copy_scores, 0)])

            @block.vector
            def _(dve):
                V = nc.vector
                first = Link(dve, sems("ate_first"))
                first(V.memset(top[:], 0.0))
                first(V.memset(num[:], 0.0))
                first(V.memset(den[:], 0.0))
                passed(dve, sems)

                def weigh(t, link):
                    h = t.h
                    dve.wait_ge(n_("score"), t.n() + 1)
                    dve.wait_ge(mask_in[h], t.slot(32))
                    link(V.scalar_tensor_tensor(lrel[:], score[:], 0.2, score[:], ALU.mult, ALU.max))
                    V.sem_inc(n_("score_used"), 1)
                    link(V.tensor_copy(top[:, h, 0:1], top[:, 1 - h, EB:EB + 1]))
                    link(V.tensor_tensor_scan(top[:, h, 1:EB + 1], mask[:, h, 1, :], lrel[:], top[:, h, 0:1], ALU.add, ALU.max))
                    V.tensor_tensor(diff[:], lrel[:], top[:, h, 1:EB + 1], ALU.subtract).then_inc(n_("diff"), 1)
                    link(V.tensor_tensor(down[:], top[:, h, 0:EB], top[:, h, 1:EB + 1], ALU.subtract))
                    link(V.tensor_scalar(down[:], down[:], 0.0, None, ALU.min))
                    V.sem_inc(n_("down"), 1)
                    dve.wait_ge(n_("r0"), t.n())
                    dve.wait_ge(n_("r_spread"), t.n())
                    link(V.tensor_tensor(r[:], r0[:], mask[:, h, 0, :], ALU.mult))
                    V.sem_inc(n_("r"), 1)
                    dve.wait_ge(n_("p"), t.n())
                    dve.wait_ge(n_("back"), t.n())
                    link(V.tensor_tensor_scan(den[:, h, :], r[:], p[:], den[:, 1 - h, EB - 1:EB], ALU.mult, ALU.add))
                    V.sem_inc(n_("mask_used"), 1)

                def sum_up(t, link):
                    h = t.h
                    dve.wait_ge(n_("p_spread"), t.n() + 1)
                    link(V.tensor_tensor(px[:], psB[:], xT[:, h, :], ALU.mult))
                    V.sem_inc(n_("px"), 1)
                    dve.wait_ge(n_("r_spread"), t.n() + 1)
                    dve.wait_ge(n_("back"), t.n())
                    link(V.tensor_tensor_scan(num[:, h, :], psR[:], px[:], num[:, 1 - h, EB - 1:EB], ALU.mult, ALU.add))
                    V.sem_inc(n_("num"), 1)
                pipeline(dve, sems("ate_link"), [(2, sum_up, 2), (1, weigh, 7)])
        stores_done(nc, sems, [(stored, 16)], 0)


class Turned:

    def __init__(self, nc, sb, pb, sems, name, width=D):
        self.nc, self.width = nc, width
        self.hT = sb(name + "_hT", [P, 2, WPAIRS * P])
        self.psT = pb(name + "_psT", [P, 2, 512])
        self.psR = pb(name + "_psR", [P, 2, max(512, WB * width)])
        self.ready, self.turned, self.copied, self.multiplied, self.used = (
            sems(name + "_" + n) for n in ("ready", "turned", "copied", "multiplied", "used"))

    def product(self, h):
        return self.psR[:, h, 0:WB * self.width].rearrange("p (n c) -> p n c", n=WB)

    def turn(self, pe, t, tiles, ident):
        pe.wait_ge(self.ready, t.n())
        pe.wait_ge(self.copied, t.n())
        for k in range(WPAIRS):
            last = self.nc.tensor.transpose(self.psT[:, t.h, k * P:(k + 1) * P], tiles[:, t.h, k, :], ident[:])
        last.then_inc(self.turned, 1)

    def scalar(self, act, t):
        act.wait_ge(self.turned, t.n() + 2)
        act.wait_ge(self.multiplied, t.n())
        self.nc.scalar.copy(self.hT[:, t.h], self.psT[:, t.h, 0:WPAIRS * P]).then_inc(self.copied, 1)

    def multiply(self, pe, t, w):
        pe.wait_ge(self.copied, t.n() + 2)
        pe.wait_ge(self.used, t.n())
        for k in range(WPAIRS):
            last = self.nc.tensor.matmul(self.psR[:, t.h, k * 2 * self.width:(k + 1) * 2 * self.width],
                                         self.hT[:, t.h, k * P:(k + 1) * P], w[:], start=True, stop=True)
        last.then_inc(self.multiplied, 1)


def index_loads(nc, sp, mem, sems, name, t, index, ends, pairs):
    if not t.first:
        sp.wait_ge(sems.pair(name + "_got")[t.h], t.slot(32 * pairs) - 32 * pairs)
    sp.dma_start(index[:, t.h], mem[ends][:, bass.ds(t.s * pairs, pairs), :]).then_inc(sems.pair(name + "_index_in")[t.h], 16)


def gathers(nc, pool, sems, name, t, got, table, index):
    pool.wait_ge(sems.pair(name + "_index_in")[t.h], t.slot())
    pool.wait_ge(sems(name + "_got_used"), t.n())
    passed(pool, sems)
    for n in range(index.shape[1]):
        gather(pool, got[:, t.h, n, :], table, index[:, n]).then_inc(sems.pair(name + "_got")[t.h], 16)


def store_rows(act, table, rows, q, sem, pairs=WPAIRS):
    for g in range(2):
        act.dma_start(node_rows(table, g, q, pairs), rows.rearrange("p (k g) c -> p k g c", g=2)[:, :, g, :]).then_inc(sem, 16)


def attention_nodes(nc, mem, sems):
    io = mem["io"]
    with ExitStack() as ctx:
        sb = lambda n, s, dt=F32: ctx.enter_context(nc.sbuf_tensor("atn_" + n, s, dt))
        pb = lambda n, s: ctx.enter_context(nc.psum_tensor("atn_" + n, s, F32))
        index, got = sb("index", [P, 2, WB], I32), sb("got", [P, 2, WB, S0W])
        x, x1, h_ = sb("x", [P, 2, WPAIRS, 2, D]), sb("x1", [P, 2, WB, D]), sb("h", [P, 2, WPAIRS, 2 * D])
        half_has, dens = sb("half_has", [P, HALF, 2]), sb("dens", [P, WB, 2])
        heads, both = sb("heads", [P, WB, 2, D]), sb("both", [P, WB, D])
        w, bias = sb("w", [P, 2 * D]), sb("bias", [P, D])
        rows = sb("msg_rows", [P, 2, WB, D])
        norm = Norm(nc, sb, sems, "atn_norm")
        turn = Turned(nc, sb, pb, sems, "atn")
        loaded, x_in, got_in = sems("atn_in"), sems.pair("atn_x_in"), sems.pair("atn_got")
        x1_stored, hT_stored, rows_stored = sems.pair("atn_x1_stored"), sems.pair("atn_hT_stored"), sems.pair("atn_rows_stored")
        x1_ready, used = sems("atn_x1_ready"), sems("atn_got_used")
        with nc.Block() as block:
            @block.sync
            def _(sp):
                sp.dma_start(w[:], io["w_top"][0]).then_inc(loaded, 16)
                sp.dma_start(bias[:], io["att_bias"]).then_inc(loaded, 16)

                def loads(t, link):
                    index_loads(nc, sp, mem, sems, "atn", t, index[:].rearrange("p h (k g) -> p h k g", g=2), "end_src", WPAIRS)
                    sp.wait_ge(used, t.n())
                    for g in range(2):
                        sp.dma_start(x[:, t.h, :, g, :], node_rows(io["x"], g, t.s * WPAIRS)).then_inc(x_in[t.h], 16)
                node_pipeline(sp, None, [(0, loads, 0)], peel=2)

            @block.gpsimd
            def _(pool):
                node_pipeline(pool, None, [(0, lambda t, link: gathers(
                    nc, pool, sems, "atn", t, got, mem["att_scan"], index[:, t.h].rearrange("p (n o) -> p n o", o=1)), 0)])

            @block.vector
            def _(dve):
                V = nc.vector
                dve.wait_ge(loaded, 32)
                first = Link(dve, sems("atn_first"))
                first(V.memset(norm.eps[:], EPS))
                first(V.tensor_scalar(half_has[:], mem["has_s"][:], 0.5, None, ALU.mult))
                passed(dve, sems)

                def sum_heads(t, link):
                    own = half_has[:, bass.ds(t.s * WPAIRS, WPAIRS), :].rearrange("p k g -> p (k g)")
                    dve.wait_ge(got_in[t.h], t.slot(16 * WB))
                    dve.wait_ge(x_in[t.h], t.slot(32))
                    dve.wait_ge(x1_stored[t.h], t.slot(32))
                    link(V.tensor_scalar(dens[:], got[:, t.h, :, 2 * D:S0W], 1e-16, None, ALU.add))
                    link(V.reciprocal(dens[:], dens[:]))
                    link(V.tensor_tensor(dens[:], dens[:], own.unsqueeze(2).broadcast_to([P, WB, 2]), ALU.mult))
                    link(V.tensor_tensor(heads[:], got[:, t.h, :, 0:2 * D].rearrange("p n (a d) -> p n a d", a=2),
                                         dens[:].unsqueeze(3).broadcast_to([P, WB, 2, D]), ALU.mult))
                    link(V.tensor_tensor(both[:], heads[:, :, 0, :], heads[:, :, 1, :], ALU.add))
                    link(V.tensor_tensor(both[:], both[:], per_feature(bias[:], WB), ALU.add))
                    link(V.tensor_tensor(x1[:, t.h], both[:], x[:, t.h].rearrange("p k g d -> p (k g) d"), ALU.add))
                    V.sem_inc(used, 1)
                    V.sem_inc(x1_ready, 1)
                    norm.first(link, t, x1[:, t.h])

                def normed(t, link):
                    dve.wait_ge(turn.turned, t.n())
                    norm.second(dve, link, t, h_[:, t.h].rearrange("p k (g d) -> p (k g) d", g=2))
                    V.sem_inc(turn.ready, 1)
                node_pipeline(dve, sems("atn_link"), [(0, sum_heads, 7 + Norm.FIRST), (1, normed, Norm.SECOND)])

            @block.scalar
            def _(act):
                nc.scalar.preload_act_table(ACT.Sqrt)

                def store_x1(t, link):
                    act.wait_ge(x1_ready, t.n())
                    store_rows(act, mem["x1"], x1[:, t.h], t.s * WPAIRS, x1_stored[t.h])

                def keep_h(t, link):
                    act.wait_ge(hT_stored[t.h], t.slot())
                    turn.scalar(act, t)
                    act.wait_ge(turn.copied, t.n() + 2)
                    act.dma_start(mem["hT"][:, bass.ds(t.s * (WPAIRS * P), WPAIRS * P)], turn.hT[:, t.h]).then_inc(hT_stored[t.h], 16)

                def keep_rows(t, link):
                    act.wait_ge(turn.multiplied, t.n() + 2)
                    act.wait_ge(rows_stored[t.h], t.slot(32))
                    nc.scalar.copy(rows[:, t.h], turn.product(t.h)).then_inc(turn.used, 1)
                    act.wait_ge(turn.used, t.n() + 2)
                    store_rows(act, mem["msg_table"], rows[:, t.h], t.s * WPAIRS, rows_stored[t.h])
                node_pipeline(act, None, [(0, store_x1, 0), (0, lambda t, link: norm.scalar(act, t), 0), (1, keep_h, 0),
                                     (3, keep_rows, 0)])

            @block.tensor
            def _(pe):
                pe.wait_ge(loaded, 32)
                node_pipeline(pe, None, [(1, lambda t, link: turn.turn(pe, t, h_, mem["ident"]), 0),
                                    (2, lambda t, link: turn.multiply(pe, t, w), 0)])
        stores_done(nc, sems, [(x1_stored, 32), (hT_stored, 16), (rows_stored, 32)], 0, WSTEPS)


def pna_edges(nc, mem, sems, rep):
    with ExitStack() as ctx:
        sb = lambda n, s, dt=F32: ctx.enter_context(nc.sbuf_tensor("pne_" + n, s, dt))
        pb = lambda n, s: ctx.enter_context(nc.psum_tensor("pne_" + n, s, F32))
        index, mask = sb("index", [P, 2, TB], I32), sb("mask", [P, 2, 2, EB], BF16)
        z = sb("z", [P, 2, TB, 3 * D])
        sums, tops = sb("sums", [P, 2, EB]), sb("tops", [P, 2, EB])
        out = sb("out", [P, 2, TB, 4 * D])
        psS, psM = pb("psS", [P, 2, EB]), pb("psM", [P, 2, EB])
        psB = pb("psB", [P, 2, TB, 2 * D])
        n_ = lambda name: sems("pne_" + name)
        index_in, mask_in, got_in, stored = (sems.pair("pne_" + n) for n in ("index_in", "mask_in", "got", "stored"))
        ident = mem["ident"]
        with nc.Block() as block:
            @block.sync
            def _(sp):
                def loads(t, link):
                    if not t.first:
                        sp.wait_ge(got_in[t.h], t.slot(16 * TB) - 16 * TB)
                    sp.dma_start(index[:, t.h, :], mem["dst_src"][:, bass.ds(t.s * TB, TB)]).then_inc(index_in[t.h], 16)

                def load_masks(t, link):
                    sp.wait_ge(n_("scanned"), t.n())
                    sp.dma_start(mask[:, t.h].rearrange("p a f -> p (a f)"),
                                 mem["mask_dst"][bass.ds(t.s, 1), :].broadcast_to([P, 2 * EB])).then_inc(mask_in[t.h], 16)
                pipeline(sp, None, [(0, loads, 0), (1, load_masks, 0)], rep, peel=2)

            @block.gpsimd
            def _(pool):
                def gathers_a(t, link):
                    pool.wait_ge(index_in[t.h], t.slot())
                    pool.wait_ge(n_("turned"), t.n())
                    passed(pool, sems)
                    for j in range(TB):
                        gather(pool, z[:, t.h, j, D:2 * D], mem["msg_table"], index[:, t.h, j:j + 1]).then_inc(got_in[t.h], 16)
                pipeline(pool, None, [(0, gathers_a, 0)], rep)

            @block.tensor
            def _(pe):
                def turn(t, link):
                    pe.wait_ge(n_("squared"), t.n())
                    pe.wait_ge(n_("negated"), t.n())
                    pe.wait_ge(n_("scanned"), t.n())
                    for j in range(TB):
                        nc.tensor.transpose(psS[:, t.h, j * P:(j + 1) * P], z[:, t.h, j, 0:2 * D], ident[:])
                        last = nc.tensor.transpose(psM[:, t.h, j * P:(j + 1) * P], z[:, t.h, j, D:3 * D], ident[:])
                    last.then_inc(n_("turned"), 1)

                def turn_back(t, link):
                    pe.wait_ge(n_("scanned"), t.n() + 2)
                    for b, scans in enumerate((sums, tops)):
                        pe.wait_ge(n_("copied"), t.n(2) + (b - 1))
                        for j in range(TB):
                            last = nc.tensor.transpose(psB[:, b, j, :], scans[:, t.h, j * P:(j + 1) * P], ident[:])
                        last.then_inc(n_("back"), 1)
                pipeline(pe, None, [(0, turn, 0), (1, turn_back, 0)], rep)

            @block.scalar
            def _(act):
                S = nc.scalar
                S.preload_act_table(ACT.Square)

                def square(t, link):
                    act.wait_ge(got_in[t.h], t.slot(16 * TB))
                    S.activation(z[:, t.h, :, 0:D], z[:, t.h, :, D:2 * D], ACT.Square).then_inc(n_("squared"), 1)

                def store(t, link):
                    act.wait_ge(stored[t.h], t.slot())
                    for b in range(2):
                        act.wait_ge(n_("back"), t.n(2) + (b - 1))
                        S.copy(out[:, t.h, :, b * 2 * D:(b + 1) * 2 * D], psB[:, b]).then_inc(n_("copied"), 1)
                    act.wait_ge(n_("copied"), t.n(2) + 2)
                    act.dma_start(mem["pna_scan"][0:ROWS, :].rearrange("(t p) c -> p t c", p=P)[:, bass.ds(t.s * TB, TB), :],
                                  out[:, t.h]).then_inc(stored[t.h], 16)
                pipeline(act, None, [(0, square, 0), (2, store, 0)], rep)

            @block.vector
            def _(dve):
                V = nc.vector
                first = Link(dve, sems("pne_first"), rep * 2)
                first(V.memset(sums[:], 0.0))
                first(V.memset(tops[:], 0.0))
                passed(dve, sems)

                def negate(t, link):
                    dve.wait_ge(got_in[t.h], t.slot(16 * TB))
                    V.tensor_scalar(z[:, t.h, :, 2 * D:3 * D], z[:, t.h, :, D:2 * D], -1.0, None, ALU.mult).then_inc(n_("negated"), 1)

                def scan(t, link):
                    dve.wait_ge(n_("turned"), t.n() + 2)
                    dve.wait_ge(mask_in[t.h], t.slot())
                    V.tensor_tensor_scan(sums[:, t.h, :], mask[:, t.h, 0, :], psS[:, t.h, :], sums[:, 1 - t.h, EB - 1:EB],
                                         ALU.mult, ALU.add)
                    link(V.tensor_tensor_scan(tops[:, t.h, :], mask[:, t.h, 1, :], psM[:, t.h, :], tops[:, 1 - t.h, EB - 1:EB],
                                              ALU.add, ALU.max))
                    V.sem_inc(n_("scanned"), 1)
                pipeline(dve, sems("pne_link"), [(0, negate, 0), (1, scan, 1)], rep)
        stores_done(nc, sems, [(stored, 16)], rep)


def stores_done(nc, sems, which, rep, steps=STEPS):
    with nc.Block() as block:
        @block.sync
        def _(sp):
            for pair, k in which:
                for h, s in enumerate(pair):
                    sp.wait_ge(s, rep * (steps // 2 * k) + ((steps + 1 - h) // 2 + 1) * k)
            passed(sp, sems)


def pna_nodes(nc, mem, sems, rep):
    io = mem["io"]
    W = 3 * D
    with ExitStack() as ctx:
        sb = lambda n, s, dt=F32: ctx.enter_context(nc.sbuf_tensor("pnn_" + n, s, dt))
        pb = lambda n, s: ctx.enter_context(nc.psum_tensor("pnn_" + n, s, F32))
        index, got = sb("index", [P, 2, TB], I32), sb("got", [P, 2, TB, 4 * D])
        hT, hT2 = sb("hT", [P, 2, PAIRS * P]), sb("hT2", [P, 2, PAIRS * P])
        w_bot, w_own, w_agg = sb("w_bot", [P, 2 * D]), sb("w_own", [P, 2 * D]), sb("w_agg", [P, 3, W])
        bM, bU, tiny = sb("bM", [P, D]), sb("bU", [P, 1]), sb("tiny", [P, 1])
        mq, m2 = sb("mq", [P, TB, 2 * D]), sb("m2", [P, TB, D])
        base = sb("base", [P, TB, D])
        agg = sb("agg", [P, 2, TB, 6 * D])
        aggT = sb("aggT", [P, 2, 3, TB * P])
        u0, u1, u2 = sb("u0", [P, TB, D]), sb("u1", [P, TB, D]), sb("u2", [P, 2, PAIRS, 2 * D])
        psO, psU = pb("psO", [P, 512]), pb("psU", [P, 512])
        psT = pb("psT", [P, 2, 512])
        psH = pb("psH", [P, 2, TB, 256])
        n_ = lambda name: sems("pnn_" + name)
        loaded, got_in, hT_in, hT2_in = n_("in"), sems.pair("pnn_got"), sems.pair("pnn_hT_in"), sems.pair("pnn_hT2_in")
        ident, U = mem["ident"], mem["U"]
        agg_of = lambda t, a: agg[:, t.h, :, a * D:(a + 1) * D]
        with nc.Block() as block:
            @block.sync
            def _(sp):
                lay = lambda a: a[bass.ds(rep, 1)].rearrange("o p c -> p (o c)")
                sp.dma_start(w_bot[:], lay(io["w_bot"])).then_inc(loaded, 16)
                sp.dma_start(w_own[:], lay(io["w_own"])).then_inc(loaded, 16)
                sp.dma_start(w_agg[:].rearrange("p c w -> p (c w)"), lay(io["w_agg"])).then_inc(loaded, 16)
                sp.dma_start(bM[:], lay(io["bM"])).then_inc(loaded, 16)
                sp.dma_start(bU[:], lay(io["bU"])).then_inc(loaded, 16)

                def loads(t, link):
                    index_loads(nc, sp, mem, sems, "pnn", t, index[:].rearrange("p h (k g) -> p h k g", g=2), "end_dst", PAIRS)
                    sp.wait_ge(n_("own"), t.n())
                    sp.dma_start(hT[:, t.h], mem["hT"][:, bass.ds(t.s * (PAIRS * P), PAIRS * P)]).then_inc(hT_in[t.h], 16)

                def load_again(t, link):
                    sp.wait_ge(n_("multiplied"), t.n())
                    sp.dma_start(hT2[:, t.h], mem["hT"][:, bass.ds(t.s * (PAIRS * P), PAIRS * P)]).then_inc(hT2_in[t.h], 16)
                pipeline(sp, None, [(0, loads, 0), (2, load_again, 0)], rep)

            @block.gpsimd
            def _(pool):
                def gather_scans(t, link):
                    gathers(nc, pool, sems, "pnn", t, got, mem["pna_scan"], index[:, t.h].rearrange("p (n o) -> p n o", o=1))
                pipeline(pool, None, [(0, gather_scans, 0)], rep)

            @block.vector
            def _(dve):
                V = nc.vector
                dve.wait_ge(loaded, rep * 80 + 80)
                first = Link(dve, n_("first"), rep * 2)
                first(V.memset(tiny[:], 1e-30))
                first(V.tensor_scalar(bU[:], bU[:], NSCALE, None, ALU.mult))
                V.sem_inc(n_("scaled"), 1)
                passed(dve, sems)

                def own(t, name, w=D):
                    return mem[name][:, bass.ds(t.s * PAIRS, PAIRS), :].rearrange("p k g -> p (k g)").unsqueeze(2).broadcast_to([P, TB, w])

                def aggregate(t, link):
                    dve.wait_ge(got_in[t.h], t.slot(16 * TB))
                    dve.wait_ge(n_("agg_turned"), t.n(3))
                    moments = link.put(V.tensor_tensor(mq[:], got[:, t.h, :, 0:2 * D], own(t, "inv", 2 * D), ALU.mult))
                    dve.wait_ge(n_("own"), t.n() + 2)
                    biased = link.put(V.tensor_tensor(base[:], psO[:, 0:TB * D].rearrange("p (n d) -> p n d", d=D),
                                                      per_feature(bM[:], TB), ALU.add))
                    link.on(moments)
                    squared = link.put(V.tensor_tensor(m2[:], mq[:, :, D:2 * D], mq[:, :, D:2 * D], ALU.mult))
                    link.on(biased)
                    V.sem_inc(n_("own_used"), 1)
                    owned = link.put(V.tensor_tensor(base[:], base[:], own(t, "has"), ALU.mult))
                    link.on(squared)
                    spread = link.put(V.tensor_tensor(m2[:], mq[:, :, 0:D], m2[:], ALU.subtract))
                    link.on(owned)
                    mean = link.put(V.tensor_tensor(agg_of(t, 0), mq[:, :, D:2 * D], base[:], ALU.add))
                    link.on(spread)
                    V.tensor_scalar(agg_of(t, 4), m2[:], 0.0, None, ALU.max).then_inc(n_("var"), 1)
                    link.on(mean)
                    V.tensor_tensor(agg_of(t, 5), agg_of(t, 0), own(t, "deg"), ALU.mult)
                    V.tensor_tensor(agg_of(t, 1), got[:, t.h, :, 2 * D:3 * D], base[:], ALU.add)
                    link(V.tensor_tensor(agg_of(t, 2), base[:], got[:, t.h, :, 3 * D:4 * D], ALU.subtract))
                    V.sem_inc(n_("agg"), 1)
                    V.sem_inc(n_("got_used"), 1)

                def combine(t, link):
                    dve.wait_ge(n_("multiplied"), t.n() + 2)
                    dve.wait_ge(n_("u_turned"), t.n())
                    amped = link.put(V.tensor_tensor(u0[:], psH[:, t.h, :, D:2 * D], own(t, "amp"), ALU.mult))
                    V.tensor_tensor(u1[:], psH[:, t.h, :, 2 * D:3 * D], own(t, "att"), ALU.mult)
                    link.on(amped)
                    link(V.scalar_tensor_tensor(u0[:], psH[:, t.h, :, 0:D], NSCALE, u0[:], ALU.mult, ALU.add))
                    V.sem_inc(n_("product_used"), 1)
                    link(V.tensor_tensor(u2[:, t.h].rearrange("p k (g d) -> p (k g) d", g=2), u0[:], u1[:], ALU.add))
                    V.sem_inc(n_("u"), 1)
                pipeline(dve, n_("link"), [(3, combine, 3), (0, aggregate, 7)], rep)

            @block.scalar
            def _(act):
                nc.scalar.preload_act_table(ACT.Sqrt)
                act.wait_ge(n_("scaled"), rep + 1)
                passed(act, sems)

                def root(t, link):
                    act.wait_ge(n_("var"), t.n())
                    nc.scalar.activation(agg_of(t, 3), agg_of(t, 4), ACT.Sqrt, bias=tiny[:]).then_inc(n_("std"), 1)

                def copy_agg(t, link):
                    act.wait_ge(n_("multiplied"), t.n())
                    for c in range(3):
                        act.wait_ge(n_("agg_turned"), t.n(3) + (c + 4))
                        nc.scalar.copy(aggT[:, t.h, c, :], psT[:, (t.h + c) % 2, :]).then_inc(n_("aggT"), 1)

                def keep_u(t, link):
                    act.wait_ge(n_("u_turned"), t.n() + 2)
                    passed(act, sems)
                    nc.scalar.activation(U[:, bass.ds(t.s * (PAIRS * P), PAIRS * P)], psU[:, 0:PAIRS * P],
                                         ACT.Identity, bias=bU[:]).then_inc(n_("u_kept"), 1)
                pipeline(act, None, [(1, copy_agg, 0), (0, root, 0), (4, keep_u, 0)], rep)

            @block.tensor
            def _(pe):
                pe.wait_ge(loaded, rep * 80 + 80)
                passed(pe, sems)

                def multiply_own(t, link):
                    pe.wait_ge(hT_in[t.h], t.slot())
                    pe.wait_ge(n_("own_used"), t.n())
                    for k in range(PAIRS):
                        last = nc.tensor.matmul(psO[:, k * 2 * D:(k + 1) * 2 * D], hT[:, t.h, k * P:(k + 1) * P], w_bot[:],
                                                start=True, stop=True)
                    last.then_inc(n_("own"), 1)

                def turn_agg(t, link):
                    pe.wait_ge(n_("agg"), t.n())
                    pe.wait_ge(n_("std"), t.n())
                    for c in range(3):
                        pe.wait_ge(n_("aggT"), t.n(3) + (c - 1))
                        for n in range(TB):
                            last = nc.tensor.transpose(psT[:, (t.h + c) % 2, n * P:(n + 1) * P], agg[:, t.h, n, c * P:(c + 1) * P], ident[:])
                        last.then_inc(n_("agg_turned"), 1)

                def multiply(t, link):
                    pe.wait_ge(n_("aggT"), t.n(3) + 3)
                    pe.wait_ge(hT2_in[t.h], t.slot())
                    pe.wait_ge(n_("product_used"), t.n())
                    for n in range(TB):
                        k, g = n // 2, n % 2
                        for c in range(3):
                            last = nc.tensor.matmul(psH[:, t.h, n, 0:W], aggT[:, t.h, c, n * P:(n + 1) * P], w_agg[:, c, :],
                                                    start=(c == 0), stop=(c == 2))
                            if c == 0:
                                nc.tensor.matmul(psH[:, t.h, n, 0:D], hT2[:, t.h, k * P:(k + 1) * P], w_own[:, g * D:(g + 1) * D],
                                                 start=False, stop=False)
                    last.then_inc(n_("multiplied"), 1)

                def turn_u(t, link):
                    pe.wait_ge(n_("u"), t.n())
                    pe.wait_ge(n_("u_kept"), t.n())
                    for k in range(PAIRS):
                        last = nc.tensor.transpose(psU[:, k * P:(k + 1) * P], u2[:, t.h, k, :], ident[:])
                    last.then_inc(n_("u_turned"), 1)
                pipeline(pe, None, [(0, multiply_own, 0), (1, turn_agg, 0), (2, multiply, 0), (4, turn_u, 0)], rep)


def feature_stats(nc, mem, sems, rep, name, sb, pb, gamma, beta):
    U = mem["U"]
    stats, rest = sb("stats", [P, STATN, 6]), sb("rest", [P, 6])
    mv, mvr = sb("mv", [P, 2]), sb("mvr", [P, 2])
    raw, rawr = sb("raw", [P, 2]), sb("rawr", [P, 2])
    mean, var, sd = sb("mean", [P, 2]), sb("var", [P, 1]), sb("sd", [P, 1])
    scale, shift, eps = sb("scale", [P, 1]), sb("shift", [P, 1]), sb("eps", [P, 1])
    psF = pb("psF", [P, 512])
    loaded, summed, folded, asked, rooted = (sems(name + "_" + n) for n in ("in", "summed", "folded", "asked", "rooted"))
    with nc.Block() as block:
        @block.vector
        def _(dve):
            V = nc.vector
            dve.wait_ge(loaded, rep * 32 + 32)
            passed(dve, sems)
            counted = sems(name + "_counted")
            with dve.Fori(0, STATN // STATB) as i:
                for j in range(STATB):
                    V.bn_stats(stats[:, bass.ds(i * STATB + j, 1), :].rearrange("p o c -> p (o c)"),
                               U[:, bass.ds((i * STATB + j) * STATF, STATF)]).then_inc(counted, 1)
            V.bn_stats(rest[0:D, :], U[0:D, G1COLS:COLS]).then_inc(counted, 1)
            dve.wait_ge(counted, rep * (STATN + 1) + STATN + 1)
            link = Link(dve, sems(name + "_link"), rep * 21)
            link(V.memset(eps[:], EPS))
            passed(dve, sems)
            link(V.bn_aggr(mv[:], stats[:]))
            link(V.memset(mvr[:], 0.0))
            passed(dve, sems)
            link(V.bn_aggr(mvr[0:D, :], rest[0:D, :].unsqueeze(1)))
            for (m, r, n) in ((mv, raw, G1COLS), (mvr, rawr, COLS - G1COLS)):
                link(V.tensor_tensor(r[:, 1:2], m[:, 0:1], m[:, 0:1], ALU.mult))
                link(V.tensor_tensor(r[:, 1:2], r[:, 1:2], m[:, 1:2], ALU.add))
                link(V.tensor_scalar(r[:, 1:2], r[:, 1:2], float(n), None, ALU.mult))
                link(V.tensor_scalar(r[:, 0:1], m[:, 0:1], float(n), None, ALU.mult))
            link(V.tensor_tensor(raw[:], raw[:], rawr[:], ALU.add))
            V.sem_inc(summed, 1)
            dve.wait_ge(folded, rep + 1)
            link(V.tensor_scalar(mean[:], psF[:, 0:2], 1.0 / N, None, ALU.mult))
            link(V.tensor_tensor(var[:], mean[:, 0:1], mean[:, 0:1], ALU.mult))
            link(V.tensor_tensor(var[:], mean[:, 1:2], var[:], ALU.subtract))
            link(V.tensor_scalar(var[:], var[:], 0.0, None, ALU.max))
            V.sem_inc(asked, 1)
            dve.wait_ge(rooted, rep + 1)
            link(V.reciprocal(scale[:], sd[:]))
            link(V.tensor_tensor(scale[:], scale[:], gamma[:], ALU.mult))
            link(V.tensor_tensor(shift[:], mean[:, 0:1], scale[:], ALU.mult))
            link(V.tensor_tensor(shift[:], beta[:], shift[:], ALU.subtract))
            passed(dve, sems)
            assert link.n == 21, link.n

        @block.tensor
        def _(pe):
            pe.wait_ge(summed, rep + 1)
            nc.tensor.matmul(psF[:, 0:2], mem["fold"][:], raw[:], start=True, stop=True).then_inc(folded, 1)

        @block.scalar
        def _(act):
            act.wait_ge(asked, rep + 1)
            nc.scalar.activation(sd[:], var[:], ACT.Sqrt, bias=eps[:]).then_inc(rooted, 1)

        @block.sync
        def _(sp):
            lay = lambda a: a[bass.ds(rep, 1)].rearrange("o p c -> p (o c)")
            g, b = ("gamma_t", "beta_t") if name == "mix" else ("gamma_o", "beta_o")
            sp.dma_start(gamma[:], lay(mem["io"][g])).then_inc(loaded, 16)
            sp.dma_start(beta[:], lay(mem["io"][b])).then_inc(loaded, 16)
    return scale, shift


def pna_mix(nc, mem, sems, rep):
    io, U = mem["io"], mem["U"]
    with ExitStack() as ctx:
        sb = lambda n, s, dt=F32: ctx.enter_context(nc.sbuf_tensor("mix_" + n, s, dt))
        pb = lambda n, s: ctx.enter_context(nc.psum_tensor("mix_" + n, s, F32))
        gamma, beta = sb("gamma", [P, 1]), sb("beta", [P, 1])
        scale, shift = feature_stats(nc, mem, sems, rep, "mix", sb, pb, gamma, beta)
        w, ws, bias, moved = sb("w", [P, 2 * D]), sb("ws", [P, 2 * D]), sb("bias", [P, 1]), sb("moved", [P, 1])
        hT, y, z = sb("hT", [P, 2, DC]), sb("y", [P, 2, DC]), sb("z", [P, 2, DC])
        psM, psB = pb("psM", [P, 2, 2, 512]), pb("psB", [P, 512])
        n_ = lambda name: sems("mix_" + name)
        loaded, hT_in = n_("w_in"), sems.pair("mix_hT_in")
        with nc.Block() as block:
            @block.sync
            def _(sp):
                lay = lambda a: a[bass.ds(rep, 1)].rearrange("o p c -> p (o c)")
                sp.dma_start(w[:], lay(io["w_mix"])).then_inc(loaded, 16)
                sp.dma_start(bias[:], lay(io["b_mix"])).then_inc(loaded, 16)

                def load_h(t, link):
                    sp.wait_ge(n_("mixed"), t.n())
                    sp.dma_start(hT[:, t.h], mem["hT"][:, bass.ds(t.s * DC, DC)]).then_inc(hT_in[t.h], 16)
                pipeline(sp, None, [(0, load_h, 0)], rep, DSTEPS)

            @block.tensor
            def _(pe):
                pe.wait_ge(loaded, rep * 32 + 32)
                nc.tensor.matmul(psB[:, 0:1], w[:], shift[:], start=True, stop=True).then_inc(n_("shifted"), 1)
                pe.wait_ge(n_("scaled"), rep + 1)
                passed(pe, sems)

                def multiply(t, link):
                    pe.wait_ge(n_("biased"), t.n())
                    for m in range(2):
                        last = nc.tensor.matmul(psM[:, t.h, m, 0:DM], ws[:], U[:, bass.ds(t.s * DC + m * DM, DM)],
                                                start=True, stop=True)
                    last.then_inc(n_("multiplied"), 1)
                pipeline(pe, None, [(0, multiply, 0)], rep, DSTEPS)

            @block.scalar
            def _(act):
                act.wait_ge(n_("scaled"), rep + 1)
                passed(act, sems)
                nc.scalar.preload_act_table(ACT.Identity)

                def add_bias(t, link):
                    act.wait_ge(n_("multiplied"), t.n())
                    act.wait_ge(n_("mixed"), t.n())
                    nc.scalar.activation(y[:, t.h].rearrange("p (m c) -> p m c", m=2), psM[:, t.h, :, 0:DM], ACT.Identity,
                                         bias=moved[:]).then_inc(n_("biased"), 1)
                pipeline(act, None, [(0, add_bias, 0)], rep, DSTEPS)

            @block.vector
            def _(dve):
                V = nc.vector
                first = Link(dve, n_("first"), rep * 2)
                dve.wait_ge(loaded, rep * 32 + 32)
                first(V.tensor_scalar(ws[:], w[:], scale[:], None, ALU.mult))
                dve.wait_ge(n_("shifted"), rep + 1)
                first(V.tensor_tensor(moved[:], psB[:, 0:1], bias[:], ALU.add))
                V.sem_inc(n_("scaled"), 1)
                passed(dve, sems)

                def mix(t, link):
                    dve.wait_ge(n_("biased"), t.n() + 2)
                    dve.wait_ge(hT_in[t.h], t.slot())
                    link(V.scalar_tensor_tensor(z[:, t.h], y[:, t.h], 0.01, y[:, t.h], ALU.mult, ALU.max))
                    link(V.tensor_tensor(U[:, bass.ds(t.s * DC, DC)], z[:, t.h], hT[:, t.h], ALU.add))
                    V.sem_inc(n_("mixed"), 1)
                pipeline(dve, n_("dve_link"), [(0, mix, 2)], rep, DSTEPS)


def pna_out(nc, mem, sems, rep):
    io, U = mem["io"], mem["U"]
    with ExitStack() as ctx:
        sb = lambda n, s, dt=F32: ctx.enter_context(nc.sbuf_tensor("pno_" + n, s, dt))
        pb = lambda n, s: ctx.enter_context(nc.psum_tensor("pno_" + n, s, F32))
        gamma, beta = sb("gamma", [P, 1]), sb("beta", [P, 1])
        scale, shift = feature_stats(nc, mem, sems, rep, "pno", sb, pb, gamma, beta)
        w = sb("w", [P, 2 * D])
        hT, y, hn = sb("hT", [P, 2, DC]), sb("y", [P, DC]), sb("hn", [P, 2, DC])
        rows = sb("msg_rows", [P, 2, 2 * DPAIRS, D])
        psR = pb("psR", [P, 2, 2, 512])
        n_ = lambda name: sems("pno_" + name)
        loaded, hT_in, hn_stored, rows_stored = (n_("w_in"), sems.pair("pno_hT_in"), sems.pair("pno_hn_stored"),
                                                 sems.pair("pno_rows_stored"))
        with nc.Block() as block:
            @block.sync
            def _(sp):
                sp.dma_start(w[:], io["w_top"][bass.ds(rep + 1, 1)].rearrange("o p c -> p (o c)")).then_inc(loaded, 16)

                def load_h(t, link):
                    sp.wait_ge(n_("made"), t.n())
                    sp.dma_start(hT[:, t.h], mem["hT"][:, bass.ds(t.s * DC, DC)]).then_inc(hT_in[t.h], 16)
                pipeline(sp, None, [(0, load_h, 0)], rep, DSTEPS)

            @block.vector
            def _(dve):
                V = nc.vector

                def make(t, link):
                    link(V.tensor_scalar(y[:], U[:, bass.ds(t.s * DC, DC)], scale[:], shift[:], ALU.mult, ALU.add))
                    dve.wait_ge(hT_in[t.h], t.slot())
                    dve.wait_ge(hn_stored[t.h], t.slot())
                    dve.wait_ge(n_("multiplied"), t.n())
                    link(V.scalar_tensor_tensor(hn[:, t.h], y[:], 0.0, hT[:, t.h], ALU.max, ALU.add))
                    V.sem_inc(n_("made"), 1)
                pipeline(dve, n_("dve_link"), [(0, make, 2)], rep, DSTEPS)

            @block.tensor
            def _(pe):
                pe.wait_ge(loaded, rep * 16 + 16)
                passed(pe, sems)

                def multiply(t, link):
                    pe.wait_ge(n_("made"), t.n() + 2)
                    pe.wait_ge(n_("rows"), t.n(2))
                    for k in range(DPAIRS):
                        last = nc.tensor.matmul(psR[:, t.h, k // 4, k % 4 * 2 * D:(k % 4 + 1) * 2 * D],
                                                hn[:, t.h, k * P:(k + 1) * P], w[:], start=True, stop=True)
                    last.then_inc(n_("multiplied"), 1)
                pipeline(pe, None, [(0, multiply, 0)], rep, DSTEPS)

            @block.scalar
            def _(act):
                nc.scalar.preload_act_table(ACT.Square)

                def store_h(t, link):
                    act.wait_ge(n_("made"), t.n() + 2)
                    act.dma_start(mem["hT"][:, bass.ds(t.s * DC, DC)], hn[:, t.h]).then_inc(hn_stored[t.h], 16)

                def keep_rows(t, link):
                    act.wait_ge(n_("multiplied"), t.n() + 2)
                    act.wait_ge(rows_stored[t.h], t.slot(32))
                    for b, pairs in ((0, 4), (1, DPAIRS - 4)):
                        nc.scalar.copy(rows[:, t.h, b * 8:b * 8 + 2 * pairs],
                                       psR[:, t.h, b, 0:pairs * 2 * D].rearrange("p (n d) -> p n d", d=D)).then_inc(n_("rows"), 1)
                    act.wait_ge(n_("rows"), t.n(2) + 4)
                    store_rows(act, mem["msg_table"], rows[:, t.h], t.s * DPAIRS, rows_stored[t.h], DPAIRS)
                pipeline(act, None, [(0, store_h, 0), (1, keep_rows, 0)], rep, DSTEPS)
        stores_done(nc, sems, [(hn_stored, 16), (rows_stored, 32)], rep, DSTEPS)


def pna_end(nc, mem, sems):
    C = WPAIRS * P
    with ExitStack() as ctx:
        sb = lambda n, s, dt=F32: ctx.enter_context(nc.sbuf_tensor("end_" + n, s, dt))
        pb = lambda n, s: ctx.enter_context(nc.psum_tensor("end_" + n, s, F32))
        hT, x1, x2 = sb("hT", [P, 2, C]), sb("x1", [P, 2, WPAIRS, 2, D]), sb("x2", [P, 2, WB, D])
        hn, rows = sb("hn", [P, WB, D]), sb("rows", [P, 2, WB, D])
        psT = pb("psT", [P, 2, 512])
        norm = Norm(nc, sb, sems, "end_norm")
        n_ = lambda name: sems("end_" + name)
        x_in = sems.pair("end_x_in")
        x2_stored, rows_stored = sems.pair("end_x2_stored"), sems.pair("end_rows_stored")
        with nc.Block() as block:
            @block.sync
            def _(sp):
                def loads(t, link):
                    sp.wait_ge(n_("summed"), t.n())
                    sp.dma_start(hT[:, t.h], mem["hT"][:, bass.ds(t.s * C, C)]).then_inc(x_in[t.h], 16)
                    for g in range(2):
                        sp.dma_start(x1[:, t.h, :, g, :], node_rows(mem["x1"], g, t.s * WPAIRS)).then_inc(x_in[t.h], 16)
                node_pipeline(sp, None, [(0, loads, 0)])

            @block.tensor
            def _(pe):
                def turn(t, link):
                    pe.wait_ge(x_in[t.h], t.slot(48))
                    pe.wait_ge(n_("summed"), t.n())
                    for k in range(WPAIRS):
                        last = nc.tensor.transpose(psT[:, t.h, k * P:(k + 1) * P], hT[:, t.h, k * P:(k + 1) * P], mem["ident"][:])
                    last.then_inc(n_("turned"), 1)
                node_pipeline(pe, None, [(0, turn, 0)])

            @block.vector
            def _(dve):
                V = nc.vector
                first = Link(dve, n_("first"))
                first(V.memset(norm.eps[:], EPS))
                passed(dve, sems)

                def add_center(t, link):
                    dve.wait_ge(n_("turned"), t.n())
                    dve.wait_ge(x_in[t.h], t.slot(48))
                    dve.wait_ge(x2_stored[t.h], t.slot(32))
                    link(V.tensor_tensor(x2[:, t.h], psT[:, t.h, 0:WB * D].rearrange("p (n d) -> p n d", d=D),
                                         x1[:, t.h].rearrange("p k g d -> p (k g) d"), ALU.add))
                    V.sem_inc(n_("summed"), 1)
                    norm.first(link, t, x2[:, t.h])

                def make_rows(t, link):
                    norm.second(dve, link, t, hn[:])
                    dve.wait_ge(rows_stored[t.h], t.slot(32))
                    link(V.tensor_tensor(rows[:, t.h], hn[:], per_tile(own_nodes(mem, "dis", t)), ALU.mult))
                    V.sem_inc(n_("rows"), 1)
                node_pipeline(dve, n_("link"), [(0, add_center, 1 + Norm.FIRST), (1, make_rows, Norm.SECOND + 1)])

            @block.scalar
            def _(act):
                nc.scalar.preload_act_table(ACT.Sqrt)

                def store_x2(t, link):
                    act.wait_ge(n_("summed"), t.n() + 2)
                    store_rows(act, mem["x2"], x2[:, t.h], t.s * WPAIRS, x2_stored[t.h])

                def store(t, link):
                    act.wait_ge(n_("rows"), t.n())
                    store_rows(act, mem["table1"], rows[:, t.h], t.s * WPAIRS, rows_stored[t.h])
                node_pipeline(act, None, [(0, store_x2, 0), (0, lambda t, link: norm.scalar(act, t), 0), (1, store, 0)])
        stores_done(nc, sems, [(x2_stored, 32), (rows_stored, 32)], 0, WSTEPS)


def own_nodes(mem, name, t):
    return mem[name][:, bass.ds(t.s * WPAIRS, WPAIRS), :].rearrange("p k g -> p (k g)")


def sum_edges(nc, mem, sems, rep, table, order):
    by_src = order == "src"
    with ExitStack() as ctx:
        sb = lambda n, s, dt=F32: ctx.enter_context(nc.sbuf_tensor("sum%d_" % rep + n, s, dt))
        pb = lambda n, s: ctx.enter_context(nc.psum_tensor("sum%d_" % rep + n, s, F32))
        index, mask = sb("index", [P, 2, TB], I32), sb("mask", [D, 2, EB], BF16)
        pay = sb("pay", [P, TILES, PAYW]) if by_src else None
        dst = sb("dst", [P, TILES], I32) if by_src else None
        index_table = dst if by_src else mem["dst_src"]
        got, z, sums = sb("got", [P, 2, TB, D]), sb("z", [P, 2, TB, D]), sb("sums", [D, 2, EB])
        out = sb("out", [P, 2, TB, D])
        psS, psB = pb("psS", [D, 2, EB]), pb("psB", [P, 2, 512])
        n_ = lambda name: sems("sum_" + name)
        index_in, mask_in, got_in, stored = (sems.pair("sum_" + n) for n in ("index_in", "mask_in", "got", "stored"))
        with nc.Block() as block:
            @block.sync
            def _(sp):
                if by_src:
                    sp.dma_start(pay[:].rearrange("p t c -> p (t c)"), mem["pay_sorted"]).then_inc(n_("pay_in"), 16)
                    sp.wait_ge(n_("split"), 1)

                def loads(t, link):
                    if not t.first:
                        sp.wait_ge(got_in[t.h], t.slot(16 * TB) - 16 * TB)
                    sp.dma_start(index[:, t.h, :], index_table[:, bass.ds(t.s * TB, TB)]).then_inc(index_in[t.h], 16)

                def load_mask(t, link):
                    sp.wait_ge(n_("scanned"), t.n())
                    sp.dma_start(mask[:, t.h], mem["mask_" + order][bass.ds(t.s, 1), 0:EB].broadcast_to([D, EB])).then_inc(mask_in[t.h], 16)
                pipeline(sp, None, [(0, loads, 0), (1, load_mask, 0)], rep, peel=2)

            @block.gpsimd
            def _(pool):
                def gather_rows(t, link):
                    pool.wait_ge(index_in[t.h], t.slot())
                    if by_src:
                        pool.wait_ge(n_("weighted"), t.n() - rep * STEPS)
                    else:
                        pool.wait_ge(n_("turned"), t.n())
                    passed(pool, sems)
                    for j in range(TB):
                        gather(pool, got[:, t.h, j, :], table, index[:, t.h, j:j + 1]).then_inc(got_in[t.h], 16)
                pipeline(pool, None, [(0, gather_rows, 0)], rep)

            @block.tensor
            def _(pe):
                def turn(t, link):
                    if by_src:
                        pe.wait_ge(n_("weighted"), t.n() - rep * STEPS + 2)
                    else:
                        pe.wait_ge(got_in[t.h], t.slot(16 * TB))
                    pe.wait_ge(n_("scanned"), t.n())
                    passed(pe, sems)
                    for j in range(TB):
                        last = nc.tensor.transpose(psS[:, t.h, j * P:(j + 1) * P], (z if by_src else got)[:, t.h, j, :], mem["ident"][:])
                    last.then_inc(n_("turned"), 1)

                def turn_back(t, link):
                    pe.wait_ge(n_("scanned"), t.n() + 2)
                    pe.wait_ge(n_("copied"), t.n())
                    passed(pe, sems)
                    for j in range(TB):
                        last = nc.tensor.transpose(psB[:, t.h, j * D:(j + 1) * D], sums[:, t.h, j * P:(j + 1) * P], mem["ident"][0:D, 0:D])
                    last.then_inc(n_("back"), 1)
                pipeline(pe, None, [(0, turn, 0), (1, turn_back, 0)], rep)

            @block.vector
            def _(dve):
                V = nc.vector
                first = Link(dve, n_("first"), rep)
                first(V.memset(sums[:], 0.0))
                if by_src:
                    dve.wait_ge(n_("pay_in"), 16)
                    V.tensor_copy(dst[:], pay[:, :, PAYW - 1].bitcast(I32)).then_inc(n_("split"), 1)
                passed(dve, sems)

                def weigh(t, link):
                    dve.wait_ge(got_in[t.h], t.slot(16 * TB))
                    dve.wait_ge(n_("turned"), t.n())
                    V.tensor_tensor(z[:, t.h], got[:, t.h], pay[:, bass.ds(t.s * TB, TB), PAYW - 2:PAYW - 1].broadcast_to([P, TB, D]),
                                    ALU.mult).then_inc(n_("weighted"), 1)

                def scan(t, link):
                    dve.wait_ge(n_("turned"), t.n() + 2)
                    dve.wait_ge(mask_in[t.h], t.slot())
                    link(V.tensor_tensor_scan(sums[:, t.h, :], mask[:, t.h, :], psS[:, t.h, :], sums[:, 1 - t.h, EB - 1:EB], ALU.mult, ALU.add))
                    V.sem_inc(n_("scanned"), 1)
                pipeline(dve, n_("link"), ([(0, weigh, 0)] if by_src else []) + [(1, scan, 1)], rep)

            @block.scalar
            def _(act):
                nc.scalar.preload_act_table(ACT.Square)

                def store(t, link):
                    act.wait_ge(n_("back"), t.n())
                    act.wait_ge(stored[t.h], t.slot())
                    nc.scalar.copy(out[:, t.h], psB[:, t.h, 0:TB * D].rearrange("p (j d) -> p j d", d=D)).then_inc(n_("copied"), 1)
                    act.wait_ge(n_("copied"), t.n() + 2)
                    act.dma_start(mem["sum_scan"][0:ROWS, :].rearrange("(t p) c -> p t c", p=P)[:, bass.ds(t.s * TB, TB), :],
                                  out[:, t.h]).then_inc(stored[t.h], 16)
                pipeline(act, None, [(1, store, 0)], rep)
        stores_done(nc, sems, [(stored, 16)], rep)


def conv_hidden(nc, mem, sems):
    io = mem["io"]
    with ExitStack() as ctx:
        sb = lambda n, s, dt=F32: ctx.enter_context(nc.sbuf_tensor("hid_" + n, s, dt))
        pb = lambda n, s: ctx.enter_context(nc.psum_tensor("hid_" + n, s, F32))
        index, got = sb("index", [P, 2, WB], I32), sb("got", [P, 2, WB, D])
        y, w, rows = sb("y", [P, 2, WPAIRS, 2 * D]), sb("w", [P, 2 * D]), sb("rows", [P, 2, WB, D])
        turn = Turned(nc, sb, pb, sems, "hid")
        n_ = lambda name: sems("hid_" + name)
        got_in, stored, loaded = sems.pair("hid_got"), sems.pair("hid_stored"), n_("in")
        with nc.Block() as block:
            @block.sync
            def _(sp):
                sp.dma_start(w[:], io["w1"]).then_inc(loaded, 16)

                def loads(t, link):
                    index_loads(nc, sp, mem, sems, "hid", t, index[:].rearrange("p h (k g) -> p h k g", g=2), "end_dst", WPAIRS)
                node_pipeline(sp, None, [(0, loads, 0)], peel=2)

            @block.gpsimd
            def _(pool):
                node_pipeline(pool, None, [(0, lambda t, link: gathers(
                    nc, pool, sems, "hid", t, got, mem["sum_scan"], index[:, t.h].rearrange("p (n o) -> p n o", o=1)), 0)])

            @block.tensor
            def _(pe):
                pe.wait_ge(loaded, 16)
                node_pipeline(pe, None, [(0, lambda t, link: turn.turn(pe, t, y, mem["ident"]), 0),
                                    (1, lambda t, link: turn.multiply(pe, t, w), 0)])

            @block.vector
            def _(dve):
                V = nc.vector

                def scale(t, link):
                    dve.wait_ge(got_in[t.h], t.slot(16 * WB))
                    dve.wait_ge(turn.turned, t.n())
                    link(V.tensor_tensor(y[:, t.h].rearrange("p k (g d) -> p (k g) d", g=2), got[:, t.h],
                                         per_tile(own_nodes(mem, "dis", t)), ALU.mult))
                    V.sem_inc(n_("got_used"), 1)
                    V.sem_inc(turn.ready, 1)

                def make_rows(t, link):
                    dve.wait_ge(turn.multiplied, t.n() + 2)
                    dve.wait_ge(stored[t.h], t.slot(32))
                    link(V.scalar_tensor_tensor(rows[:, t.h], turn.product(t.h), 0.0, per_tile(own_nodes(mem, "dis", t)),
                                                ALU.max, ALU.mult))
                    V.sem_inc(turn.used, 1)
                    V.sem_inc(n_("rows"), 1)
                node_pipeline(dve, n_("link"), [(0, scale, 1), (2, make_rows, 1)])

            @block.scalar
            def _(act):
                nc.scalar.preload_act_table(ACT.Square)

                def store(t, link):
                    act.wait_ge(n_("rows"), t.n())
                    store_rows(act, mem["table2"], rows[:, t.h], t.s * WPAIRS, stored[t.h])
                node_pipeline(act, None, [(0, lambda t, link: turn.scalar(act, t), 0), (2, store, 0)])
        stores_done(nc, sems, [(stored, 32)], 0, WSTEPS)


def conv_out(nc, mem, sems):
    io = mem["io"]
    with ExitStack() as ctx:
        sb = lambda n, s, dt=F32: ctx.enter_context(nc.sbuf_tensor("cou_" + n, s, dt))
        pb = lambda n, s: ctx.enter_context(nc.psum_tensor("cou_" + n, s, F32))
        index, got = sb("index", [P, 2, WB], I32), sb("got", [P, 2, WB, D])
        y, w, w3 = sb("y", [P, 2, WPAIRS, 2 * D]), sb("w", [P, 2 * D]), sb("w3", [P, 2 * D])
        rows, hn = sb("rows", [P, 2, WB, D]), sb("hn", [P, 2, WPAIRS, 2 * D])
        x2, x3 = sb("x2", [P, 2, WPAIRS, 2, D]), sb("x3", [P, 2, WB, D])
        turn = Turned(nc, sb, pb, sems, "cou")
        turn3 = Turned(nc, sb, pb, sems, "cou_three")
        norm = Norm(nc, sb, sems, "cou_norm")
        n_ = lambda name: sems("cou_" + name)
        got_in, loaded, x_in = sems.pair("cou_got"), n_("in"), sems.pair("cou_x_in")
        x3_stored, rows_stored = sems.pair("cou_x3_stored"), sems.pair("cou_rows_stored")
        with nc.Block() as block:
            @block.sync
            def _(sp):
                sp.dma_start(w[:], io["w2"]).then_inc(loaded, 16)
                sp.dma_start(w3[:], io["w3"]).then_inc(loaded, 16)

                def loads(t, link):
                    index_loads(nc, sp, mem, sems, "cou", t, index[:].rearrange("p h (k g) -> p h k g", g=2), "end_dst", WPAIRS)

                def load_x2(t, link):
                    sp.wait_ge(n_("summed"), t.n())
                    for g in range(2):
                        sp.dma_start(x2[:, t.h, :, g, :], node_rows(mem["x2"], g, t.s * WPAIRS)).then_inc(x_in[t.h], 16)
                node_pipeline(sp, None, [(0, loads, 0), (2, load_x2, 0)], peel=2)

            @block.gpsimd
            def _(pool):
                node_pipeline(pool, None, [(0, lambda t, link: gathers(
                    nc, pool, sems, "cou", t, got, mem["sum_scan"], index[:, t.h].rearrange("p (n o) -> p n o", o=1)), 0)])

            @block.tensor
            def _(pe):
                pe.wait_ge(loaded, 32)
                node_pipeline(pe, None, [(0, lambda t, link: turn.turn(pe, t, y, mem["ident"]), 0),
                                    (1, lambda t, link: turn.multiply(pe, t, w), 0),
                                    (3, lambda t, link: turn3.turn(pe, t, hn, mem["ident"]), 0),
                                    (4, lambda t, link: turn3.multiply(pe, t, w3), 0)])

            @block.vector
            def _(dve):
                V = nc.vector
                first = Link(dve, n_("first"))
                first(V.memset(norm.eps[:], EPS))

                def scale(t, link):
                    dve.wait_ge(got_in[t.h], t.slot(16 * WB))
                    dve.wait_ge(turn.turned, t.n())
                    link(V.tensor_tensor(y[:, t.h].rearrange("p k (g d) -> p (k g) d", g=2), got[:, t.h],
                                         per_tile(own_nodes(mem, "dis", t)), ALU.mult))
                    V.sem_inc(n_("got_used"), 1)
                    V.sem_inc(turn.ready, 1)

                def add_center(t, link):
                    dve.wait_ge(turn.multiplied, t.n() + 2)
                    dve.wait_ge(x3_stored[t.h], t.slot(32))
                    dve.wait_ge(x_in[t.h], t.slot(32))
                    link(V.tensor_tensor(x3[:, t.h], turn.product(t.h), x2[:, t.h].rearrange("p k g d -> p (k g) d"), ALU.add))
                    V.sem_inc(turn.used, 1)
                    V.sem_inc(n_("summed"), 1)
                    norm.first(link, t, x3[:, t.h])

                def normed(t, link):
                    dve.wait_ge(turn3.turned, t.n())
                    norm.second(dve, link, t, hn[:, t.h].rearrange("p k (g d) -> p (k g) d", g=2))
                    V.sem_inc(turn3.ready, 1)

                def make_rows(t, link):
                    dve.wait_ge(turn3.multiplied, t.n() + 2)
                    dve.wait_ge(rows_stored[t.h], t.slot(32))
                    link(V.tensor_tensor(rows[:, t.h], turn3.product(t.h), per_tile(own_nodes(mem, "dis_s", t)), ALU.mult))
                    V.sem_inc(turn3.used, 1)
                    V.sem_inc(n_("rows"), 1)
                node_pipeline(dve, n_("link"), [(0, scale, 1), (2, add_center, 1 + Norm.FIRST), (3, normed, Norm.SECOND),
                                           (5, make_rows, 1)])

            @block.scalar
            def _(act):
                nc.scalar.preload_act_table(ACT.Sqrt)

                def store_x3(t, link):
                    act.wait_ge(n_("summed"), t.n() + 2)
                    store_rows(act, mem["x3"], x3[:, t.h], t.s * WPAIRS, x3_stored[t.h])

                def store(t, link):
                    act.wait_ge(n_("rows"), t.n())
                    store_rows(act, mem["table3"], rows[:, t.h], t.s * WPAIRS, rows_stored[t.h])
                node_pipeline(act, None, [(0, lambda t, link: turn.scalar(act, t), 0), (2, store_x3, 0),
                                     (2, lambda t, link: norm.scalar(act, t), 0),
                                     (3, lambda t, link: turn3.scalar(act, t), 0), (5, store, 0)])
        stores_done(nc, sems, [(x3_stored, 32), (rows_stored, 32)], 0, WSTEPS)


def last_nodes(nc, mem, sems):
    io = mem["io"]
    with ExitStack() as ctx:
        sb = lambda n, s, dt=F32: ctx.enter_context(nc.sbuf_tensor("fin_" + n, s, dt))
        index, got = sb("index", [P, 2, WB], I32), sb("got", [P, 2, WB, D])
        bias, x3, y = sb("bias", [P, D]), sb("x3", [P, 2, WPAIRS, 2, D]), sb("y", [P, 2, WB, D])
        n_ = lambda name: sems("fin_" + name)
        got_in, stored, loaded, x_in = sems.pair("fin_got"), sems.pair("fin_stored"), n_("in"), sems.pair("fin_x_in")
        with nc.Block() as block:
            @block.sync
            def _(sp):
                sp.dma_start(bias[:], io["last_bias"]).then_inc(loaded, 16)

                def loads(t, link):
                    index_loads(nc, sp, mem, sems, "fin", t, index[:].rearrange("p h (k g) -> p h k g", g=2), "end_src", WPAIRS)
                    sp.wait_ge(n_("got_used"), t.n())
                    for g in range(2):
                        sp.dma_start(x3[:, t.h, :, g, :], node_rows(mem["x3"], g, t.s * WPAIRS)).then_inc(x_in[t.h], 16)
                node_pipeline(sp, None, [(0, loads, 0)], peel=2)

            @block.gpsimd
            def _(pool):
                node_pipeline(pool, None, [(0, lambda t, link: gathers(
                    nc, pool, sems, "fin", t, got, mem["sum_scan"], index[:, t.h].rearrange("p (n o) -> p n o", o=1)), 0)])

            @block.vector
            def _(dve):
                V = nc.vector
                dve.wait_ge(loaded, 16)

                def add(t, link):
                    dve.wait_ge(got_in[t.h], t.slot(16 * WB))
                    dve.wait_ge(x_in[t.h], t.slot(32))
                    dve.wait_ge(stored[t.h], t.slot(32))
                    link(V.tensor_tensor(y[:, t.h], got[:, t.h], per_tile(own_nodes(mem, "dis_s", t)), ALU.mult))
                    link(V.tensor_tensor(y[:, t.h], y[:, t.h], per_feature(bias[:], WB), ALU.add))
                    link(V.tensor_tensor(y[:, t.h], y[:, t.h], x3[:, t.h].rearrange("p k g d -> p (k g) d"), ALU.add))
                    V.sem_inc(n_("got_used"), 1)
                    V.sem_inc(n_("y"), 1)
                node_pipeline(dve, n_("link"), [(0, add, 3)])

            @block.scalar
            def _(act):
                def store(t, link):
                    act.wait_ge(n_("y"), t.n())
                    store_rows(act, mem["out"], y[:, t.h], t.s * WPAIRS, stored[t.h])
                node_pipeline(act, None, [(0, store, 0)])
        stores_done(nc, sems, [(stored, 32)], 0, WSTEPS)


def both_halves(w, w1=None):
    w1 = w if w1 is None else w1
    z = np.zeros(w.shape[:-2] + (D, w.shape[-1]), np.float32)
    return np.concatenate([np.concatenate([w, z], -1), np.concatenate([z, w1], -1)], -2)


def layout(inputs):
    g = {k: np.asarray(v) for k, v in inputs.items()}
    a = {}
    pad = ROWS - E
    src = np.concatenate([g["src"], np.zeros(pad, np.int32)])
    dst = np.concatenate([g["dst"], np.full(pad, PAD_KEY, np.int32)])
    a["src_cols"] = np.ascontiguousarray(src.reshape(TILES, P).T)
    a["dst_cols"] = np.ascontiguousarray(dst.reshape(TILES, P).T)
    a["dst_line"] = np.concatenate([np.full(1, -1, np.int32), dst])[:, None]
    a["src_sort"] = np.concatenate([g["src"], np.full(pad, PAD_KEY, np.int32),
                                    np.full(P * SORTF - ROWS, 57000, np.int32)]).reshape(P, SORTF)
    i = np.arange(P * SORTF).reshape(P, SORTF)
    a["sort_index"] = i.astype(np.float32)
    bit = [(i >> k) & 1 for k in range(1, LEVELS + 1)]
    turn = [bit[0]] + [bit[k - 1] ^ bit[k] for k in range(1, LEVELS)]
    a["sort_signs"] = np.ascontiguousarray(np.stack([1.0 - 2.0 * t for t in turn], 1).astype(np.float32))
    a["zeros"] = np.zeros((1, 4 * D), np.float32)
    a["minus_one"] = np.full((1, 1), -1.0, np.float32)
    eye = np.eye(P, dtype=np.float32)
    fold = np.tile(np.eye(D, dtype=np.float32), (2, 2))
    tri = np.triu(np.ones((P, P), np.float32))
    sel = np.zeros((P, P), np.float32)
    sel[0, 0:D] = 1.0
    sel[1, D:] = 1.0
    zeros = lambda n: np.zeros((pad, n), np.float32)
    a["pay"] = np.concatenate([np.concatenate([g["edge_attr_5"], zeros(5)]),
                               np.ones((ROWS, 1), np.float32),
                               np.concatenate([g["edge_weight"][:, None], zeros(1)]),
                               np.zeros((ROWS, 1), np.float32)], 1)
    a["x"] = np.concatenate([g["x"], zeros(D)])
    rows = lambda v: np.ascontiguousarray(np.broadcast_to(v.reshape(1, -1), (P, v.size)))
    a["w_lin"] = both_halves(g["L0_gnn_W_lin"])
    a["b_lin"] = rows(g["L0_gnn_b_lin"])
    a["att_own"] = rows(g["L0_gnn_att"][0, :, :D])
    a["att_other"] = both_halves(g["L0_gnn_att"][0, 0, D:, None], g["L0_gnn_att"][0, 1, D:, None])
    a["w_edge"] = np.concatenate([g["L0_gnn_W_edge"], g["L0_gnn_b_edge"][None]])
    a["att_bias"] = rows(g["L0_gnn_bias"])
    wide = lambda v: np.ascontiguousarray(np.broadcast_to(v[:, None, :], (LAYERS, P, D)))
    twice = lambda v: np.ascontiguousarray(np.concatenate([v, v], 1)[:, :, None])
    top = both_halves(g["L1_gnn_WM"][:, :D])
    a["w_top"] = np.concatenate([top, top[:1]])
    a["w_bot"] = both_halves(g["L1_gnn_WM"][:, D:])
    a["w_own"] = both_halves(g["L1_gnn_WU"][:, :D])
    agg = g["L1_gnn_WU"][:, D:].reshape(LAYERS, 3, 3, P, D)
    a["w_agg"] = np.ascontiguousarray(agg.transpose(0, 3, 2, 1, 4)).reshape(LAYERS, P, 9 * D)
    a["bM"], a["bU"] = wide(g["L1_gnn_bM"]), twice(g["L1_gnn_bU"])
    a["w_mix"] = both_halves(g["L1_gnn_Wmix"])
    a["b_mix"] = twice(g["L1_gnn_bmix"])
    for name in ("gamma_t", "beta_t", "gamma_o", "beta_o"):
        a[name] = twice(g["L1_gnn_" + name])
    a["w1"], a["w2"] = both_halves(g["L2_gnn_W1"]), both_halves(g["L2_gnn_W2"])
    a["w3"], a["last_bias"] = both_halves(g["L3_gnn_weight"]), rows(g["L3_gnn_bias"])
    a["consts"] = np.concatenate([eye, fold, tri, sel, np.tile(np.arange(TILES, dtype=np.float32), (P, 1))], 1)
    return a


def kernel(**inputs):
    import concourse.bacc as bacc
    from concourse.bass_utils import run_bass_kernel_spmd

    nc = bacc.Bacc("TRN2", target_bir_lowering=False, num_devices=1)
    arrays = {"in_" + k: np.ascontiguousarray(v) for k, v in layout(inputs).items()}
    io = {k[3:]: nc.dram_tensor(k, a.shape, mybir.dt.from_np(a.dtype), kind="ExternalInput").ap() for k, a in arrays.items()}
    out = nc.dram_tensor("out", [ROWS, D], F32, kind="ExternalOutput").ap()
    program(nc, io, out)
    r = run_bass_kernel_spmd(nc, [arrays], core_ids=[0])
    return r.results[0]["out"][:N]
```
